# Optimizing a Trainium2 kernel written in Bass

```python
import numpy as np
import jax
import jax.numpy as jnp

def _softmax(x, axis=-1):
    return jax.nn.softmax(x, axis=axis)

def _gelu(x):
    return jax.nn.gelu(x, approximate=True)

def _silu(x):
    return jax.nn.silu(x)

def _sigmoid(x):
    return jax.nn.sigmoid(x)

def _layernorm(x, axis=-1, eps=1e-05):
    m = jnp.mean(x, axis=axis, keepdims=True)
    v = jnp.var(x, axis=axis, keepdims=True)
    return (x - m) / jnp.sqrt(v + eps)

def _scatter_add(tgt, idx, src, axis=0):
    return tgt.at[idx].add(src)

def _segment_sum(src, seg, n):
    return jax.ops.segment_sum(src, seg, n)
kernel_name = 'mk_gnn_resnorm_d2_gnn_r8_21434a'

def setup_inputs(seed: int=0):
    np.random.seed(seed)
    _w = jnp.asarray

    def _rec_inputs():
        import jax
        import jax.numpy as jnp
        _gk = jax.random.key(seed)
        x = -0.0001126 + 1 * jax.random.normal(jax.random.fold_in(_gk, 1), (3750, 256), jnp.float32)
        src = jax.random.randint(jax.random.fold_in(_gk, 2), (120000,), 0, 3750, jnp.int32)
        dst = jnp.minimum((3750 * jax.random.uniform(jax.random.fold_in(_gk, 3), (120000,)) ** 2.0).astype(jnp.int32), 29999)
        _o = jnp.argsort(dst, stable=True)
        src = src[_o]
        dst = dst[_o]
        edge_type_8 = jax.random.randint(jax.random.fold_in(_gk, 12), (120000,), 0, 8, jnp.int32)
        return (x, src, dst, edge_type_8)
    x, src, dst, edge_type_8 = _rec_inputs()

    def _L0_gnn_setup():
        import jax, jax.numpy as jnp
        import numpy as np
        N_NODES = 3750
        N_EDGES = 60000
        IN_FEAT = 256
        OUT_FEAT = 256
        N_RELS = 8
        N_HEADS = 4
        HEAD_DIM = OUT_FEAT // N_HEADS
        LEAKY_SLOPE = 0.2
        key = jax.random.key(seed)
        ks = jax.random.split(key, 8)
        inputs = jax.random.normal(ks[0], (N_NODES, IN_FEAT), dtype=jnp.float32)
        conv_weights = jax.random.normal(ks[1], (N_RELS, N_HEADS, IN_FEAT, HEAD_DIM), dtype=jnp.float32) * (1.0 / np.sqrt(IN_FEAT))
        attn_l = jax.random.normal(ks[2], (N_RELS, N_HEADS, HEAD_DIM), dtype=jnp.float32) * 0.1
        attn_r = jax.random.normal(ks[3], (N_RELS, N_HEADS, HEAD_DIM), dtype=jnp.float32) * 0.1
        h_bias = jax.random.normal(ks[4], (OUT_FEAT,), dtype=jnp.float32) * 0.02
        edge_src = jax.random.randint(ks[5], (N_EDGES,), 0, N_NODES, dtype=jnp.int32)
        edge_dst = jax.random.randint(ks[6], (N_EDGES,), 0, N_NODES, dtype=jnp.int32)
        edge_type = jax.random.randint(ks[7], (N_EDGES,), 0, N_RELS, dtype=jnp.int32)
        return {'inputs': inputs, 'conv_weights': conv_weights, 'attn_l': attn_l, 'attn_r': attn_r, 'h_bias': h_bias, 'edge_src': edge_src, 'edge_dst': edge_dst, 'edge_type': edge_type}
    _L0_gnn_all = _L0_gnn_setup()
    _L0_gnn_in = {k: v for k, v in _L0_gnn_all.items() if k in ('conv_weights', 'attn_l', 'attn_r', 'h_bias')}
    del _L0_gnn_all

    def _L1_gnn_setup():
        import jax, jax.numpy as jnp
        import numpy as np
        N_NODES = 2048
        N_EDGES = 32768
        D_IN = 256
        D = 256
        H = 512
        E = 64
        TOP_K = 2
        CAP = 1024
        BN_EPS = 1e-05

        def _moe_ff(x, Wg, bg, w1, b1, w2, b2):
            N = x.shape[0]
            logits = x @ Wg + bg
            vals, idx = jax.lax.top_k(logits, TOP_K)
            gates = jax.nn.softmax(vals, axis=-1)
            e_flat = idx.reshape(-1)
            g_flat = gates.reshape(-1)
            tok = jnp.arange(N * TOP_K) // TOP_K
            order = jnp.argsort(e_flat)
            e_s, tok_s, g_s = (e_flat[order], tok[order], g_flat[order])
            counts = jnp.bincount(e_flat, length=E)
            offs = jnp.concatenate([jnp.zeros((1,), counts.dtype), jnp.cumsum(counts)[:-1]])
            rank = jnp.arange(N * TOP_K) - offs[e_s]
            valid = rank < CAP
            slot = jnp.where(valid, e_s * CAP + rank, E * CAP)
            buf = jnp.zeros((E * CAP + 1, D), x.dtype).at[slot].set(x[tok_s])
            h = buf[:E * CAP].reshape(E, CAP, D)
            h1 = jax.nn.gelu(jnp.einsum('ecd,edh->ech', h, w1) + b1[:, None, :], approximate=False)
            h2 = jnp.einsum('ech,ehd->ecd', h1, w2) + b2[:, None, :]
            out_buf = h2.reshape(E * CAP, D)
            y_s = jnp.where(valid[:, None], out_buf[jnp.minimum(slot, E * CAP - 1)], 0.0)
            return jnp.zeros((N, D), x.dtype).at[tok_s].add(g_s[:, None] * y_s)

        def _forward(feats, W_gc, b_gc, W_res, b_res, Wg, bg, w1, b1, w2, b2, gamma, beta, src, dst):
            n = feats.shape[0]
            ones = jnp.ones((src.shape[0],), feats.dtype)
            deg_out = jnp.clip(jax.ops.segment_sum(ones, src, num_segments=n), 1.0)
            deg_in = jnp.clip(jax.ops.segment_sum(ones, dst, num_segments=n), 1.0)
            h = feats * jax.lax.rsqrt(deg_out)[:, None]
            m = jax.ops.segment_sum(h[src], dst, num_segments=n) * jax.lax.rsqrt(deg_in)[:, None]
            gc = m @ W_gc + b_gc
            x = gc + (feats @ W_res + b_res)
            core = _moe_ff(x, Wg, bg, w1, b1, w2, b2)
            y = x + core
            mean = jnp.mean(y, axis=0)
            var = jnp.mean((y - mean) ** 2, axis=0)
            return (y - mean) * jax.lax.rsqrt(var + BN_EPS) * gamma + beta
        key = jax.random.key(seed)
        ks = jax.random.split(key, 16)
        s = lambda d: 1.0 / np.sqrt(d)
        inp = {'feats': jax.random.normal(ks[0], (N_NODES, D_IN), jnp.float32), 'W_gc': jax.random.normal(ks[1], (D_IN, D), jnp.float32) * s(D_IN), 'b_gc': jnp.zeros((D,), jnp.float32), 'W_res': jax.random.normal(ks[2], (D_IN, D), jnp.float32) * s(D_IN), 'b_res': jnp.zeros((D,), jnp.float32), 'Wg': jax.random.normal(ks[3], (D, E), jnp.float32) * s(D), 'bg': jnp.zeros((E,), jnp.float32), 'w1': jax.random.normal(ks[4], (E, D, H), jnp.float32) * s(D), 'b1': jnp.zeros((E, H), jnp.float32), 'w2': jax.random.normal(ks[5], (E, H, D), jnp.float32) * s(H), 'b2': jnp.zeros((E, D), jnp.float32), 'gamma': jnp.ones((D,), jnp.float32), 'beta': jnp.zeros((D,), jnp.float32), 'src': jax.random.randint(ks[6], (N_EDGES,), 0, N_NODES), 'dst': jax.random.randint(ks[7], (N_EDGES,), 0, N_NODES)}
        return inp
    _L1_gnn_all = _L1_gnn_setup()
    _L1_gnn_in = {k: v for k, v in _L1_gnn_all.items() if k in ('W_gc', 'b_gc', 'W_res', 'b_res', 'Wg', 'bg', 'w1', 'b1', 'w2', 'b2', 'gamma', 'beta')}
    del _L1_gnn_all
    return {'x': x, 'src': src, 'dst': dst, 'edge_type_8': edge_type_8, 'L0_gnn_conv_weights': _L0_gnn_in['conv_weights'], 'L0_gnn_attn_l': _L0_gnn_in['attn_l'], 'L0_gnn_attn_r': _L0_gnn_in['attn_r'], 'L0_gnn_h_bias': _L0_gnn_in['h_bias'], 'L1_gnn_W_gc': _L1_gnn_in['W_gc'], 'L1_gnn_b_gc': _L1_gnn_in['b_gc'], 'L1_gnn_W_res': _L1_gnn_in['W_res'], 'L1_gnn_b_res': _L1_gnn_in['b_res'], 'L1_gnn_Wg': _L1_gnn_in['Wg'], 'L1_gnn_bg': _L1_gnn_in['bg'], 'L1_gnn_w1': _L1_gnn_in['w1'], 'L1_gnn_b1': _L1_gnn_in['b1'], 'L1_gnn_w2': _L1_gnn_in['w2'], 'L1_gnn_b2': _L1_gnn_in['b2'], 'L1_gnn_gamma': _L1_gnn_in['gamma'], 'L1_gnn_beta': _L1_gnn_in['beta']}

def reference(x, src, dst, edge_type_8, L0_gnn_conv_weights, L0_gnn_attn_l, L0_gnn_attn_r, L0_gnn_h_bias, L1_gnn_W_gc, L1_gnn_b_gc, L1_gnn_W_res, L1_gnn_b_res, L1_gnn_Wg, L1_gnn_bg, L1_gnn_w1, L1_gnn_b1, L1_gnn_w2, L1_gnn_b2, L1_gnn_gamma, L1_gnn_beta):
    import jax
    import jax.numpy as jnp

    def _L0_gnn_ref(inputs, conv_weights, attn_l, attn_r, h_bias, edge_src, edge_dst, edge_type):
        import jax, jax.numpy as jnp
        import numpy as np
        N_NODES = 3750
        N_EDGES = 60000
        IN_FEAT = 256
        OUT_FEAT = 256
        N_RELS = 8
        N_HEADS = 4
        HEAD_DIM = OUT_FEAT // N_HEADS
        LEAKY_SLOPE = 0.2
        feat_all = jnp.einsum('ni,rhid->rnhd', inputs, conv_weights)
        feat_src_e = feat_all[edge_type, edge_src]
        feat_dst_e = feat_all[edge_type, edge_dst]
        el = jnp.sum(feat_src_e * attn_l[edge_type], axis=-1)
        er = jnp.sum(feat_dst_e * attn_r[edge_type], axis=-1)
        e = jax.nn.leaky_relu(el + er, negative_slope=LEAKY_SLOPE)
        m = jax.ops.segment_max(e, edge_dst, num_segments=N_NODES)
        ex = jnp.exp(e - m[edge_dst])
        denom = jax.ops.segment_sum(ex, edge_dst, num_segments=N_NODES)
        alpha = ex / denom[edge_dst]
        h = jax.ops.segment_sum(alpha[..., None] * feat_src_e, edge_dst, num_segments=N_NODES)
        h = h.reshape(N_NODES, OUT_FEAT) + h_bias
        return h

    def _L1_gnn_ref(feats, W_gc, b_gc, W_res, b_res, Wg, bg, w1, b1, w2, b2, gamma, beta, src, dst):
        import jax, jax.numpy as jnp
        import numpy as np
        N_NODES = 2048
        N_EDGES = 32768
        D_IN = 256
        D = 256
        H = 512
        E = 64
        TOP_K = 2
        CAP = 1024
        BN_EPS = 1e-05

        def _moe_ff(x, Wg, bg, w1, b1, w2, b2):
            N = x.shape[0]
            logits = x @ Wg + bg
            vals, idx = jax.lax.top_k(logits, TOP_K)
            gates = jax.nn.softmax(vals, axis=-1)
            e_flat = idx.reshape(-1)
            g_flat = gates.reshape(-1)
            tok = jnp.arange(N * TOP_K) // TOP_K
            order = jnp.argsort(e_flat)
            e_s, tok_s, g_s = (e_flat[order], tok[order], g_flat[order])
            counts = jnp.bincount(e_flat, length=E)
            offs = jnp.concatenate([jnp.zeros((1,), counts.dtype), jnp.cumsum(counts)[:-1]])
            rank = jnp.arange(N * TOP_K) - offs[e_s]
            valid = rank < CAP
            slot = jnp.where(valid, e_s * CAP + rank, E * CAP)
            buf = jnp.zeros((E * CAP + 1, D), x.dtype).at[slot].set(x[tok_s])
            h = buf[:E * CAP].reshape(E, CAP, D)
            h1 = jax.nn.gelu(jnp.einsum('ecd,edh->ech', h, w1) + b1[:, None, :], approximate=False)
            h2 = jnp.einsum('ech,ehd->ecd', h1, w2) + b2[:, None, :]
            out_buf = h2.reshape(E * CAP, D)
            y_s = jnp.where(valid[:, None], out_buf[jnp.minimum(slot, E * CAP - 1)], 0.0)
            return jnp.zeros((N, D), x.dtype).at[tok_s].add(g_s[:, None] * y_s)

        def _forward(feats, W_gc, b_gc, W_res, b_res, Wg, bg, w1, b1, w2, b2, gamma, beta, src, dst):
            n = feats.shape[0]
            ones = jnp.ones((src.shape[0],), feats.dtype)
            deg_out = jnp.clip(jax.ops.segment_sum(ones, src, num_segments=n), 1.0)
            deg_in = jnp.clip(jax.ops.segment_sum(ones, dst, num_segments=n), 1.0)
            h = feats * jax.lax.rsqrt(deg_out)[:, None]
            m = jax.ops.segment_sum(h[src], dst, num_segments=n) * jax.lax.rsqrt(deg_in)[:, None]
            gc = m @ W_gc + b_gc
            x = gc + (feats @ W_res + b_res)
            core = _moe_ff(x, Wg, bg, w1, b1, w2, b2)
            y = x + core
            mean = jnp.mean(y, axis=0)
            var = jnp.mean((y - mean) ** 2, axis=0)
            return (y - mean) * jax.lax.rsqrt(var + BN_EPS) * gamma + beta
        return _forward(feats, W_gc, b_gc, W_res, b_res, Wg, bg, w1, b1, w2, b2, gamma, beta, src, dst)
    x = _layernorm(x + _L0_gnn_ref(x, L0_gnn_conv_weights, L0_gnn_attn_l, L0_gnn_attn_r, L0_gnn_h_bias, src, dst, edge_type_8), axis=-1)
    x = _layernorm(x + _L1_gnn_ref(x, L1_gnn_W_gc, L1_gnn_b_gc, L1_gnn_W_res, L1_gnn_b_res, L1_gnn_Wg, L1_gnn_bg, L1_gnn_w1, L1_gnn_b1, L1_gnn_w2, L1_gnn_b2, L1_gnn_gamma, L1_gnn_beta, src, dst), axis=-1)
    return x

_drawn_inputs = setup_inputs


def setup_inputs(seed=0):
    import zlib

    import numpy as np

    out = dict(_drawn_inputs(seed))
    spreads = {'L1_gnn_b_gc': (0.0, 0.1),
     'L1_gnn_b_res': (0.0, 0.1),
     'L1_gnn_bg': (0.0, 0.1),
     'L1_gnn_b1': (0.0, 0.1),
     'L1_gnn_b2': (0.0, 0.1),
     'L1_gnn_gamma': (1.0, 0.2),
     'L1_gnn_beta': (0.0, 0.1)}
    factors = {}
    for name, (base, spread) in spreads.items():
        noise = np.random.default_rng([zlib.crc32(name.encode()), seed]).standard_normal(out[name].shape)
        drawn = base * np.exp(spread * noise) if base else spread * noise
        out[name] = jnp.asarray(drawn.astype(out[name].dtype))
    for name, factor in factors.items():
        out[name] = (out[name] * factor).astype(out[name].dtype)
    return out
```

```python
from contextlib import ExitStack

import concourse.bass as bass
from concourse import mybir

ALU = mybir.AluOpType
ACT = mybir.ActivationFunctionType
AX = mybir.AxisListType
F32 = mybir.dt.float32
BF16 = mybir.dt.bfloat16
I32 = mybir.dt.int32
U32 = mybir.dt.uint32

P = 128
N = 3750
E = 120000
F = 256
R = 8
H = 4
HD = F // H
NT = -(-N // P)
NB = -(-E // P)
CH = 22
NPAIR = NB + NT - 1
NCH = -(-NPAIR // CH)
NPAIR = NCH * CH
NG = -(-NPAIR // P)
ROWS = CH * H
FULL = E // P
TAIL = E - FULL * P
LAST = N - (NT - 1) * P
FW = F + H
GW = FW + 1
GS = 264
BIG = 1.0e30
PAD_DST = 8191
PAD_SRC = 4095
NE = 64
HID = 512
CAP = 1024
NX = (2 * N + NE * (P - 1)) // P
assert NPAIR <= NG * P and NB <= NG * P


class Chain:

    def __init__(self, eng, sem, base=0):
        self.eng, self.sem, self.base, self.n = eng, sem, base, 0

    def link(self, ins):
        self.n += 1
        ins.then_inc(self.sem, 1)
        self.eng.wait_ge(self.sem, self.base + self.n)


def col(ap, n):
    return ap.rearrange("p (m o) -> p m o", o=1).to_broadcast([ap.shape[0], ap.shape[1], n])


def clear(nc, sems):
    nc.clear_and_free_semaphores(sems)
    nc.all_engine_barrier(sem_only=True)


def setup_phase(nc, C, D):
    ctx, sems = ExitStack(), []
    with ctx:
        def sb(name, shape, dt=F32):
            return ctx.enter_context(nc.sbuf_tensor(name, shape, dt))

        def sem(name):
            sems.append(nc.alloc_semaphore(name))
            return sems[-1]

        raw = sb("raw", [P, 3, NG, P], I32)
        rec = sb("rec", [P, NG, 4, P])
        rawsrc = sb("rawsrc", [P, NG, P])
        pairrec = sb("pairrec", [P, NG, 4, P])
        loc = sb("loc", [P, NG, P])
        junk = sb("junk", [P, NG * P])
        below = sb("below", [P, NT + 1])
        starts = sb("starts", [P, NT + 1])
        istart = sb("istart", [P, NT + 1], I32)
        firstb = sb("firstb", [P, NT + 1])
        endb = sb("endb", [P, NT])
        some = sb("some", [P, NT])
        count = sb("count", [P, NT])
        offend = sb("offend", [P, NT])
        shift = sb("shift", [P, NT + 1])
        step = sb("step", [P, NT])
        ones_t = sb("ones_t", [P, NT])
        pid = sb("pid", [P, NG])
        ge = sb("ge", [P, NG, NT])
        gest = sb("gest", [P, NG, NT])
        tp = sb("tp", [P, NG])
        tbase = sb("tbase", [P, NG])
        blk = sb("blk", [P, NG])
        blki = sb("blki", [P, NG], I32)
        ps = ctx.enter_context(nc.psum_tensor("ps_setup", [P, 2, 512], F32))
        pcount = ctx.enter_context(nc.psum_tensor("pcount", [P, 512], F32))
        prow = ctx.enter_context(nc.psum_tensor("prow", [1, 2, 512], F32))

        filled = sem("pads_filled")
        loaded = sem("edges_loaded")
        xloaded = sem("x_loaded")
        wloaded = sem("w_loaded")
        consts = sem("consts_ready")
        dch = sem("dve_setup")
        recs_ready = sem("recs_ready")
        recs_stored = sem("recs_stored")
        below_ready = sem("below_ready")
        starts_ready = sem("starts_ready")
        blk_ready = sem("blk_ready")
        gathered = C.first_slots
        loc_ready = sem("loc_ready")
        turned = sem("turned")
        evacuated = sem("turned_evacuated")
        tp_turned = sem("tp_turned")
        ctx.callback(clear, nc, sems)
        block = ctx.enter_context(nc.Block())

        @block.sync
        def _(sp):
            sp.wait_ge(filled, 4)
            for k, a in enumerate((D.src, D.dst, D.typ)):
                whole = (FULL // P) * P
                sp.dma_start(raw[:, k, 0:FULL // P, :],
                             a[0:whole * P].rearrange("(g p e) -> p g e", p=P, e=P)).then_inc(loaded, 16)
                sp.dma_start(raw[0:FULL - whole, k, FULL // P, :],
                             a[whole * P:FULL * P].rearrange("(p e) -> p e", e=P)).then_inc(loaded, 16)
                sp.dma_start(raw[FULL - whole:FULL - whole + 1, k, FULL // P, 0:TAIL],
                             a[FULL * P:E].rearrange("(p e) -> p e", p=1)).then_inc(loaded, 16)
            sp.dma_start(C.x[:, 0:NT - 1, :],
                         D.x[0:(NT - 1) * P, :].rearrange("(t p) f -> p t f", p=P)).then_inc(xloaded, 16)
            sp.dma_start(C.x[0:LAST, NT - 1, :], D.x[(NT - 1) * P:N, :]).then_inc(xloaded, 16)
            sp.wait_ge(recs_ready, 1)
            sp.dma_start(D.rec.rearrange("(g p) f -> p g f", p=P),
                         rec[:, :, :, :].rearrange("p g k e -> p g (k e)")).then_inc(recs_stored, 16)
            sp.wait_ge(xloaded, 32)

        @block.gpsimd
        def _(g):
            g.memset(raw[:, 0, :, :], PAD_SRC).then_inc(filled, 1)
            g.memset(raw[:, 1, :, :], PAD_DST).then_inc(filled, 1)
            g.memset(raw[:, 2, :, :], 0).then_inc(filled, 1)
            g.memset(C.x[:, NT - 1, :], 0.0).then_inc(filled, 1)
            g.iota(C.iota[:, :], [[1, P]], base=0, channel_multiplier=0,
                   allow_small_or_imprecise_dtypes=True).then_inc(consts, 1)
            g.iota(C.ioch[:, :], [[0, 1]], base=0, channel_multiplier=1,
                   allow_small_or_imprecise_dtypes=True).then_inc(consts, 1)
            g.iota(pid[:, :], [[P, NG]], base=0, channel_multiplier=1,
                   allow_small_or_imprecise_dtypes=True).then_inc(consts, 1)
            g.memset(C.ones[:, :], 1.0).then_inc(consts, 1)
            g.wait_ge(recs_stored, 16)
            g.wait_ge(blk_ready, 1)
            for k in range(NG):
                g.indirect_dma_start(pairrec[:, k, :, :].rearrange("p k e -> p (k e)"), None, D.rec,
                                     bass.IndirectOffsetOnAxis(ap=blki[:, k:k + 1], axis=0)
                                     ).then_inc(gathered[k].sem, 16)

        @block.vector
        def _(dve):
            v = nc.vector
            c = Chain(dve, dch)
            dve.wait_ge(consts, 4)
            c.link(v.tensor_scalar(C.ident[:, :], C.iota[:, :], C.ioch[:, 0:1], None, ALU.is_equal))
            c.link(v.tensor_scalar(C.iota2[:, :], C.iota[:, :], -1.0, float(P - 1), ALU.mult, ALU.add))
            c.link(v.tensor_scalar(C.anti[:, :], C.iota2[:, :], C.ioch[:, 0:1], None, ALU.is_equal))
            c.link(v.memset(ones_t[:, :], 1.0))
            dve.wait_ge(loaded, 9 * 16)
            c.link(v.tensor_copy(rawsrc[:, :, :], raw[:, 0, :, :]))
            c.link(v.tensor_scalar(rec[:, :, 1, :], raw[:, 0, :, :], float(N - 1), None, ALU.min))
            c.link(v.tensor_copy(rec[:, :, 2, :], raw[:, 1, :, :]))
            c.link(v.tensor_copy(rec[:, :, 3, :], raw[:, 2, :, :]))
            c.link(v.scalar_tensor_tensor(rec[:, :, 0, :], rec[:, :, 1, :], float(R), rec[:, :, 3, :],
                                          ALU.mult, ALU.add))
            v.tensor_copy(junk[:, 0:1], rec[:, 0, 0, 0:1]).then_inc(recs_ready, 1)
            c.link(v.memset(below[:, 0:1], 0.0))
            dsts = rec[:, :, 2, :]
            jv = junk[:, :].rearrange("p (g e) -> p g e", e=P)
            for t in range(1, NT + 1):
                c.link(v.tensor_scalar(jv, dsts, float(P * t), 0.0, ALU.is_lt, ALU.add,
                                       accum_out=below[:, t:t + 1]))
            v.tensor_copy(junk[:, 0:1], below[:, 0:1]).then_inc(below_ready, 1)
            dve.wait_ge(starts_ready, 1)
            c.link(v.tensor_copy(starts[:, :], pcount[:, 0:NT + 1]))
            c.link(v.tensor_copy(istart[:, :], starts[:, :]))
            c.link(v.tensor_scalar(istart[:, :], istart[:, :], 7, None, ALU.arith_shift_right))
            c.link(v.tensor_copy(firstb[:, :], istart[:, :]))
            c.link(v.tensor_scalar(junk[:, 0:NT], starts[:, 1:NT + 1], float(P - 1), None, ALU.add))
            c.link(v.tensor_copy(istart[:, 0:NT], junk[:, 0:NT]))
            c.link(v.tensor_scalar(istart[:, 0:NT], istart[:, 0:NT], 7, None, ALU.arith_shift_right))
            c.link(v.tensor_copy(endb[:, :], istart[:, 0:NT]))
            c.link(v.tensor_tensor(some[:, :], starts[:, 1:NT + 1], starts[:, 0:NT], ALU.is_gt))
            c.link(v.tensor_tensor(count[:, :], endb[:, :], firstb[:, 0:NT], ALU.subtract))
            c.link(v.tensor_tensor(count[:, :], count[:, :], some[:, :], ALU.mult))
            c.link(v.tensor_tensor_scan(offend[:, :], ones_t[:, :], count[:, :], 0.0, ALU.mult, ALU.add))
            c.link(v.tensor_copy(shift[:, 0:1], firstb[:, 0:1]))
            c.link(v.tensor_tensor(shift[:, 1:NT + 1], firstb[:, 1:NT + 1], offend[:, :], ALU.subtract))
            c.link(v.tensor_tensor(step[:, :], shift[:, 1:NT + 1], shift[:, 0:NT], ALU.subtract))
            offb = offend[:, :].rearrange("p (o t) -> p o t", o=1).to_broadcast([P, NG, NT])
            stepb = step[:, :].rearrange("p (o t) -> p o t", o=1).to_broadcast([P, NG, NT])
            c.link(v.tensor_tensor(ge[:, :, :], offb, col(pid[:, :], NT), ALU.is_le))
            c.link(v.tensor_tensor(gest[:, :, :], ge[:, :, :], stepb, ALU.mult))
            c.link(v.tensor_reduce(tp[:, :], ge[:, :, :], AX.X, ALU.add))
            c.link(v.tensor_reduce(blk[:, :], gest[:, :, :], AX.X, ALU.add))
            c.link(v.tensor_tensor(blk[:, :], blk[:, :], pid[:, :], ALU.add))
            c.link(v.tensor_scalar(blk[:, :], blk[:, :], float(NB - 1), 0.0, ALU.min, ALU.max))
            c.link(v.tensor_scalar(tbase[:, :], tp[:, :], float(P), None, ALU.mult))
            v.tensor_copy(blki[:, :], blk[:, :]).then_inc(blk_ready, 1)
            for k in range(NG):
                dve.wait_ge(gathered[k].sem, gathered[k].base + 16)
                v.tensor_scalar(loc[:, k, :], pairrec[:, k, 2, :], tbase[:, k:k + 1], None,
                                ALU.subtract).then_inc(loc_ready, 1)
            dests = [C.fidx, C.srci, C.dstf, C.typf, C.locf, C.srcraw]
            n = 0
            for k in range(NG):
                for j, d in enumerate(dests):
                    w = min(P, (NB if j == 5 else NPAIR) - k * P)
                    dve.wait_ge(turned, n + 1)
                    v.tensor_copy(d[:, k * P:k * P + w], ps[:, n % 2, 0:w]).then_inc(evacuated, 1)
                    n += 1
            dve.wait_ge(tp_turned, 1)
            v.tensor_copy(C.tpi[:, 0:NG * P], prow[0:1, :, :].rearrange("o a b -> o (a b)")).then_inc(evacuated, 1)

        @block.tensor
        def _(pe):
            pe.wait_ge(below_ready, 1)
            nc.tensor.matmul(pcount[:, 0:NT + 1], C.ones[:, :], below[:, :], start=True,
                             stop=True).then_inc(starts_ready, 1)
            n = 0
            for k in range(NG):
                pe.wait_ge(loc_ready, k + 1)
                for a in (pairrec[:, k, 0, :], pairrec[:, k, 1, :], pairrec[:, k, 2, :],
                          pairrec[:, k, 3, :], loc[:, k, :], rawsrc[:, k, :]):
                    if n >= 2:
                        pe.wait_ge(evacuated, n - 1)
                    nc.tensor.transpose(ps[:, n % 2, 0:P], a, C.ident[:, :]).then_inc(turned, 1)
                    n += 1
            for k in range(NG):
                last = nc.tensor.matmul(prow[0:1, k // 4, (k % 4) * P:(k % 4 + 1) * P], tp[:, k:k + 1],
                                        C.ident[:, :], start=True, stop=True)
            last.then_inc(tp_turned, 1)

    for slot in gathered:
        slot.base += 16


HB = -(-NB // NT)


def table_phase(nc, C, D):
    ctx, sems = ExitStack(), []
    with ctx:
        def sb(name, shape, dt=F32):
            return ctx.enter_context(nc.sbuf_tensor(name, shape, dt))

        def sem(name):
            sems.append(nc.alloc_semaphore(name))
            return sems[-1]

        w = sb("conv_w", [P, 2, R * F])
        att = sb("att", [P, 2, R * F])
        prod = sb("att_prod", [P, R * F])
        watt = sb("watt", [P, 2, 2, R * H])
        xin = [sb(f"xin{u}", [P, F]) for u in range(2)]
        xt = [sb(f"xt{u}", [P, 2, P]) for u in range(2)]
        row = [sb(f"trow{u}", [P, R, FW]) for u in range(2)]
        low = sb("src_low", [P, NT * HB])
        high = sb("src_high", [P, NT * HB])
        isrc = sb("src_int", [P, NT * HB], I32)
        ihalf = sb("src_half", [P, NT * HB], I32)
        onelow = [sb(f"onelow{u}", [P, HB, P], BF16) for u in range(2)]
        onehigh = [sb(f"onehigh{u}", [P, HB, NT], BF16) for u in range(2)]
        zero = sb("zero_row", [P, F])
        zerob = sb("zero_b", [P, P], BF16)
        pfeat = ctx.enter_context(nc.psum_tensor("pfeat", [P, 4, 512], F32))
        px = ctx.enter_context(nc.psum_tensor("px", [P, 512], F32))
        pel = ctx.enter_context(nc.psum_tensor("pel", [P, 512], F32))
        phist = ctx.enter_context(nc.psum_tensor("phist", [P, 512], F32))

        w_loaded = sem("conv_loaded")
        att_loaded = sem("att_loaded")
        dch = sem("dve_table")
        zeros = sem("zeros_ready")
        buf_zeroed = sem("buf_zeroed")
        prep = sem("prep_done")
        xin_ready = sem("xin_ready")
        x_turned = sem("x_turned")
        xt_ready = sem("xt_ready")
        hot_ready = sem("hot_ready")
        hot_free = sem("hot_free")
        feat_ready = sem("feat_ready")
        feat_free = sem("feat_free")
        el_ready = sem("el_ready")
        row_ready = sem("row_ready")
        row_free = sem("row_free")
        row_stored = [sem(f"row_stored{u}") for u in range(2)]
        hist_ready = sem("hist_ready")
        ctx.callback(clear, nc, sems)
        block = ctx.enter_context(nc.Block())

        @block.sync
        def _(sp):
            for k in range(2):
                sp.dma_start(w[:, k, :].rearrange("p (a d) -> p a d", d=HD),
                             D.conv[:, :, k * P:(k + 1) * P, :].rearrange("r h k d -> k (r h) d")
                             ).then_inc(w_loaded, 16)
            for k, a in enumerate((D.attl, D.attr)):
                flat = a.rearrange("r h d -> (r h d)").rearrange("(o f) -> o f", o=1)
                sp.dma_start(att[:, k, :], flat.to_broadcast([P, R * F])).then_inc(att_loaded, 16)
            with sp.Fori(0, NT // 2) as i:
                for u in range(2):
                    sp.wait_ge(row_ready, 2 * i + u + 2)
                    sp.dma_start(D.tab.rearrange("(t p) f -> t p f", p=P)[bass.ds(2 * i + u, 1), :, :]
                                 .rearrange("o p f -> (o p) f"),
                                 row[u][:, :, :].rearrange("p r f -> p (r f)")).then_inc(row_stored[u], 16)
                    sp.wait_ge(row_stored[u], 16 * i + 16)
                    sp.sem_inc(row_free, 1)

        @block.scalar
        def _(act):
            act.wait_ge(zeros, 1)
            act.dma_start(D.buf.rearrange("(p t) f -> p t f", p=P),
                          zero[:, :].rearrange("p (o f) -> p o f", o=1).to_broadcast([P, NX, F])
                          ).then_inc(buf_zeroed, 16)
            act.sem_inc(row_free, 2)
            act.sem_inc(row_ready, 1)
            act.sem_inc(feat_free, 4)
            with act.Fori(0, NT // 2) as i:
                for u in range(2):
                    act.wait_ge(row_free, 2 * i + u + 1)
                    for q in range(4):
                        act.wait_ge(feat_ready, 4 * (2 * i + u) + q + 1)
                        nc.scalar.activation(row[u][:, 2 * q:2 * q + 2, 0:F],
                                             pfeat[:, q, :].rearrange("p (r f) -> p r f", r=2),
                                             ACT.Copy).then_inc(feat_free, 1)
                    act.wait_ge(el_ready, 2 * i + u + 3)
                    nc.scalar.activation(row[u][:, :, F:FW], pel[:, 0:R * H].rearrange("p (r h) -> p r h", h=H),
                                         ACT.Copy)
                    nc.scalar.activation(C.er[:, bass.ds(2 * i + u, 1), :],
                                         pel[:, R * H:2 * R * H].rearrange("p (o r) -> p o r", o=1),
                                         ACT.Copy).then_inc(row_ready, 1)
            act.wait_ge(hist_ready, 1)
            nc.scalar.activation(C.dego[:, :], phist[:, 0:NT], ACT.Copy)
            act.wait_ge(buf_zeroed, 16)

        @block.vector
        def _(dve):
            v = nc.vector
            c = Chain(dve, dch)
            v.memset(zero[:, :], 0.0).then_inc(zeros, 1)
            v.memset(C.er[:, NT, :], 0.0)
            c.link(v.memset(zerob[:, :], 0.0))
            c.link(v.memset(low[:, :], float(PAD_SRC)))
            c.link(v.tensor_copy(low[:, 0:NB], C.srcraw[:, :]))
            c.link(v.tensor_copy(isrc[:, :], low[:, :]))
            c.link(v.tensor_scalar(ihalf[:, :], isrc[:, :], P - 1, None, ALU.bitwise_and))
            c.link(v.tensor_copy(low[:, :], ihalf[:, :]))
            c.link(v.tensor_scalar(ihalf[:, :], isrc[:, :], 7, None, ALU.arith_shift_right))
            c.link(v.tensor_copy(high[:, :], ihalf[:, :]))
            dve.wait_ge(w_loaded, 32)
            dve.wait_ge(att_loaded, 32)
            for k in range(2):
                for j in range(2):
                    c.link(v.tensor_tensor(prod[:, :], w[:, k, :], att[:, j, :], ALU.mult))
                    c.link(v.tensor_reduce(watt[:, k, j, :], prod[:, :].rearrange("p (a d) -> p a d", d=HD),
                                           AX.X, ALU.add))
            dve.sem_inc(xt_ready, 1)
            dve.sem_inc(prep, 1)
            with dve.Fori(0, NT // 2) as i:
                for u in range(2):
                    v.tensor_copy(xin[u][:, :], C.x[:, bass.ds(2 * i + u, 1), :].rearrange("p o f -> p (o f)")
                                  ).then_inc(xin_ready, 1)
                    dve.wait_ge(hot_free, 2 * i + u + 1)
                    at = bass.ds((2 * i + u) * HB, HB)
                    v.tensor_tensor(onelow[u][:, :, :], col(low[:, at], P),
                                    C.iota[:, :].rearrange("p (o f) -> p o f", o=1).to_broadcast([P, HB, P]),
                                    ALU.is_equal)
                    v.tensor_tensor(onehigh[u][:, :, :], col(high[:, at], NT),
                                    C.iota[:, 0:NT].rearrange("p (o f) -> p o f", o=1).to_broadcast([P, HB, NT]),
                                    ALU.is_equal).then_inc(hot_ready, 1)
                    dve.wait_ge(x_turned, 2 * i + u + 1)
                    dve.wait_ge(el_ready, 2 * i + u + 1)
                    v.tensor_copy(xt[u][:, :, :], px[:, 0:F].rearrange("p (c n) -> p c n", c=2)
                                  ).then_inc(xt_ready, 1)

        @block.tensor
        def _(pe):
            pe.wait_ge(prep, 1)
            pe.sem_inc(hot_free, 2)
            pe.sem_inc(el_ready, 2)
            nc.tensor.matmul(phist[:, 0:NT], zerob[:, :], zerob[:, 0:NT], start=True, stop=False)
            with pe.Fori(0, NT // 2) as i:
                for u in range(2):
                    t = 2 * i + u
                    pe.wait_ge(xin_ready, t + 1)
                    pe.wait_ge(xt_ready, t + 1)
                    for k in range(2):
                        last = nc.tensor.transpose(px[:, k * P:(k + 1) * P], xin[u][:, k * P:(k + 1) * P],
                                                   C.ident[:, :])
                    last.then_inc(x_turned, 1)
                    pe.wait_ge(hot_ready, t + 1)
                    for b in range(HB):
                        last = nc.tensor.matmul(phist[:, 0:NT], onelow[u][:, b, :], onehigh[u][:, b, :],
                                                start=False, stop=False)
                    last.then_inc(hot_free, 1)
                    pe.wait_ge(xt_ready, t + 2)
                    for q in range(4):
                        pe.wait_ge(feat_free, 4 * t + q + 1)
                        for k in range(2):
                            last = nc.tensor.matmul(pfeat[:, q, :], xt[u][:, k, :], w[:, k, q * 512:(q + 1) * 512],
                                                    start=(k == 0), stop=(k == 1))
                        last.then_inc(feat_ready, 1)
                    pe.wait_ge(row_ready, t + 1)
                    for k in range(2):
                        last = nc.tensor.matmul(pel[:, 0:2 * R * H], xt[u][:, k, :],
                                                watt[:, k, :, :].rearrange("p l a -> p (l a)"),
                                                start=(k == 0), stop=(k == 1))
                    last.then_inc(el_ready, 1)
            nc.tensor.matmul(phist[:, 0:NT], zerob[:, :], zerob[:, 0:NT], start=False,
                             stop=True).then_inc(hist_ready, 1)


GR = [(b, min(4, CH - b)) for b in range(0, CH, 4)]
NGR = len(GR)


def attention_phase(nc, C, D):
    ctx, sems = ExitStack(), []
    with ctx:
        def sb(name, shape, dt=F32):
            return ctx.enter_context(nc.sbuf_tensor(name, shape, dt))

        def sem(name):
            sems.append(nc.alloc_semaphore(name))
            return sems[-1]

        gat = [sb(f"gat{u}", [P, CH, GS]) for u in range(2)]
        hot = [sb(f"hot{u}", [P, CH, P]) for u in range(2)]
        hott = sb("hott", [P, CH, P])
        gidx = [sb(f"gidx{u}", [P, CH], I32) for u in range(2)]
        tmask = sb("tmask", [P, CH, R])
        ertmp = sb("ertmp", [P, CH, R, H])
        ersel = [sb(f"ersel{u}", [P, H, CH]) for u in range(2)]
        sc = sb("scores", [P, H, CH])
        d4 = sb("dst4", [P, H, CH])
        sd = sb("sdrows", [ROWS, 2, P])
        neg = sb("neg", [ROWS, P + 1])
        fwd = sb("fwd", [ROWS, P])
        bwd = sb("bwd", [ROWS, P])
        mx = sb("mx", [ROWS, P])
        cols = sb("cols", [ROWS, 2])
        row1 = sb("row1", [1, H, CH + 1])
        nlink = sb("nlink", [1, H, CH + 1])
        nsing = sb("nsing", [1, H, CH])
        af = sb("af", [1, H, CH + 1])
        ab = sb("ab", [1, H, CH + 1])
        vf = sb("vf", [1, H, CH + 1])
        vb = sb("vb", [1, H, CH + 1])
        cof = sb("cof", [1, H, CH + 1])
        cob = sb("cob", [1, H, CH + 1])
        carry = sb("carry", [1, 2, H * CH])
        fac = sb("fac", [1, 4, H])
        hot0 = sb("hotfirst", [1, 2, P])
        ex = sb("ex", [P, H, CH])
        exin = sb("exin", [P, H, CH])
        pt = ctx.enter_context(nc.psum_tensor("pt", [P, 2, 512], F32))
        per = ctx.enter_context(nc.psum_tensor("per", [P, 2, 512], F32))
        psd = ctx.enter_context(nc.psum_tensor("psd", [P, 512], F32))
        prow = ctx.enter_context(nc.psum_tensor("prow2", [P, 512], F32))
        pacc = ctx.enter_context(nc.psum_tensor("pacc", [P, 2, 512], F32))

        gathered1 = [C.slots[u * CH:(u + 1) * CH] for u in range(2)]
        gathered = sem("chunk_gathered")
        idx_ready = sem("idx_ready")
        hot_ready = sem("hot_ready2")
        turned = sem("hot_turned")
        copied = sem("hott_copied")
        er_ready = sem("er_ready")
        ers_ready = sem("ers_ready")
        s_ready = sem("s_ready")
        sd_turned = sem("sd_turned")
        sd_copied = sem("sd_copied")
        fb_ready = sem("fb_ready")
        rows_ready = sem("rows_ready")
        carries_ready = sem("carries_ready")
        cols_ready = sem("cols_ready")
        fac_ready = sem("fac_ready")
        facm_ready = sem("facm_ready")
        m_ready = sem("m_ready")
        mt_ready = sem("mt_ready")
        exin_ready = sem("exin_ready")
        ex_ready = sem("ex_ready")
        scaled = sem("scaled")
        mm_done = sem("mm_done")
        acc_done = sem("acc_done")
        sc_ready = sem("sc_ready")
        ch0 = sem("dve_attn0")
        ch1 = sem("dve_attn1")
        ch2 = sem("dve_attn2")
        ctx.callback(clear, nc, sems)
        block = ctx.enter_context(nc.Block())

        @block.gpsimd
        def _(g):
            with g.Fori(0, NCH // 2) as i:
                for u in range(2):
                    k = 2 * i + u
                    g.wait_ge(mm_done, CH * k + CH)
                    g.tensor_copy(gidx[u][:, :], C.fidx[:, bass.ds(k * CH, CH)]).then_inc(idx_ready, 1)
                    g.wait_ge(idx_ready, k + 1)
                    g.nop(nofuse=True)
                    for b in range(CH):
                        g.indirect_dma_start(gat[u][:, b, 0:FW], None, D.tab.rearrange("n (r f) -> (n r) f", f=FW),
                                             bass.IndirectOffsetOnAxis(ap=gidx[u][:, b:b + 1], axis=0)
                                             ).then_inc(gathered1[u][b].sem, 16)

        @block.sync
        def _(sp):
            with sp.Fori(0, NCH // 2) as i:
                for u in range(2):
                    for b in range(CH):
                        sp.wait_ge(gathered1[u][b].sem, gathered1[u][b].base + 16 * i + 16)
                    sp.sem_inc(gathered, 1)

        @block.scalar
        def _(act):
            a = nc.scalar

            def ahead(k):
                act.wait_ge(er_ready, k + 1)
                for n, (b, m) in enumerate(GR):
                    act.wait_ge(turned, NGR * k + n + 1)
                    a.activation(hott[:, b:b + m, :], pt[:, n % 2, 0:m * P].rearrange("p (b e) -> p b e", e=P),
                                 ACT.Copy).then_inc(copied, 1)

            def chunk(k, more):
                act.wait_ge(sd_turned, k + 1)
                a.activation(sd[:, :, :], psd[0:ROWS, 0:2 * P].rearrange("p (a e) -> p a e", e=P),
                             ACT.Copy).then_inc(sd_copied, 1)
                act.wait_ge(fac_ready, k + 1)
                a.activation(fac[:, 1, :], fac[:, 0, :], ACT.Exp).then_inc(facm_ready, 1)
                act.wait_ge(exin_ready, k + 1)
                a.activation(ex[:, :, :], exin[:, :, :], ACT.Exp).then_inc(ex_ready, 1)
                if more:
                    ahead(k + 1)

            ahead(0)
            with act.Fori(0, NCH // 2 - 1) as i:
                for u in range(2):
                    chunk(2 * i + u, True)
            chunk(NCH - 2, True)
            chunk(NCH - 1, False)

        @block.vector
        def _(dve):
            v = nc.vector
            c0 = Chain(dve, ch0)
            for u in range(2):
                c0.link(v.memset(gat[u][:, :, FW:GW], 1.0))
            c0.link(v.memset(C.acc[:, :, :], 0.0))
            c0.link(v.memset(neg[:, 0:1], 0.0))
            c0.link(v.memset(neg[:, P:P + 1], 0.0))
            c0.link(v.memset(row1[:, :, 0:1], -1.0))
            c0.link(v.memset(nlink[:, :, CH:CH + 1], -BIG))
            c0.link(v.memset(af[:, :, 0:1], -BIG))
            c0.link(v.memset(ab[:, :, CH:CH + 1], -BIG))
            c0.link(v.memset(vf[:, :, 0:1], -BIG))
            c0.link(v.memset(vb[:, :, CH:CH + 1], -BIG))
            c0.link(v.memset(fac[:, 3, :], 1.0))
            dve.sem_inc(ers_ready, 1)
            dve.sem_inc(acc_done, 2)
            N1, N2 = 3, 27

            def ahead(k, u):
                c = Chain(dve, ch1, k * N1)
                at = bass.ds(k * CH, CH) if not isinstance(k, int) else slice(k * CH, k * CH + CH)
                v.tensor_tensor(hot[u][:, :, :], col(C.locf[:, at], P),
                                C.iota[:, :].rearrange("p (o f) -> p o f", o=1).to_broadcast([P, CH, P]),
                                ALU.is_equal).then_inc(hot_ready, 1)
                c.link(v.tensor_tensor(tmask[:, :, :], col(C.typf[:, at], R),
                                       C.iota[:, 0:R].rearrange("p (o f) -> p o f", o=1).to_broadcast([P, CH, R]),
                                       ALU.is_equal))
                dve.wait_ge(er_ready, k + 2)
                for n, (b, m) in enumerate(((0, 16), (16, CH - 16))):
                    ins = v.tensor_tensor(ertmp[:, b:b + m, :, :],
                                          per[:, n, 0:m * R * H].rearrange("p (b r h) -> p b r h", r=R, h=H),
                                          tmask[:, b:b + m, :].rearrange("p b (r o) -> p b r o", o=1)
                                          .to_broadcast([P, m, R, H]), ALU.mult)
                    c.link(ins)
                assert c.n == N1
                v.tensor_reduce(ersel[u][:, :, :].rearrange("p h b -> p b h"),
                                ertmp[:, :, :, :].rearrange("p b r h -> p b h r"), AX.X, ALU.add
                                ).then_inc(ers_ready, 1)

            def chunk(k, u, more):
                c = Chain(dve, ch2, k * N2)
                at = bass.ds(k * CH, CH) if not isinstance(k, int) else slice(k * CH, k * CH + CH)
                at0 = bass.ds(k * CH, 1) if not isinstance(k, int) else slice(k * CH, k * CH + 1)
                dve.wait_ge(ers_ready, k + 2)
                dve.wait_ge(gathered, k + 1)
                c.link(v.tensor_tensor(sc[:, :, :].rearrange("p h b -> p b h"), gat[u][:, :, F:FW],
                                       ersel[u][:, :, :].rearrange("p h b -> p b h"), ALU.add))
                v.tensor_copy(d4[:, :, :], C.dstf[:, at].rearrange("p (o b) -> p o b", o=1)
                              .to_broadcast([P, H, CH]))
                v.scalar_tensor_tensor(sc[:, :, :], sc[:, :, :], 0.2, sc[:, :, :], ALU.mult, ALU.max
                                       ).then_inc(s_ready, 1)
                c.link(v.tensor_scalar(hot0[:, 0, :], C.iota[0:1, :], C.locf[0:1, at0], None, ALU.is_equal))
                c.link(v.tensor_scalar(hot0[:, 1, :], hot0[:, 0, :], -1.0, 1.0, ALU.mult, ALU.add))
                dve.wait_ge(sd_copied, k + 1)
                c.link(v.tensor_tensor(neg[:, 1:P], sd[:, 1, 1:P], sd[:, 1, 0:P - 1], ALU.is_equal))
                c.link(v.tensor_scalar(neg[:, 1:P], neg[:, 1:P], 1.0, BIG, ALU.subtract, ALU.mult))
                v.tensor_tensor_scan(fwd[:, :], neg[:, 0:P], sd[:, 0, :], -BIG, ALU.add, ALU.max)
                v.tensor_tensor_scan(bwd[:, ::-1], neg[:, P:0:-1], sd[:, 0, ::-1], -BIG, ALU.add,
                                     ALU.max).then_inc(fb_ready, 1)
                dve.wait_ge(rows_ready, k + 1)
                pr = prow[0:1, 0:4 * ROWS].rearrange("o (a h b) -> o a h b", a=4, h=H)
                lf, ff, df, dl = (pr[:, j, :, :] for j in range(4))
                c.link(v.tensor_copy(row1[:, :, 1:CH + 1], dl))
                c.link(v.tensor_tensor(nlink[:, :, 0:CH], df, row1[:, :, 0:CH], ALU.is_equal))
                c.link(v.tensor_tensor(nsing[:, :, :], df, row1[:, :, 1:CH + 1], ALU.is_equal))
                c.link(v.tensor_copy(fac[:, 2, :], nlink[:, :, 0:1].rearrange("o h b -> o (h b)")))
                c.link(v.tensor_scalar(nlink[:, :, 0:CH], nlink[:, :, 0:CH], 1.0, BIG, ALU.subtract, ALU.mult))
                c.link(v.tensor_scalar(nsing[:, :, :], nsing[:, :, :], 1.0, BIG, ALU.subtract, ALU.mult))
                c.link(v.tensor_tensor(af[:, :, 1:CH + 1], nlink[:, :, 0:CH], nsing[:, :, :], ALU.add))
                c.link(v.tensor_tensor(ab[:, :, 0:CH], nlink[:, :, 1:CH + 1], nsing[:, :, :], ALU.add))
                c.link(v.tensor_copy(vf[:, :, 1:CH + 1], lf))
                c.link(v.tensor_copy(vb[:, :, 0:CH], ff))

                def flat(t):
                    return t[:, :, :].rearrange("o h b -> o (h b)")

                c.link(v.tensor_tensor_scan(flat(cof), flat(af), flat(vf), -BIG, ALU.add, ALU.max))
                c.link(v.tensor_tensor_scan(flat(cob)[:, ::-1], flat(ab)[:, ::-1], flat(vb)[:, ::-1], -BIG,
                                            ALU.add, ALU.max))
                cv = carry[:, :, :].rearrange("o a (h b) -> o a h b", h=H)
                c.link(v.tensor_tensor(cv[:, 0, :, :], cof[:, :, 0:CH], nlink[:, :, 0:CH], ALU.add))
                v.tensor_tensor(cv[:, 1, :, :], cob[:, :, 1:CH + 1], nlink[:, :, 1:CH + 1], ALU.add
                                ).then_inc(carries_ready, 1)
                c.link(v.tensor_tensor(fac[:, 0, :].rearrange("o (h b) -> o h b", b=1), vf[:, :, 0:1],
                                       cob[:, :, 0:1], ALU.subtract))
                c.link(v.tensor_scalar(fac[:, 0, :], fac[:, 0, :], 0.0, None, ALU.min))
                v.tensor_tensor(fac[:, 0, :], fac[:, 0, :], fac[:, 2, :], ALU.mult).then_inc(fac_ready, 1)
                c.link(v.tensor_copy(vf[:, :, 0:1], cof[:, :, CH:CH + 1]))
                c.link(v.tensor_copy(row1[:, :, 0:1], row1[:, :, CH:CH + 1]))
                dve.wait_ge(cols_ready, k + 1)
                c.link(v.tensor_copy(cols[:, :], psd[0:ROWS, 384:386]))
                v.tensor_tensor_scan(fwd[:, :], neg[:, 0:P], sd[:, 0, :], cols[:, 0:1], ALU.add, ALU.max)
                c.link(v.tensor_tensor_scan(bwd[:, ::-1], neg[:, P:0:-1], sd[:, 0, ::-1], cols[:, 1:2],
                                            ALU.add, ALU.max))
                v.tensor_tensor(mx[:, :], fwd[:, :], bwd[:, :], ALU.max).then_inc(m_ready, 1)
                dve.wait_ge(mt_ready, k + 1)
                v.tensor_tensor(exin[:, :, :], sc[:, :, :],
                                psd[:, 256:256 + ROWS].rearrange("p (h b) -> p h b", h=H), ALU.subtract
                                ).then_inc(exin_ready, 1)
                if more:
                    ahead(k + 1, 1 - u)
                dve.wait_ge(ex_ready, k + 1)
                c.link(v.tensor_copy(gat[u][:, :, F:FW], ex[:, :, :].rearrange("p h b -> p b h")))
                t0 = dve.value_load(C.tpi[0:1, at0], min_val=0, max_val=NT)
                dve.wait_ge(facm_ready, k + 1)
                dve.wait_ge(rows_ready, k + 1)
                dve.wait_ge(sc_ready, k + 1)
                dve.wait_ge(acc_done, CH * k + 2)
                tile = C.acc[:, bass.ds(t0, 1), :].rearrange("p o f -> p (o f)")
                fv = prow[:, 400:400 + H]
                c.link(v.tensor_tensor(tile[:, 0:F].rearrange("p (h d) -> p h d", h=H),
                                       tile[:, 0:F].rearrange("p (h d) -> p h d", h=H), col(fv, HD), ALU.mult))
                c.link(v.tensor_tensor(tile[:, F:FW], tile[:, F:FW], fv, ALU.mult))
                assert c.n == N2

                def scale(n):
                    b, m = GR[n]
                    gv = gat[u][:, b:b + m, 0:F].rearrange("p b (h d) -> p b h d", h=H)
                    v.tensor_tensor(gv, gv, ex[:, :, b:b + m].rearrange("p h (b o) -> p b h o", o=1)
                                    .to_broadcast([P, m, H, HD]), ALU.mult).then_inc(scaled, 1)

                scale(0)
                for n, (b, m) in enumerate(GR):
                    if n + 1 < NGR:
                        scale(n + 1)
                    for j in range(b, b + m):
                        at = bass.ds(k * CH + j, 1) if not isinstance(k, int) else slice(k * CH + j, k * CH + j + 1)
                        t = dve.value_load(C.tpi[0:1, at], min_val=0, max_val=NT)
                        dve.wait_ge(mm_done, CH * (k + 2) + j + 1)
                        if j:
                            dve.wait_ge(acc_done, CH * k + j + 2)
                        tile = C.acc[:, bass.ds(t, 1), :].rearrange("p o f -> p (o f)")
                        v.tensor_tensor(tile, tile, pacc[:, j % 2, 0:GW], ALU.add).then_inc(acc_done, 1)

            ahead(0, 0)
            with dve.Fori(0, NCH // 2 - 1) as i:
                for u in range(2):
                    chunk(2 * i + u, u, True)
            chunk(NCH - 2, 0, True)
            chunk(NCH - 1, 1, False)

        @block.tensor
        def _(pe):
            t_ = nc.tensor
            pe.sem_inc(er_ready, 1)
            pe.sem_inc(mm_done, 2 * CH)

            def ahead(k, u):
                pe.wait_ge(hot_ready, k + 1)
                pe.wait_ge(ers_ready, k + 1)

                def turn(n):
                    b, m = GR[n]
                    if n >= 2:
                        pe.wait_ge(copied, NGR * k + n - 1)
                    for j in range(m):
                        last = t_.transpose(pt[:, n % 2, j * P:(j + 1) * P], hot[u][:, b + j, :], C.ident[:, :])
                    last.then_inc(turned, 1)

                def ers(n):
                    b, m = GR[n]
                    pe.wait_ge(copied, NGR * k + n + 1)
                    for j in range(b, b + m):
                        at = bass.ds(k * CH + j, 1) if not isinstance(k, int) else slice(k * CH + j, k * CH + j + 1)
                        t = pe.value_load(C.tpi[0:1, at], min_val=0, max_val=NT)
                        last = t_.matmul(per[:, j // 16, (j % 16) * R * H:(j % 16 + 1) * R * H], hott[:, j, :],
                                         C.er[:, bass.ds(t, 1), :].rearrange("p o r -> p (o r)"),
                                         start=True, stop=True)
                    return last

                turn(0)
                for n in range(NGR):
                    if n + 1 < NGR:
                        turn(n + 1)
                    last = ers(n)
                last.then_inc(er_ready, 1)

            def chunk(k, u, more):
                pe.wait_ge(s_ready, k + 1)
                t_.transpose(psd[0:ROWS, 0:P], sc[:, :, :].rearrange("p h b -> p (h b)"), C.ident[:, :])
                t_.transpose(psd[0:ROWS, P:2 * P], d4[:, :, :].rearrange("p h b -> p (h b)"),
                             C.ident[:, :]).then_inc(sd_turned, 1)
                pe.wait_ge(fb_ready, k + 1)
                for j, a in enumerate((fwd[:, P - 1:P], bwd[:, 0:1], sd[:, 1, 0:1], sd[:, 1, P - 1:P])):
                    last = t_.matmul(prow[0:1, j * ROWS:(j + 1) * ROWS], a, C.ident[0:ROWS, 0:ROWS],
                                     start=True, stop=True)
                last.then_inc(rows_ready, 1)
                pe.wait_ge(carries_ready, k + 1)
                for j in range(2):
                    last = t_.matmul(psd[0:ROWS, 384 + j:385 + j], carry[:, j, :], C.ones[0:1, 0:1],
                                     start=True, stop=True)
                last.then_inc(cols_ready, 1)
                pe.wait_ge(facm_ready, k + 1)
                t_.matmul(prow[:, 400:400 + H], hot0[:, 0, :], fac[:, 1, :], start=True, stop=False)
                t_.matmul(prow[:, 400:400 + H], hot0[:, 1, :], fac[:, 3, :], start=False,
                          stop=True).then_inc(sc_ready, 1)
                pe.wait_ge(m_ready, k + 1)
                t_.transpose(psd[:, 256:256 + ROWS], mx[:, :], C.ident[0:ROWS, 0:ROWS]).then_inc(mt_ready, 1)
                if more:
                    ahead(k + 1, 1 - u)
                for n, (b, m) in enumerate(GR):
                    pe.wait_ge(scaled, NGR * k + n + 1)
                    for j in range(b, b + m):
                        pe.wait_ge(acc_done, CH * k + j + 1)
                        t_.matmul(pacc[:, j % 2, 0:GW], hot[u][:, j, :], gat[u][:, j, 0:GW],
                                  start=True, stop=True).then_inc(mm_done, 1)

            ahead(0, 0)
            with pe.Fori(0, NCH // 2 - 1) as i:
                for u in range(2):
                    chunk(2 * i + u, u, True)
            chunk(NCH - 2, 0, True)
            chunk(NCH - 1, 1, False)

    for slot in C.slots:
        slot.base += 16 * (NCH // 2)


def across(row, n):
    return row.rearrange("p (o m) -> p o m", o=1).to_broadcast([row.shape[0], n, row.shape[1]])


def layernorm(nc, c, act_sqrt, x, sq, mean, var):
    v = nc.vector
    nt = x.shape[1]
    c.link(v.tensor_reduce(mean, x, AX.X, ALU.add))
    c.link(v.tensor_scalar(mean, mean, 1.0 / F, None, ALU.mult))
    c.link(v.tensor_tensor(x, x, col(mean, F), ALU.subtract))
    c.link(v.tensor_tensor(sq, x, x, ALU.mult))
    c.link(v.tensor_reduce(var, sq, AX.X, ALU.add))
    c.link(v.tensor_scalar(var, var, 1.0 / F, 1e-5, ALU.mult, ALU.add))
    c.link(v.reciprocal(var, var))
    act_sqrt()
    c.link(v.tensor_tensor(x, x, col(var, F), ALU.mult))


def norm_phase(nc, C, D):
    ctx, sems = ExitStack(), []
    with ctx:
        def sb(name, shape, dt=F32):
            return ctx.enter_context(nc.sbuf_tensor(name, shape, dt))

        def sem(name):
            sems.append(nc.alloc_semaphore(name))
            return sems[-1]

        bias = sb("hbias", [P, F])
        rden = sb("rden", [P, NT, H])
        mean = sb("mean0", [P, NT])
        var = sb("var0", [P, NT])
        bias_loaded = sem("hbias_loaded")
        dch = sem("dve_norm0")
        var_ready = sem("var_ready0")
        std_ready = sem("std_ready0")
        deg_ready = sem("deg_ready0")
        hs_ready = sem("hs_ready")
        hs_stored = sem("hs_stored")
        ctx.callback(clear, nc, sems)
        block = ctx.enter_context(nc.Block())

        @block.sync
        def _(sp):
            sp.dma_start(bias[:, :], D.hbias.rearrange("(o f) -> o f", o=1).to_broadcast([P, F])
                         ).then_inc(bias_loaded, 16)
            sp.wait_ge(hs_ready, 1)
            sp.dma_start(D.hs.rearrange("(t p) f -> p t f", p=P), C.acc[:, 0:NT, 0:F]).then_inc(hs_stored, 16)
            sp.wait_ge(hs_stored, 16)

        @block.scalar
        def _(act):
            act.wait_ge(deg_ready, 1)
            nc.scalar.activation(C.rdego[:, :], C.rdego[:, :], ACT.Sqrt)
            nc.scalar.activation(C.rdegi[:, :], C.rdegi[:, :], ACT.Sqrt).then_inc(std_ready, 1)
            act.wait_ge(var_ready, 1)
            nc.scalar.activation(var[:, :], var[:, :], ACT.Sqrt).then_inc(std_ready, 1)

        @block.vector
        def _(dve):
            v = nc.vector
            c = Chain(dve, dch)
            c.link(v.tensor_scalar(C.rdego[:, :], C.dego[:, :], 1.0, None, ALU.max))
            c.link(v.reciprocal(C.rdego[:, :], C.rdego[:, :]))
            c.link(v.tensor_scalar(C.rdegi[:, :].rearrange("p (t o) -> p t o", o=1), C.acc[:, 0:NT, FW:GW],
                                   1.0, None, ALU.max))
            v.reciprocal(C.rdegi[:, :], C.rdegi[:, :]).then_inc(deg_ready, 1)
            c.link(v.tensor_scalar(rden[:, :, :], C.acc[:, 0:NT, F:FW], 1e-30, None, ALU.max))
            c.link(v.reciprocal(rden[:, :, :], rden[:, :, :]))
            hv = C.acc[:, 0:NT, 0:F].rearrange("p t (h d) -> p t h d", h=H)
            c.link(v.tensor_tensor(hv, hv, rden[:, :, :].rearrange("p t (h o) -> p t h o", o=1)
                                   .to_broadcast([P, NT, H, HD]), ALU.mult))
            c.link(v.tensor_tensor(C.x[:, :, :], C.x[:, :, :], C.acc[:, 0:NT, 0:F], ALU.add))
            dve.wait_ge(bias_loaded, 16)
            c.link(v.tensor_tensor(C.x[:, :, :], C.x[:, :, :], across(bias[:, :], NT), ALU.add))

            def root():
                v.tensor_copy(mean[:, :], var[:, :]).then_inc(var_ready, 1)
                dve.wait_ge(std_ready, 2)

            layernorm(nc, c, root, C.x[:, :, :], C.acc[:, 0:NT, 0:F], mean[:, :], var[:, :])
            v.tensor_tensor(C.acc[:, 0:NT, 0:F], C.x[:, :, :], col(C.rdego[:, :], F), ALU.mult
                            ).then_inc(hs_ready, 1)
            dve.wait_ge(hs_stored, 16)
            v.memset(C.acc[:, :, :], 0.0)


def conv_phase(nc, C, D):
    ctx, sems = ExitStack(), []
    with ctx:
        def sb(name, shape, dt=F32):
            return ctx.enter_context(nc.sbuf_tensor(name, shape, dt))

        def sem(name):
            sems.append(nc.alloc_semaphore(name))
            return sems[-1]

        gat = [sb(f"gatb{u}", [P, CH, F]) for u in range(2)]
        hot = [sb(f"hotb{u}", [P, CH, P]) for u in range(2)]
        gidx = [sb(f"gidxb{u}", [P, CH], I32) for u in range(2)]
        pacc = ctx.enter_context(nc.psum_tensor("paccb", [P, 4, 512], F32))
        gathered = [C.slots[u * CH:(u + 1) * CH] for u in range(2)]
        idx_ready = sem("idx_readyb")
        hot_ready = sem("hot_readyb")
        mm_done = sem("mm_doneb")
        acc_done = sem("acc_doneb")
        ctx.callback(clear, nc, sems)
        block = ctx.enter_context(nc.Block())

        @block.gpsimd
        def _(g):
            with g.Fori(0, NCH // 2) as i:
                for u in range(2):
                    k = 2 * i + u
                    g.wait_ge(mm_done, CH * k + CH)
                    g.tensor_copy(gidx[u][:, :], C.srci[:, bass.ds(k * CH, CH)]).then_inc(idx_ready, 1)
                    g.wait_ge(idx_ready, k + 1)
                    g.nop(nofuse=True)
                    for b in range(CH):
                        g.indirect_dma_start(gat[u][:, b, :], None, D.hs,
                                             bass.IndirectOffsetOnAxis(ap=gidx[u][:, b:b + 1], axis=0)
                                             ).then_inc(gathered[u][b].sem, 16)

        @block.vector
        def _(dve):
            v = nc.vector
            dve.sem_inc(acc_done, 4)
            with dve.Fori(0, NCH // 2) as i:
                for u in range(2):
                    k = 2 * i + u
                    v.tensor_tensor(hot[u][:, :, :], col(C.locf[:, bass.ds(k * CH, CH)], P),
                                    across(C.iota[:, :], CH), ALU.is_equal).then_inc(hot_ready, 1)
                    for j in range(CH):
                        t = dve.value_load(C.tpi[0:1, bass.ds(k * CH + j, 1)], min_val=0, max_val=NT)
                        dve.wait_ge(mm_done, CH * (k + 2) + j + 1)
                        if j:
                            dve.wait_ge(acc_done, CH * k + j + 4)
                        tile = C.acc[:, bass.ds(t, 1), 0:F].rearrange("p o f -> p (o f)")
                        v.tensor_tensor(tile, tile, pacc[:, (CH * u + j) % 4, 0:F], ALU.add
                                        ).then_inc(acc_done, 1)

        @block.tensor
        def _(pe):
            pe.sem_inc(mm_done, 2 * CH)
            with pe.Fori(0, NCH // 2) as i:
                for u in range(2):
                    k = 2 * i + u
                    pe.wait_ge(hot_ready, k + 1)
                    for j in range(CH):
                        pe.wait_ge(gathered[u][j].sem, gathered[u][j].base + 16 * i + 16)
                        pe.wait_ge(acc_done, CH * k + j + 1)
                        nc.tensor.matmul(pacc[:, (CH * u + j) % 4, 0:F], hot[u][:, j, :], gat[u][:, j, :],
                                         start=True, stop=True).then_inc(mm_done, 1)

    for slot in C.slots:
        slot.base += 16 * (NCH // 2)


def gate_phase(nc, C, D):
    ctx, sems = ExitStack(), []
    with ctx:
        def sb(name, shape, dt=F32):
            return ctx.enter_context(nc.sbuf_tensor(name, shape, dt))

        def sem(name):
            sems.append(nc.alloc_semaphore(name))
            return sems[-1]

        w = sb("w_gcres", [P, 4, F])
        wgate = sb("wgate", [P, 2, NE])
        brow = sb("brow", [1, 2, F])
        bgrow = sb("bgrow", [1, NE])
        stage = [sb(f"stage{u}", [P, 2 * F]) for u in range(2)]
        xt = [sb(f"xmt{u}", [P, 4, P]) for u in range(2)]
        x2t = [sb(f"x2t{u}", [P, 2, P]) for u in range(2)]
        logit = sb("logit", [P, NT, NE])
        top = sb("top", [P, NT, 8])
        topi = sb("topi", [P, NT, 8], U32)
        topf = sb("topf", [P, NT, 2])
        m = [sb(f"mask{k}", [P, NT, NE]) for k in range(2)]
        mb = sb("mask_b", [P, NT, NE], BF16)
        tri = sb("tri", [P, P], BF16)
        onesb = sb("ones_b", [P, P], BF16)
        valid = sb("valid", [P, NT])
        ct = sb("ct", [P, NE, NT])
        inc = sb("inc", [P, NE, NT])
        again = sb("again", [P, NE, NT])
        rank = sb("rank", [P, NT, NE])
        tmp = sb("ranktmp", [P, NT, NE])
        tot = sb("tot", [P, NE])
        toti = sb("toti", [P, NE], I32)
        tiles = sb("tiles", [P, NE])
        onese = sb("ones_e", [P, NE])
        tend = sb("tend", [P, NE])
        toff = sb("toff", [P, NE])
        rk = sb("rk", [P, 2, NT])
        sl = sb("sl", [P, 2, NT])
        ok = sb("ok", [P, 2, NT])
        e1 = sb("e1", [P, NT])
        scat = sb("scat", [P, 2, NT], I32)
        scatf = sb("scatf", [P, 2, NT])
        ecmp = sb("ecmp", [P, NE])
        ecol = sb("ecol", [P, 1])
        bt = sb("b1_rows", [NE, HID])
        px = ctx.enter_context(nc.psum_tensor("pxg", [P, 512], F32))
        pm = ctx.enter_context(nc.psum_tensor("pmg", [P, 512], F32))
        pz = ctx.enter_context(nc.psum_tensor("pzg", [P, 512], F32))
        pl = ctx.enter_context(nc.psum_tensor("plg", [P, 512], F32))
        pr = ctx.enter_context(nc.psum_tensor("prg", [P, 4, 512], F32))

        w_loaded = sem("w_gcres_loaded")
        b_loaded = sem("bias_loaded1")
        consts = sem("gate_consts")
        dch = sem("dve_gate")
        lch = sem("dve_gate_loop")
        staged = sem("staged")
        turned = sem("turned_g")
        xt_ready = sem("xt_ready_g")
        x2_ready = sem("x2_ready")
        x2_copied = sem("x2_copied")
        x2_turned = sem("x2_turned")
        x2t_ready = sem("x2t_ready")
        l_ready = sem("l_ready")
        l_copied = sem("l_copied")
        masks_ready = sem("masks_ready")
        counts_ready = sem("counts_ready")
        counts_read = sem("counts_read")
        ranks_ready = sem("ranks_ready")
        diff_ready = sem("diff_ready")
        e_ready = sem("e_ready")
        slots_ready = sem("slots_ready")
        ecol_ready = sem("ecol_ready")
        erow_ready = sem("erow_ready")
        b1t_ready = sem("b1t_ready")
        b1t_copied = sem("b1t_copied")
        NS = 30
        scattered = C.slots[0:NS]
        ctx.callback(clear, nc, sems)
        block = ctx.enter_context(nc.Block())

        @block.sync
        def _(sp):
            sp.dma_start(w[:, 0:2, :], D.wgc.rearrange("(c p) n -> p c n", p=P)).then_inc(w_loaded, 16)
            sp.dma_start(w[:, 2:4, :], D.wres.rearrange("(c p) n -> p c n", p=P)).then_inc(w_loaded, 16)
            sp.dma_start(wgate[:, :, :], D.wg.rearrange("(c p) n -> p c n", p=P)).then_inc(w_loaded, 16)
            sp.dma_start(bt[:, :], D.b1).then_inc(b_loaded, 16)
            sp.dma_start(C.b2[:, :], D.b2).then_inc(b_loaded, 16)
            sp.dma_start(brow[:, 0, :], D.bgc.rearrange("(o f) -> o f", o=1)).then_inc(b_loaded, 16)
            sp.dma_start(brow[:, 1, :], D.bres.rearrange("(o f) -> o f", o=1)).then_inc(b_loaded, 16)
            sp.dma_start(bgrow[:, :], D.bg.rearrange("(o f) -> o f", o=1)).then_inc(b_loaded, 16)
            sp.wait_ge(w_loaded, 48)
            sp.wait_ge(b_loaded, 80)

        @block.gpsimd
        def _(g):
            g.memset(tri[:, :], 1.0).then_inc(consts, 1)
            g.wait_ge(consts, 1)
            g.affine_select(out=tri[:, :], in_=tri[:, :], compare_op=ALU.is_gt, fill=0.0, base=0,
                            pattern=[[1, P]], channel_multiplier=-1).then_inc(consts, 1)
            g.wait_ge(slots_ready, 1)
            for k in range(2):
                for t in range(NT):
                    n = k * NT + t
                    if n >= NS:
                        g.wait_ge(scattered[n % NS].sem, scattered[n % NS].base + 16 * (n // NS))
                    g.indirect_dma_start(D.buf, bass.IndirectOffsetOnAxis(ap=scat[:, k, t:t + 1], axis=0),
                                         C.x2[:, t, :], None, bounds_check=NX * P - 1, oob_is_err=False
                                         ).then_inc(scattered[n % NS].sem, 16)
            for slot in scattered:
                g.wait_ge(slot.sem, slot.base + 16 * (2 * NT // NS))

        @block.scalar
        def _(act):
            a = nc.scalar
            act.sem_inc(x2t_ready, 2)
            with act.Fori(0, NT // 2) as i:
                for u in range(2):
                    t = 2 * i + u
                    act.wait_ge(turned, t + 1)
                    act.wait_ge(x2_ready, t + 1)
                    a.activation(xt[u][:, :, :], px[:, :].rearrange("p (c n) -> p c n", n=P), ACT.Copy
                                 ).then_inc(xt_ready, 1)
                    act.wait_ge(x2_ready, t + 3)
                    a.activation(C.x2[:, bass.ds(t, 1), :].rearrange("p o f -> p (o f)"), pm[:, 0:F], ACT.Copy)
                    a.activation(stage[u][:, 0:F], pm[:, 0:F], ACT.Copy).then_inc(x2_copied, 1)
                    act.wait_ge(x2_turned, t + 1)
                    a.activation(x2t[u][:, :, :], pz[:, 0:F].rearrange("p (c n) -> p c n", n=P), ACT.Copy
                                 ).then_inc(x2t_ready, 1)
                    act.wait_ge(l_ready, t + 1)
                    a.activation(logit[:, bass.ds(t, 1), :].rearrange("p o f -> p (o f)"), pl[:, 0:NE],
                                 ACT.Copy).then_inc(l_copied, 1)
            act.wait_ge(b1t_ready, 1)
            for j in range(4):
                last = a.activation(C.b1t[:, :, j], pl[:, j * NE:(j + 1) * NE], ACT.Copy)
            last.then_inc(b1t_copied, 1)
            act.wait_ge(diff_ready, 1)
            a.activation(e1[:, :], e1[:, :], ACT.Exp).then_inc(e_ready, 1)

        @block.vector
        def _(dve):
            v = nc.vector
            c = Chain(dve, dch)
            dve.wait_ge(b_loaded, 80)
            c.link(v.tensor_tensor(brow[:, 0, :], brow[:, 0, :], brow[:, 1, :], ALU.add))
            c.link(v.memset(onesb[:, :], 1.0))
            c.link(v.memset(onese[:, :], 1.0))
            c.link(v.memset(valid[:, :], 1.0))
            c.link(v.tensor_scalar(valid[:, NT - 1:NT], C.ioch[:, :], float(LAST), None, ALU.is_lt))
            c.link(v.memset(again[:, :, :], 1.0))
            c.link(v.memset(again[:, :, 0:1], 0.0))
            with dve.Fori(0, NT // 2) as i:
                for u in range(2):
                    t = 2 * i + u
                    dve.wait_ge(x2t_ready, t + 1)
                    v.tensor_tensor(stage[u][:, 0:F], C.acc[:, bass.ds(t, 1), 0:F].rearrange("p o f -> p (o f)"),
                                    C.rdegi[:, bass.ds(t, 1)].to_broadcast([P, F]), ALU.mult)
                    v.tensor_copy(stage[u][:, F:2 * F], C.x[:, bass.ds(t, 1), :].rearrange("p o f -> p (o f)")
                                  ).then_inc(staged, 1)
            dve.wait_ge(l_copied, NT)
            for t in range(NT):
                c.link(v.max(top[:, t, :], logit[:, t, :]))
                v.max_index(topi[:, t, :], top[:, t, :], logit[:, t, :]).then_inc(lch, 1)
            dve.wait_ge(lch, NT)
            v.tensor_tensor(e1[:, :], top[:, :, 1], top[:, :, 0], ALU.subtract).then_inc(diff_ready, 1)
            c.link(v.tensor_copy(topf[:, :, :], topi[:, :, 0:2]))
            for k in range(2):
                c.link(v.tensor_tensor(m[k][:, :, :], topf[:, :, k:k + 1].to_broadcast([P, NT, NE]),
                                       across(C.iota[:, 0:NE], NT), ALU.is_equal))
                c.link(v.tensor_tensor(m[k][:, :, :], m[k][:, :, :], col(valid[:, :], NE), ALU.mult))
            v.tensor_tensor(mb[:, :, :], m[0][:, :, :], m[1][:, :, :], ALU.add).then_inc(masks_ready, 1)
            dve.wait_ge(counts_ready, 1)
            for q in range(4):
                n = min(8, NT - 8 * q)
                c.link(v.tensor_copy(ct[:, :, 8 * q:8 * q + n].rearrange("p e t -> p t e"),
                                     pr[:, q, 0:n * NE].rearrange("p (t e) -> p t e", e=NE)))
            v.tensor_copy(rk[:, 0, 0:1], ct[:, 0, 0:1]).then_inc(counts_read, 1)
            c.link(v.tensor_tensor_scan(inc[:, :, :].rearrange("p e t -> p (e t)"),
                                        again[:, :, :].rearrange("p e t -> p (e t)"),
                                        ct[:, :, :].rearrange("p e t -> p (e t)"), 0.0, ALU.mult, ALU.add))
            c.link(v.tensor_copy(tot[:, :], inc[:, :, NT - 1]))
            c.link(v.tensor_scalar(tiles[:, :], tot[:, :], float(CAP), float(P - 1), ALU.min, ALU.add))
            c.link(v.tensor_copy(toti[:, :], tiles[:, :]))
            c.link(v.tensor_scalar(toti[:, :], toti[:, :], 7, None, ALU.arith_shift_right))
            c.link(v.tensor_copy(tiles[:, :], toti[:, :]))
            c.link(v.tensor_tensor_scan(tend[:, :], onese[:, :], tiles[:, :], 0.0, ALU.mult, ALU.add))
            c.link(v.tensor_tensor(toff[:, :], tend[:, :], tiles[:, :], ALU.subtract))
            c.link(v.tensor_scalar(toff[:, :], toff[:, :], float(P), None, ALU.mult))
            c.link(v.tensor_scalar(ecmp[:, :], tend[:, :], C.ioch[:, 0:1], None, ALU.is_le))
            c.link(v.tensor_reduce(ecol[:, :], ecmp[:, :], AX.X, ALU.add))
            v.tensor_scalar(ecol[:, :], ecol[:, :], float(NE - 1), None, ALU.min).then_inc(ecol_ready, 1)
            c.link(v.tensor_tensor(inc[:, :, :], inc[:, :, :], ct[:, :, :], ALU.subtract))
            dve.wait_ge(ranks_ready, 1)
            for q in range(4):
                n = min(8, NT - 8 * q)
                c.link(v.tensor_tensor(rank[:, 8 * q:8 * q + n, :], pr[:, q, 0:n * NE].rearrange("p (t e) -> p t e", e=NE),
                                       inc[:, :, 8 * q:8 * q + n].rearrange("p e t -> p t e"), ALU.add))
            for k in range(2):
                c.link(v.tensor_tensor(tmp[:, :, :], rank[:, :, :], m[k][:, :, :], ALU.mult))
                c.link(v.tensor_reduce(rk[:, k, :], tmp[:, :, :], AX.X, ALU.add))
                c.link(v.tensor_tensor(tmp[:, :, :], across(toff[:, :], NT), m[k][:, :, :], ALU.mult))
                c.link(v.tensor_reduce(sl[:, k, :], tmp[:, :, :], AX.X, ALU.add))
            c.link(v.tensor_tensor(sl[:, :, :], sl[:, :, :], rk[:, :, :], ALU.add))
            c.link(v.tensor_scalar(ok[:, :, :], rk[:, :, :], float(CAP), None, ALU.is_lt))
            c.link(v.tensor_tensor(ok[:, :, :], ok[:, :, :], across(valid[:, :], 2), ALU.mult))
            c.link(v.tensor_tensor(sl[:, :, :], sl[:, :, :], ok[:, :, :], ALU.mult))
            c.link(v.tensor_scalar(scatf[:, :, :], ok[:, :, :], -float(NX * P), float(NX * P), ALU.mult, ALU.add))
            c.link(v.tensor_tensor(scatf[:, :, :], scatf[:, :, :], sl[:, :, :], ALU.add))
            c.link(v.tensor_copy(C.slot[:, :, :], sl[:, :, :]))
            v.tensor_copy(scat[:, :, :], scatf[:, :, :]).then_inc(slots_ready, 1)
            dve.wait_ge(e_ready, 1)
            c.link(v.tensor_scalar(C.gate[:, 0, :], e1[:, :], 1.0, None, ALU.add))
            c.link(v.reciprocal(C.gate[:, 0, :], C.gate[:, 0, :]))
            c.link(v.tensor_tensor(C.gate[:, 1, :], C.gate[:, 0, :], e1[:, :], ALU.mult))
            c.link(v.tensor_tensor(C.gate[:, :, :], C.gate[:, :, :], ok[:, :, :], ALU.mult))
            c.link(v.tensor_tensor(C.gm[:, :, :], m[0][:, :, :], col(C.gate[:, 0, :], NE), ALU.mult))
            c.link(v.tensor_tensor(tmp[:, :, :], m[1][:, :, :], col(C.gate[:, 1, :], NE), ALU.mult))
            c.link(v.tensor_tensor(C.gm[:, :, :], C.gm[:, :, :], tmp[:, :, :], ALU.add))
            c.link(v.tensor_copy(C.valid[:, :], valid[:, :]))
            dve.wait_ge(erow_ready, 1)
            v.tensor_copy(C.expert[:, :], pz[0:1, 0:P]).then_inc(lch, 1)

        @block.tensor
        def _(pe):
            t_ = nc.tensor
            pe.wait_ge(w_loaded, 48)
            pe.wait_ge(b_loaded, 80)
            pe.sem_inc(x2_ready, 2)
            with pe.Fori(0, NT // 2) as i:
                for u in range(2):
                    t = 2 * i + u
                    pe.wait_ge(staged, t + 1)
                    for c in range(4):
                        last = t_.transpose(px[:, c * P:(c + 1) * P], stage[u][:, c * P:(c + 1) * P], C.ident[:, :])
                    last.then_inc(turned, 1)
                    pe.wait_ge(xt_ready, t + 1)
                    for c in range(4):
                        t_.matmul(pm[:, 0:F], xt[u][:, c, :], w[:, c, :], start=(c == 0), stop=False)
                    t_.matmul(pm[:, 0:F], C.ones[0:1, :], brow[:, 0, :], start=False, stop=True
                              ).then_inc(x2_ready, 1)
                    pe.wait_ge(x2_copied, t + 1)
                    for c in range(2):
                        last = t_.transpose(pz[:, c * P:(c + 1) * P], stage[u][:, c * P:(c + 1) * P], C.ident[:, :])
                    last.then_inc(x2_turned, 1)
                    pe.wait_ge(x2t_ready, t + 3)
                    for c in range(2):
                        t_.matmul(pl[:, 0:NE], x2t[u][:, c, :], wgate[:, c, :], start=(c == 0), stop=False)
                    t_.matmul(pl[:, 0:NE], C.ones[0:1, :], bgrow[:, :], start=False, stop=True
                              ).then_inc(l_ready, 1)
                    pe.wait_ge(l_copied, t + 1)
            for j in range(4):
                last = t_.transpose(pl[:, j * NE:(j + 1) * NE], bt[:, j * P:(j + 1) * P], C.ident[0:NE, 0:NE])
            last.then_inc(b1t_ready, 1)
            pe.wait_ge(masks_ready, 1)
            pe.wait_ge(consts, 2)
            for turn, (lhs, done) in enumerate(((onesb, counts_ready), (tri, ranks_ready))):
                if turn:
                    pe.wait_ge(counts_read, 1)
                for q in range(4):
                    n = min(8, NT - 8 * q)
                    last = t_.matmul(pr[:, q, 0:n * NE], lhs[:, :],
                                     mb[:, 8 * q:8 * q + n, :].rearrange("p t e -> p (t e)"), start=True, stop=True)
                last.then_inc(done, 1)
            pe.wait_ge(ecol_ready, 1)
            t_.matmul(pz[0:1, 0:P], ecol[:, :], C.ident[:, :], start=True, stop=True).then_inc(erow_ready, 1)

    for slot in scattered:
        slot.base += 16 * (2 * NT // NS)


def expert_phase(nc, C, D):
    ctx, sems = ExitStack(), []
    with ctx:
        def sb(name, shape, dt=F32):
            return ctx.enter_context(nc.sbuf_tensor(name, shape, dt))

        def sem(name):
            sems.append(nc.alloc_semaphore(name))
            return sems[-1]

        w1 = [sb(f"w1_{u}", [P, 2, HID]) for u in range(2)]
        w2 = [sb(f"w2_{u}", [P, 4, F]) for u in range(2)]
        xb = [sb(f"xb{u}", [P, F]) for u in range(2)]
        xt = [sb(f"xbt{u}", [P, 2, P]) for u in range(2)]
        h1 = [sb(f"h1_{u}", [P, 4, P]) for u in range(2)]
        yb = [sb(f"yb{u}", [P, F]) for u in range(2)]
        px = ctx.enter_context(nc.psum_tensor("pxe", [P, 2, 512], F32))
        ph = ctx.enter_context(nc.psum_tensor("phe", [P, 2, 512], F32))
        py = ctx.enter_context(nc.psum_tensor("pye", [P, 2, 512], F32))
        w_loaded = [sem(f"w_loaded{u}") for u in range(2)]
        x_loaded = [sem(f"xb_loaded{u}") for u in range(2)]
        y_stored = C.slots[0:2]
        x_turned = sem("xb_turned")
        xt_ready = sem("xbt_ready")
        h_ready = sem("h_ready")
        g_ready = sem("g_ready")
        y_ready = sem("y_ready")
        y_copied = sem("y_copied")
        y_free = sem("y_free")
        ctx.callback(clear, nc, sems)
        block = ctx.enter_context(nc.Block())

        @block.sync
        def _(sp):
            rows = D.buf.rearrange("(t p) f -> t p f", p=P)
            with sp.Fori(0, NX // 2) as i:
                for u in range(2):
                    t = 2 * i + u
                    e = sp.value_load(C.expert[0:1, bass.ds(t, 1)], min_val=0, max_val=NE - 1)
                    sp.wait_ge(y_ready, t + 1)
                    sp.dma_start(xb[u][:, :], rows[bass.ds(t, 1), :, :].rearrange("o p f -> (o p) f")
                                 ).then_inc(x_loaded[u], 16)
                    sp.dma_start(w1[u][:, :, :], D.w1[bass.ds(e, 1), :, :].rearrange("o (p c) h -> (o p) c h", c=2)
                                 ).then_inc(w_loaded[u], 16)
                    sp.dma_start(w2[u][:, :, :], D.w2[bass.ds(e, 1), :, :].rearrange("o (c p) f -> (o p) c f", p=P)
                                 ).then_inc(w_loaded[u], 16)

        @block.gpsimd
        def _(g):
            g.sem_inc(y_free, 2)
            rows = D.y.rearrange("(t p) f -> t p f", p=P)
            with g.Fori(0, NX // 2) as i:
                for u in range(2):
                    t = 2 * i + u
                    g.wait_ge(y_copied, t + 3)
                    g.dma_start(rows[bass.ds(t, 1), :, :].rearrange("o p f -> (o p) f"), yb[u][:, :]
                                ).then_inc(y_stored[u].sem, 16)
                    g.wait_ge(y_stored[u].sem, y_stored[u].base + 16 * i + 16)
                    g.sem_inc(y_free, 1)

        @block.scalar
        def _(act):
            with act.Fori(0, NX // 2) as i:
                for u in range(2):
                    t = 2 * i + u
                    e = act.value_load(C.expert[0:1, bass.ds(t, 1)], min_val=0, max_val=NE - 1)
                    act.wait_ge(y_ready, t + 1)
                    act.wait_ge(h_ready, t + 1)
                    for j in range(4):
                        last = nc.scalar.activation(h1[u][:, j, :], ph[:, u, j * P:(j + 1) * P], ACT.Gelu,
                                                    bias=C.b1t[:, bass.ds(e, 1), j])
                    last.then_inc(g_ready, 1)

        @block.vector
        def _(dve):
            v = nc.vector
            dve.sem_inc(y_copied, 2)
            with dve.Fori(0, NX // 2) as i:
                for u in range(2):
                    t = 2 * i + u
                    dve.wait_ge(x_turned, t + 1)
                    v.tensor_copy(xt[u][:, :, :], px[:, u, 0:F].rearrange("p (c n) -> p c n", n=P)
                                  ).then_inc(xt_ready, 1)
                    dve.wait_ge(y_free, t + 1)
                    dve.wait_ge(y_ready, t + 3)
                    v.tensor_copy(yb[u][:, :], py[:, u, 0:F]).then_inc(y_copied, 1)

        @block.tensor
        def _(pe):
            t_ = nc.tensor
            pe.sem_inc(y_ready, 2)

            with pe.Fori(0, NX // 2) as i:
                for u in range(2):
                    t = 2 * i + u
                    pe.wait_ge(x_loaded[u], 16 * i + 16)
                    for c in range(2):
                        last = t_.transpose(px[:, u, c * P:(c + 1) * P],
                                            xb[u][:, :].rearrange("p (k c) -> p c k", c=2)[:, c, :], C.ident[:, :])
                    last.then_inc(x_turned, 1)
                    pe.wait_ge(w_loaded[u], 32 * i + 32)
                    pe.wait_ge(xt_ready, t + 1)
                    for j in range(4):
                        for c in range(2):
                            last = t_.matmul(ph[:, u, j * P:(j + 1) * P], w1[u][:, c, j * P:(j + 1) * P],
                                             xt[u][:, c, :], start=(c == 0), stop=(c == 1))
                    last.then_inc(h_ready, 1)
                    pe.wait_ge(g_ready, t + 1)
                    pe.wait_ge(y_copied, t + 1)
                    for j in range(4):
                        last = t_.matmul(py[:, u, 0:F], h1[u][:, j, :], w2[u][:, j, :],
                                         start=(j == 0), stop=(j == 3))
                    last.then_inc(y_ready, 1)

    for slot in y_stored:
        slot.base += 16 * (NX // 2)


def output_phase(nc, C, D):
    ctx, sems = ExitStack(), []
    with ctx:
        def sb(name, shape, dt=F32):
            return ctx.enter_context(nc.sbuf_tensor(name, shape, dt))

        def sem(name):
            sems.append(nc.alloc_semaphore(name))
            return sems[-1]

        NY = 4
        y = [[sb(f"y{k}_{u}", [P, F]) for u in range(NY)] for k in range(2)]
        gmt = [sb(f"gmt{u}", [NE, P]) for u in range(2)]
        vm = sb("vm", [P, P])
        mean = sb("bn_mean", [P, F])
        rstd = sb("bn_rstd", [P, F])
        gb = sb("gamma_beta", [P, 2, F])
        lmean = sb("lmean", [P, NT])
        lvar = sb("lvar", [P, NT])
        sq = C.acc[:, 0:NT, 0:F]
        pg = ctx.enter_context(nc.psum_tensor("pgo", [P, 2, 512], F32))
        pb = ctx.enter_context(nc.psum_tensor("pbo", [P, 2, 512], F32))
        ps = ctx.enter_context(nc.psum_tensor("pso", [P, 512], F32))
        gathered = [C.slots[k * NY:(k + 1) * NY] for k in range(2)]
        gb_loaded = sem("gb_loaded")
        turned = sem("gm_turned")
        gmt_ready = sem("gmt_ready")
        b2_ready = sem("b2_ready")
        y_added = sem("y_added")
        dch = sem("dve_out")
        vm_ready = sem("vm_ready")
        y_ready = sem("y_all_ready")
        sums_ready = sem("sums_ready")
        sq_ready = sem("sq_ready")
        var_ready = sem("var_ready1")
        std_ready = sem("std_ready1")
        out_ready = sem("out_ready")
        stored = sem("out_stored")
        ctx.callback(clear, nc, sems)
        block = ctx.enter_context(nc.Block())

        @block.sync
        def _(sp):
            for k, a in enumerate((D.gamma, D.beta)):
                sp.dma_start(gb[:, k, :], a.rearrange("(o f) -> o f", o=1).to_broadcast([P, F])
                             ).then_inc(gb_loaded, 16)
            sp.wait_ge(out_ready, 1)
            sp.dma_start(D.out[0:(NT - 1) * P, :].rearrange("(t p) f -> p t f", p=P), C.x[:, 0:NT - 1, :]
                         ).then_inc(stored, 16)
            sp.dma_start(D.out[(NT - 1) * P:N, :], C.x[0:LAST, NT - 1, :]).then_inc(stored, 16)
            sp.wait_ge(stored, 32)

        @block.gpsimd
        def _(g):
            for t in range(NT):
                if t >= NY:
                    g.wait_ge(y_added, t - NY + 1)
                for k in range(2):
                    g.indirect_dma_start(y[k][t % NY][:, :], None, D.y,
                                         bass.IndirectOffsetOnAxis(ap=C.slot[:, k, t:t + 1], axis=0)
                                         ).then_inc(gathered[k][t % NY].sem, 16)

        @block.scalar
        def _(act):
            for t in range(NT):
                act.wait_ge(turned, t + 1)
                if t >= 2:
                    act.wait_ge(b2_ready, t - 1)
                nc.scalar.activation(gmt[t % 2][:, :], pg[0:NE, t % 2, 0:P], ACT.Copy).then_inc(gmt_ready, 1)
            act.wait_ge(var_ready, 1)
            nc.scalar.activation(rstd[:, :], rstd[:, :], ACT.Sqrt).then_inc(std_ready, 1)
            act.wait_ge(var_ready, 2)
            nc.scalar.activation(lvar[:, :], lvar[:, :], ACT.Sqrt).then_inc(std_ready, 1)

        @block.vector
        def _(dve):
            v = nc.vector
            c = Chain(dve, dch)
            v.tensor_copy(vm[:, :], C.valid[:, NT - 1:NT].to_broadcast([P, P])).then_inc(vm_ready, 1)
            for t in range(NT):
                for k in range(2):
                    dve.wait_ge(gathered[k][t % NY].sem, gathered[k][t % NY].base + 16 * (t // NY) + 16)
                    c.link(v.scalar_tensor_tensor(C.x2[:, t, :], y[k][t % NY][:, :], C.gate[:, k, t:t + 1],
                                                  C.x2[:, t, :], ALU.mult, ALU.add))
                dve.wait_ge(b2_ready, t + 1)
                v.tensor_tensor(C.x2[:, t, :], C.x2[:, t, :], pb[:, t % 2, 0:F], ALU.add).then_inc(y_added, 1)
            dve.wait_ge(sums_ready, 1)
            c.link(v.tensor_scalar(mean[:, :], ps[:, 0:F], 1.0 / N, None, ALU.mult))
            c.link(v.tensor_tensor(C.x2[:, :, :], C.x2[:, :, :], across(mean[:, :], NT), ALU.subtract))
            v.tensor_tensor(sq, C.x2[:, :, :], C.x2[:, :, :], ALU.mult).then_inc(sq_ready, 1)
            dve.wait_ge(sums_ready, 2)
            c.link(v.tensor_scalar(rstd[:, :], ps[:, 0:F], 1.0 / N, 1e-5, ALU.mult, ALU.add))
            c.link(v.reciprocal(rstd[:, :], rstd[:, :]))
            v.tensor_copy(mean[:, :], rstd[:, :]).then_inc(var_ready, 1)
            dve.wait_ge(std_ready, 1)
            dve.wait_ge(gb_loaded, 32)
            c.link(v.tensor_tensor(rstd[:, :], rstd[:, :], gb[:, 0, :], ALU.mult))
            c.link(v.tensor_tensor(C.x2[:, :, :], C.x2[:, :, :], across(rstd[:, :], NT), ALU.mult))
            c.link(v.tensor_tensor(C.x2[:, :, :], C.x2[:, :, :], across(gb[:, 1, :], NT), ALU.add))
            c.link(v.tensor_tensor(C.x[:, :, :], C.x[:, :, :], C.x2[:, :, :], ALU.add))

            def root():
                v.tensor_copy(lmean[:, :], lvar[:, :]).then_inc(var_ready, 1)
                dve.wait_ge(std_ready, 2)

            layernorm(nc, c, root, C.x[:, :, :], sq, lmean[:, :], lvar[:, :])
            v.tensor_copy(lmean[:, :], lvar[:, :]).then_inc(out_ready, 1)

        @block.tensor
        def _(pe):
            t_ = nc.tensor
            for t in range(NT):
                if t >= 2:
                    pe.wait_ge(gmt_ready, t - 1)
                t_.transpose(pg[0:NE, t % 2, 0:P], C.gm[:, t, :], C.ident[:, :]).then_inc(turned, 1)
                pe.wait_ge(gmt_ready, t + 1)
                if t >= 2:
                    pe.wait_ge(y_added, t - 1)
                t_.matmul(pb[:, t % 2, 0:F], gmt[t % 2][:, :], C.b2[:, :], start=True, stop=True
                          ).then_inc(b2_ready, 1)
            pe.wait_ge(vm_ready, 1)
            pe.wait_ge(y_added, NT)
            for n, a in enumerate((C.x2, sq)):
                if n:
                    pe.wait_ge(sq_ready, 1)
                for t in range(NT):
                    last = t_.matmul(ps[:, 0:F], vm[:, :] if t == NT - 1 else C.ones[:, :], a[:, t, :],
                                     start=(t == 0), stop=(t == NT - 1))
                last.then_inc(sums_ready, 1)


class Slot:

    def __init__(self, sem):
        self.sem, self.base = sem, 0


class Bag:
    pass


def gnn_program(nc, x, src, dst, typ, conv, attl, attr, hbias, wgc, bgc, wres, bres, wg, bg, w1, b1, w2,
                b2, gamma, beta, out, dbg):
    D, C = Bag(), Bag()
    D.x, D.src, D.dst, D.typ = x, src, dst, typ
    D.conv, D.attl, D.attr = conv, attl, attr
    D.tab = nc.dram_tensor("feature_table", (NT * P, R * FW), F32, kind="Internal").ap()
    D.buf = nc.dram_tensor("expert_rows", (NX * P, F), F32, kind="Internal").ap()
    D.hbias, D.wgc, D.bgc, D.wres, D.bres, D.wg, D.bg = hbias, wgc, bgc, wres, bres, wg, bg
    D.w1, D.b1, D.w2, D.b2, D.gamma, D.beta, D.out = w1, b1, w2, b2, gamma, beta, out
    D.hs = nc.dram_tensor("scaled_rows", (NT * P, F), F32, kind="Internal").ap()
    D.y = nc.dram_tensor("expert_out", (NX * P, F), F32, kind="Internal").ap()
    D.rec = nc.dram_tensor("edge_records", (NG * P, 4 * P), F32, kind="Internal").ap()
    ctx = ExitStack()
    with ctx:
        def sb(name, shape, dt=F32):
            return ctx.enter_context(nc.sbuf_tensor(name, shape, dt))

        C.ident = sb("ident", [P, P])
        C.anti = sb("anti", [P, P])
        C.iota = sb("iota", [P, P])
        C.iota2 = sb("iota2", [P, P])
        C.ioch = sb("ioch", [P, 1])
        C.ones = sb("ones", [P, P])
        C.x = sb("x_sb", [P, NT, F])
        C.acc = sb("acc", [P, NT + 1, GW])
        C.rdego = sb("rdego", [P, NT])
        C.rdegi = sb("rdegi", [P, NT])
        C.dego = sb("dego", [P, NT])
        C.slots = [Slot(ctx.enter_context(nc.semaphore(f"gather_slot{n}"))) for n in range(2 * CH)]
        C.first_slots = [Slot(ctx.enter_context(nc.semaphore(f"first_slot{n}"))) for n in range(NG)]
        edges = ctx.enter_context(ExitStack())

        def eb(name, shape, dt=F32):
            return edges.enter_context(nc.sbuf_tensor(name, shape, dt))

        C.er = eb("er", [P, NT + 1, R * H])
        C.fidx = eb("fidx", [P, NPAIR], I32)
        C.srci = eb("srci", [P, NPAIR], I32)
        C.dstf = eb("dstf", [P, NPAIR])
        C.typf = eb("typf", [P, NPAIR])
        C.locf = eb("locf", [P, NPAIR])
        C.srcraw = eb("srcraw", [P, NB])
        C.tpi = eb("tpi", [1, NG * P], I32)
        setup_phase(nc, C, D)
        table_phase(nc, C, D)
        attention_phase(nc, C, D)
        norm_phase(nc, C, D)
        conv_phase(nc, C, D)
        edges.close()
        C.x2 = sb("x2", [P, NT, F])
        C.b2 = sb("b2_sb", [NE, F])
        C.b1t = sb("b1t", [P, NE, 4])
        C.gate = sb("gate", [P, 2, NT])
        C.slot = sb("slot", [P, 2, NT], I32)
        C.gm = sb("gate_by_expert", [P, NT, NE])
        C.valid = sb("valid_rows", [P, NT])
        C.expert = sb("expert_of_tile", [1, P], I32)
        gate_phase(nc, C, D)
        expert_phase(nc, C, D)
        output_phase(nc, C, D)


_INS = ["x", "src", "dst", "edge_type_8", "L0_gnn_conv_weights", "L0_gnn_attn_l", "L0_gnn_attn_r",
        "L0_gnn_h_bias", "L1_gnn_W_gc", "L1_gnn_b_gc", "L1_gnn_W_res", "L1_gnn_b_res", "L1_gnn_Wg",
        "L1_gnn_bg", "L1_gnn_w1", "L1_gnn_b1", "L1_gnn_w2", "L1_gnn_b2", "L1_gnn_gamma", "L1_gnn_beta"]
DBG = False


def kernel(**inputs):
    import numpy as _np
    import concourse.bacc as _bacc
    from concourse import mybir as _mybir
    from concourse.bass_utils import run_bass_kernel_spmd as _run

    nc = _bacc.Bacc("TRN2", target_bir_lowering=False, num_devices=1)
    arrays, args = {}, []
    for name in _INS:
        a = _np.ascontiguousarray(inputs[name])
        arrays[f"in_{name}"] = a
        args.append(nc.dram_tensor(f"in_{name}", a.shape, _mybir.dt.from_np(a.dtype), kind="ExternalInput").ap())
    args.append(nc.dram_tensor("out", (N, F), _mybir.dt.float32, kind="ExternalOutput").ap())
    args.append(nc.dram_tensor("dbg", (8, 128, 8192), _mybir.dt.float32, kind="ExternalOutput").ap() if DBG else None)
    gnn_program(nc, *args)
    r = _run(nc, [arrays], core_ids=[0])
    return r.results[0]["out"]
```

```python
from contextlib import ExitStack

import concourse.bass as bass
from concourse import mybir

ALU = mybir.AluOpType
ACT = mybir.ActivationFunctionType
AX = mybir.AxisListType
F32 = mybir.dt.float32
BF16 = mybir.dt.bfloat16
I32 = mybir.dt.int32
U32 = mybir.dt.uint32

P = 128
N = 3750
E = 120000
F = 256
R = 8
H = 4
HD = F // H
NT = -(-N // P)
NB = -(-E // P)
G = 4
CH = 24
MOSTPAIRS = (NB + NT - 1 + NT * (G - 1)) // G * G
NCH = -(-MOSTPAIRS // CH)
NPAIR = NCH * CH
NGR = CH // G
NG = -(-NPAIR // P)
NRG = -(-(NB + 1) // P)
ROWS = CH * H
FULL = E // P
TAIL = E - FULL * P
LAST = N - (NT - 1) * P
FW = F + H
GW = FW + 1
GS = 264
BIG = 1.0e30
APART = 2.0 ** 80
W = CH + 2
PAD_DST = 8191
PAD_SRC = 4095
NE = 64
HID = 512
CAP = 1024
XG = 4
NX = -(-((2 * N + NE * (P - 1)) // P) // XG) * XG


class Chain:

    def __init__(self, eng, sem, base=0):
        self.eng, self.sem, self.base, self.n = eng, sem, base, 0

    def link(self, ins):
        self.n += 1
        ins.then_inc(self.sem, 1)
        self.eng.wait_ge(self.sem, self.base + self.n)


def col(ap, n):
    return ap.rearrange("p (m o) -> p m o", o=1).to_broadcast([ap.shape[0], ap.shape[1], n])


def clear(nc, sems):
    nc.clear_and_free_semaphores(sems)
    nc.all_engine_barrier(sem_only=True)


def setup_phase(nc, C, D):
    ctx, sems = ExitStack(), []
    with ctx:
        def sb(name, shape, dt=F32):
            return ctx.enter_context(nc.sbuf_tensor(name, shape, dt))

        def sem(name):
            sems.append(nc.alloc_semaphore(name))
            return sems[-1]

        raw = sb("raw", [P, 3, NRG, P], I32)
        rec = sb("rec", [P, NRG, 4, P])
        rawsrc = sb("rawsrc", [P, NRG, P])
        pairrec = sb("pairrec", [P, NG, 4, P])
        loc = sb("loc", [P, NG, P])
        junk = sb("junk", [P, NRG * P])
        below = sb("below", [P, NT + 1])
        starts = sb("starts", [P, NT + 1])
        istart = sb("istart", [P, NT + 1], I32)
        firstb = sb("firstb", [P, NT + 1])
        endb = sb("endb", [P, NT])
        some = sb("some", [P, NT])
        count = sb("count", [P, NT])
        offend = sb("offend", [P, NT])
        shift = sb("shift", [P, NT + 1])
        step = sb("step", [P, NT])
        ones_t = sb("ones_t", [P, NT])
        pid = sb("pid", [P, NG])
        ge = sb("ge", [P, NG, NT])
        gest = sb("gest", [P, NG, NT])
        tp = sb("tp", [P, NG])
        tbase = sb("tbase", [P, NG])
        blk = sb("blk", [P, NG])
        blki = sb("blki", [P, NG], I32)
        ps = ctx.enter_context(nc.psum_tensor("ps_setup", [P, 2, 512], F32))
        pcount = ctx.enter_context(nc.psum_tensor("pcount", [P, 512], F32))
        prow = ctx.enter_context(nc.psum_tensor("prow", [1, 3, 512], F32))

        filled = sem("pads_filled")
        loaded = sem("edges_loaded")
        xloaded = sem("x_loaded")
        wloaded = sem("w_loaded")
        consts = sem("consts_ready")
        dch = sem("dve_setup")
        recs_ready = sem("recs_ready")
        recs_stored = sem("recs_stored")
        below_ready = sem("below_ready")
        starts_ready = sem("starts_ready")
        blk_ready = sem("blk_ready")
        gathered = C.first_slots
        loc_ready = sem("loc_ready")
        turned = sem("turned")
        evacuated = sem("turned_evacuated")
        tp_turned = sem("tp_turned")
        ctx.callback(clear, nc, sems)
        block = ctx.enter_context(nc.Block())

        @block.sync
        def _(sp):
            sp.wait_ge(filled, 4)
            for k, a in enumerate((D.src, D.dst, D.typ)):
                whole = (FULL // P) * P
                sp.dma_start(raw[:, k, 0:FULL // P, :],
                             a[0:whole * P].rearrange("(g p e) -> p g e", p=P, e=P)).then_inc(loaded, 16)
                sp.dma_start(raw[0:FULL - whole, k, FULL // P, :],
                             a[whole * P:FULL * P].rearrange("(p e) -> p e", e=P)).then_inc(loaded, 16)
                sp.dma_start(raw[FULL - whole:FULL - whole + 1, k, FULL // P, 0:TAIL],
                             a[FULL * P:E].rearrange("(p e) -> p e", p=1)).then_inc(loaded, 16)
            sp.dma_start(C.x[:, 0:NT - 1, :],
                         D.x[0:(NT - 1) * P, :].rearrange("(t p) f -> p t f", p=P)).then_inc(xloaded, 16)
            sp.dma_start(C.x[0:LAST, NT - 1, :], D.x[(NT - 1) * P:N, :]).then_inc(xloaded, 16)
            sp.wait_ge(recs_ready, 1)
            sp.dma_start(D.rec.rearrange("(g p) f -> p g f", p=P),
                         rec[:, :, :, :].rearrange("p g k e -> p g (k e)")).then_inc(recs_stored, 16)
            sp.wait_ge(xloaded, 32)

        @block.gpsimd
        def _(g):
            g.memset(raw[:, 0, :, :], PAD_SRC).then_inc(filled, 1)
            g.memset(raw[:, 1, :, :], PAD_DST).then_inc(filled, 1)
            g.memset(raw[:, 2, :, :], 0).then_inc(filled, 1)
            g.memset(C.x[:, NT - 1, :], 0.0).then_inc(filled, 1)
            g.iota(C.iota[:, :], [[1, P]], base=0, channel_multiplier=0,
                   allow_small_or_imprecise_dtypes=True).then_inc(consts, 1)
            g.iota(C.ioch[:, :], [[0, 1]], base=0, channel_multiplier=1,
                   allow_small_or_imprecise_dtypes=True).then_inc(consts, 1)
            g.iota(pid[:, :], [[P, NG]], base=0, channel_multiplier=1,
                   allow_small_or_imprecise_dtypes=True).then_inc(consts, 1)
            g.memset(C.ones[:, :], 1.0).then_inc(consts, 1)
            g.wait_ge(recs_stored, 16)
            g.wait_ge(blk_ready, 1)
            for k in range(NG):
                g.indirect_dma_start(pairrec[:, k, :, :].rearrange("p k e -> p (k e)"), None, D.rec,
                                     bass.IndirectOffsetOnAxis(ap=blki[:, k:k + 1], axis=0)
                                     ).then_inc(gathered[k].sem, 16)

        @block.vector
        def _(dve):
            v = nc.vector
            c = Chain(dve, dch)
            dve.wait_ge(consts, 4)
            c.link(v.tensor_scalar(C.ident[:, :], C.iota[:, :], C.ioch[:, 0:1], None, ALU.is_equal))
            c.link(v.tensor_scalar(C.iota2[:, :], C.iota[:, :], -1.0, float(P - 1), ALU.mult, ALU.add))
            c.link(v.tensor_scalar(C.anti[:, :], C.iota2[:, :], C.ioch[:, 0:1], None, ALU.is_equal))
            c.link(v.memset(ones_t[:, :], 1.0))
            dve.wait_ge(loaded, 9 * 16)
            c.link(v.tensor_copy(rawsrc[:, :, :], raw[:, 0, :, :]))
            c.link(v.tensor_scalar(rec[:, :, 1, :], raw[:, 0, :, :], float(N - 1), None, ALU.min))
            c.link(v.tensor_copy(rec[:, :, 2, :], raw[:, 1, :, :]))
            c.link(v.tensor_copy(rec[:, :, 3, :], raw[:, 2, :, :]))
            c.link(v.scalar_tensor_tensor(rec[:, :, 0, :], rec[:, :, 1, :], float(R), rec[:, :, 3, :],
                                          ALU.mult, ALU.add))
            v.tensor_copy(junk[:, 0:1], rec[:, 0, 0, 0:1]).then_inc(recs_ready, 1)
            c.link(v.memset(below[:, 0:1], 0.0))
            dsts = rec[:, :, 2, :]
            jv = junk[:, :].rearrange("p (g e) -> p g e", e=P)
            for t in range(1, NT + 1):
                c.link(v.tensor_scalar(jv, dsts, float(P * t), 0.0, ALU.is_lt, ALU.add,
                                       accum_out=below[:, t:t + 1]))
            v.tensor_copy(junk[:, 0:1], below[:, 0:1]).then_inc(below_ready, 1)
            dve.wait_ge(starts_ready, 1)
            c.link(v.tensor_copy(starts[:, :], pcount[:, 0:NT + 1]))
            c.link(v.tensor_copy(istart[:, :], starts[:, :]))
            c.link(v.tensor_scalar(istart[:, :], istart[:, :], 7, None, ALU.arith_shift_right))
            c.link(v.tensor_copy(firstb[:, :], istart[:, :]))
            c.link(v.tensor_scalar(junk[:, 0:NT], starts[:, 1:NT + 1], float(P - 1), None, ALU.add))
            c.link(v.tensor_copy(istart[:, 0:NT], junk[:, 0:NT]))
            c.link(v.tensor_scalar(istart[:, 0:NT], istart[:, 0:NT], 7, None, ALU.arith_shift_right))
            c.link(v.tensor_copy(endb[:, :], istart[:, 0:NT]))
            c.link(v.tensor_tensor(some[:, :], starts[:, 1:NT + 1], starts[:, 0:NT], ALU.is_gt))
            c.link(v.tensor_tensor(count[:, :], endb[:, :], firstb[:, 0:NT], ALU.subtract))
            c.link(v.tensor_tensor(count[:, :], count[:, :], some[:, :], ALU.mult))
            c.link(v.tensor_scalar(junk[:, 0:NT], count[:, :], float(G - 1), None, ALU.add))
            c.link(v.tensor_copy(istart[:, 0:NT], junk[:, 0:NT]))
            c.link(v.tensor_scalar(istart[:, 0:NT], istart[:, 0:NT], -G, None, ALU.bitwise_and))
            c.link(v.tensor_copy(count[:, :], istart[:, 0:NT]))
            c.link(v.tensor_tensor_scan(offend[:, :], ones_t[:, :], count[:, :], 0.0, ALU.mult, ALU.add))
            c.link(v.tensor_copy(shift[:, 0:1], firstb[:, 0:1]))
            c.link(v.tensor_tensor(shift[:, 1:NT + 1], firstb[:, 1:NT + 1], offend[:, :], ALU.subtract))
            c.link(v.tensor_tensor(step[:, :], shift[:, 1:NT + 1], shift[:, 0:NT], ALU.subtract))
            offb = offend[:, :].rearrange("p (o t) -> p o t", o=1).to_broadcast([P, NG, NT])
            stepb = step[:, :].rearrange("p (o t) -> p o t", o=1).to_broadcast([P, NG, NT])
            c.link(v.tensor_tensor(ge[:, :, :], offb, col(pid[:, :], NT), ALU.is_le))
            c.link(v.tensor_tensor(gest[:, :, :], ge[:, :, :], stepb, ALU.mult))
            c.link(v.tensor_reduce(tp[:, :], ge[:, :, :], AX.X, ALU.add))
            c.link(v.tensor_reduce(blk[:, :], gest[:, :, :], AX.X, ALU.add))
            c.link(v.tensor_tensor(blk[:, :], blk[:, :], pid[:, :], ALU.add))
            c.link(v.tensor_scalar(blk[:, :], blk[:, :], float(NB), 0.0, ALU.min, ALU.max))
            c.link(v.tensor_scalar(tbase[:, :], tp[:, :], float(P), None, ALU.mult))
            v.tensor_copy(blki[:, :], blk[:, :]).then_inc(blk_ready, 1)
            for k in range(NG):
                dve.wait_ge(gathered[k].sem, gathered[k].base + 16)
                v.tensor_scalar(loc[:, k, :], pairrec[:, k, 2, :], tbase[:, k:k + 1], None,
                                ALU.subtract).then_inc(loc_ready, 1)
            dests = [C.fidx, C.srci, C.dstf, C.typf, C.locf, C.srcraw]
            n = 0
            for k in range(NG):
                for j, d in enumerate(dests):
                    w = min(P, (NB if j == 5 else NPAIR) - k * P)
                    if w <= 0:
                        continue
                    dve.wait_ge(turned, n + 1)
                    v.tensor_scalar(d[:, k * P:k * P + w], ps[:, n % 2, 0:w], APART if j == 2 else 1.0, None,
                                    ALU.mult).then_inc(evacuated, 1)
                    n += 1
            dve.wait_ge(tp_turned, 1)
            v.tensor_copy(C.tpi[:, 0:NG * P], prow[0:1, :, :].rearrange("o a b -> o (a b)")[:, 0:NG * P]).then_inc(evacuated, 1)

        @block.tensor
        def _(pe):
            pe.wait_ge(below_ready, 1)
            nc.tensor.matmul(pcount[:, 0:NT + 1], C.ones[:, :], below[:, :], start=True,
                             stop=True).then_inc(starts_ready, 1)
            n = 0
            for k in range(NG):
                pe.wait_ge(loc_ready, k + 1)
                for j, a in enumerate((pairrec[:, k, 0, :], pairrec[:, k, 1, :], pairrec[:, k, 2, :],
                                       pairrec[:, k, 3, :], loc[:, k, :], rawsrc[:, k % NRG, :])):
                    if j == 5 and k >= NRG:
                        continue
                    if n >= 2:
                        pe.wait_ge(evacuated, n - 1)
                    nc.tensor.transpose(ps[:, n % 2, 0:P], a, C.ident[:, :]).then_inc(turned, 1)
                    n += 1
            for k in range(NG):
                last = nc.tensor.matmul(prow[0:1, k // 4, (k % 4) * P:(k % 4 + 1) * P], tp[:, k:k + 1],
                                        C.ident[:, :], start=True, stop=True)
            last.then_inc(tp_turned, 1)

    for slot in gathered:
        slot.base += 16


HB = -(-NB // NT)


def table_phase(nc, C, D):
    ctx, sems = ExitStack(), []
    with ctx:
        def sb(name, shape, dt=F32):
            return ctx.enter_context(nc.sbuf_tensor(name, shape, dt))

        def sem(name):
            sems.append(nc.alloc_semaphore(name))
            return sems[-1]

        w = sb("conv_w", [P, 2, R * F])
        att = sb("att", [P, 2, R * F])
        prod = sb("att_prod", [P, R * F])
        watt = sb("watt", [P, 2, 2, R * H])
        xin = [sb(f"xin{u}", [P, F]) for u in range(2)]
        xt = [sb(f"xt{u}", [P, 2, P]) for u in range(2)]
        row = [sb(f"trow{u}", [P, R, FW]) for u in range(2)]
        low = sb("src_low", [P, NT * HB])
        high = sb("src_high", [P, NT * HB])
        isrc = sb("src_int", [P, NT * HB], I32)
        ihalf = sb("src_half", [P, NT * HB], I32)
        onelow = [sb(f"onelow{u}", [P, HB, P], BF16) for u in range(2)]
        onehigh = [sb(f"onehigh{u}", [P, HB, NT], BF16) for u in range(2)]
        zero = sb("zero_row", [P, F])
        zerob = sb("zero_b", [P, P], BF16)
        pfeat = ctx.enter_context(nc.psum_tensor("pfeat", [P, 4, 512], F32))
        px = ctx.enter_context(nc.psum_tensor("px", [P, 512], F32))
        pel = ctx.enter_context(nc.psum_tensor("pel", [P, 512], F32))
        phist = ctx.enter_context(nc.psum_tensor("phist", [P, 512], F32))

        w_loaded = sem("conv_loaded")
        att_loaded = sem("att_loaded")
        dch = sem("dve_table")
        zeros = sem("zeros_ready")
        buf_zeroed = sem("buf_zeroed")
        prep = sem("prep_done")
        xin_ready = sem("xin_ready")
        x_turned = sem("x_turned")
        xt_ready = sem("xt_ready")
        hot_ready = sem("hot_ready")
        hot_free = sem("hot_free")
        feat_ready = sem("feat_ready")
        feat_free = sem("feat_free")
        el_ready = sem("el_ready")
        row_ready = sem("row_ready")
        row_free = sem("row_free")
        row_stored = [sem(f"row_stored{u}") for u in range(2)]
        hist_ready = sem("hist_ready")
        ctx.callback(clear, nc, sems)
        block = ctx.enter_context(nc.Block())

        @block.sync
        def _(sp):
            for k in range(2):
                sp.dma_start(w[:, k, :].rearrange("p (a d) -> p a d", d=HD),
                             D.conv[:, :, k * P:(k + 1) * P, :].rearrange("r h k d -> k (r h) d")
                             ).then_inc(w_loaded, 16)
            for k, a in enumerate((D.attl, D.attr)):
                flat = a.rearrange("r h d -> (r h d)").rearrange("(o f) -> o f", o=1)
                sp.dma_start(att[:, k, :], flat.to_broadcast([P, R * F])).then_inc(att_loaded, 16)
            with sp.Fori(0, NT // 2) as i:
                for u in range(2):
                    sp.wait_ge(row_ready, 2 * i + u + 2)
                    sp.dma_start(D.tab.rearrange("(t p) f -> t p f", p=P)[bass.ds(2 * i + u, 1), :, :]
                                 .rearrange("o p f -> (o p) f"),
                                 row[u][:, :, :].rearrange("p r f -> p (r f)")).then_inc(row_stored[u], 16)
                    sp.wait_ge(row_stored[u], 16 * i + 16)
                    sp.sem_inc(row_free, 1)

        @block.scalar
        def _(act):
            act.wait_ge(zeros, 1)
            act.dma_start(D.buf.rearrange("(p t) f -> p t f", p=P),
                          zero[:, :].rearrange("p (o f) -> p o f", o=1).to_broadcast([P, NX, F])
                          ).then_inc(buf_zeroed, 16)
            act.sem_inc(row_free, 2)
            act.sem_inc(row_ready, 1)
            act.sem_inc(feat_free, 4)
            with act.Fori(0, NT // 2) as i:
                for u in range(2):
                    act.wait_ge(row_free, 2 * i + u + 1)
                    for q in range(4):
                        act.wait_ge(feat_ready, 4 * (2 * i + u) + q + 1)
                        nc.scalar.activation(row[u][:, 2 * q:2 * q + 2, 0:F],
                                             pfeat[:, q, :].rearrange("p (r f) -> p r f", r=2),
                                             ACT.Copy).then_inc(feat_free, 1)
                    act.wait_ge(el_ready, 2 * i + u + 3)
                    nc.scalar.activation(row[u][:, :, F:FW], pel[:, 0:R * H].rearrange("p (r h) -> p r h", h=H),
                                         ACT.Copy)
                    nc.scalar.activation(C.er[:, bass.ds(2 * i + u, 1), :],
                                         pel[:, R * H:2 * R * H].rearrange("p (o r) -> p o r", o=1),
                                         ACT.Copy).then_inc(row_ready, 1)
            act.wait_ge(hist_ready, 1)
            nc.scalar.activation(C.dego[:, :], phist[:, 0:NT], ACT.Copy)
            act.wait_ge(buf_zeroed, 16)

        @block.vector
        def _(dve):
            v = nc.vector
            c = Chain(dve, dch)
            v.memset(zero[:, :], 0.0).then_inc(zeros, 1)
            v.memset(C.er[:, NT, :], 0.0)
            c.link(v.memset(zerob[:, :], 0.0))
            c.link(v.memset(low[:, :], float(PAD_SRC)))
            c.link(v.tensor_copy(low[:, 0:NB], C.srcraw[:, :]))
            c.link(v.tensor_copy(isrc[:, :], low[:, :]))
            c.link(v.tensor_scalar(ihalf[:, :], isrc[:, :], P - 1, None, ALU.bitwise_and))
            c.link(v.tensor_copy(low[:, :], ihalf[:, :]))
            c.link(v.tensor_scalar(ihalf[:, :], isrc[:, :], 7, None, ALU.arith_shift_right))
            c.link(v.tensor_copy(high[:, :], ihalf[:, :]))
            dve.wait_ge(w_loaded, 32)
            dve.wait_ge(att_loaded, 32)
            for k in range(2):
                for j in range(2):
                    c.link(v.tensor_tensor(prod[:, :], w[:, k, :], att[:, j, :], ALU.mult))
                    c.link(v.tensor_reduce(watt[:, k, j, :], prod[:, :].rearrange("p (a d) -> p a d", d=HD),
                                           AX.X, ALU.add))
            dve.sem_inc(xt_ready, 1)
            dve.sem_inc(prep, 1)
            with dve.Fori(0, NT // 2) as i:
                for u in range(2):
                    v.tensor_copy(xin[u][:, :], C.x[:, bass.ds(2 * i + u, 1), :].rearrange("p o f -> p (o f)")
                                  ).then_inc(xin_ready, 1)
                    dve.wait_ge(hot_free, 2 * i + u + 1)
                    at = bass.ds((2 * i + u) * HB, HB)
                    v.tensor_tensor(onelow[u][:, :, :], col(low[:, at], P),
                                    C.iota[:, :].rearrange("p (o f) -> p o f", o=1).to_broadcast([P, HB, P]),
                                    ALU.is_equal)
                    v.tensor_tensor(onehigh[u][:, :, :], col(high[:, at], NT),
                                    C.iota[:, 0:NT].rearrange("p (o f) -> p o f", o=1).to_broadcast([P, HB, NT]),
                                    ALU.is_equal).then_inc(hot_ready, 1)
                    dve.wait_ge(x_turned, 2 * i + u + 1)
                    dve.wait_ge(el_ready, 2 * i + u + 1)
                    v.tensor_copy(xt[u][:, :, :], px[:, 0:F].rearrange("p (c n) -> p c n", c=2)
                                  ).then_inc(xt_ready, 1)

        @block.tensor
        def _(pe):
            pe.wait_ge(prep, 1)
            pe.sem_inc(hot_free, 2)
            pe.sem_inc(el_ready, 2)
            nc.tensor.matmul(phist[:, 0:NT], zerob[:, :], zerob[:, 0:NT], start=True, stop=False)
            with pe.Fori(0, NT // 2) as i:
                for u in range(2):
                    t = 2 * i + u
                    pe.wait_ge(xin_ready, t + 1)
                    pe.wait_ge(xt_ready, t + 1)
                    for k in range(2):
                        last = nc.tensor.transpose(px[:, k * P:(k + 1) * P], xin[u][:, k * P:(k + 1) * P],
                                                   C.ident[:, :])
                    last.then_inc(x_turned, 1)
                    pe.wait_ge(hot_ready, t + 1)
                    for b in range(HB):
                        last = nc.tensor.matmul(phist[:, 0:NT], onelow[u][:, b, :], onehigh[u][:, b, :],
                                                start=False, stop=False)
                    last.then_inc(hot_free, 1)
                    pe.wait_ge(xt_ready, t + 2)
                    for q in range(4):
                        pe.wait_ge(feat_free, 4 * t + q + 1)
                        for k in range(2):
                            last = nc.tensor.matmul(pfeat[:, q, :], xt[u][:, k, :], w[:, k, q * 512:(q + 1) * 512],
                                                    start=(k == 0), stop=(k == 1))
                        last.then_inc(feat_ready, 1)
                    pe.wait_ge(row_ready, t + 1)
                    for k in range(2):
                        last = nc.tensor.matmul(pel[:, 0:2 * R * H], xt[u][:, k, :],
                                                watt[:, k, :, :].rearrange("p l a -> p (l a)"),
                                                start=(k == 0), stop=(k == 1))
                    last.then_inc(el_ready, 1)
            nc.tensor.matmul(phist[:, 0:NT], zerob[:, :], zerob[:, 0:NT], start=False,
                             stop=True).then_inc(hist_ready, 1)


def attention_phase(nc, C, D):
    ctx, sems = ExitStack(), []
    with ctx:
        def sb(name, shape, dt=F32):
            return ctx.enter_context(nc.sbuf_tensor(name, shape, dt))

        def sem(name):
            sems.append(nc.alloc_semaphore(name))
            return sems[-1]

        gat = [sb(f"gat{u}", [P, CH, GS]) for u in range(2)]
        hot = [sb(f"hot{u}", [P, CH, P]) for u in range(2)]
        hott = sb("hott", [P, CH, P])
        gidx = [sb(f"gidx{u}", [P, CH], I32) for u in range(2)]
        tmask = sb("tmask", [P, CH, R])
        ertmp = sb("ertmp", [P, CH, R, H])
        ersel = [sb(f"ersel{u}", [P, H, CH]) for u in range(2)]
        sc = sb("scores", [P, H, CH])
        d4 = sb("dst4", [P, H, CH])
        sd = sb("sdrows", [ROWS, 2, P])
        neg = sb("neg", [ROWS, P + 1])
        fwd = sb("fwd", [ROWS, P])
        bwd = sb("bwd", [ROWS, P])
        mx = sb("mx", [ROWS, P])
        rows = sb("rows", [1, 4, H, W])
        link = sb("link", [1, 2, H, W])
        af = sb("af", [1, H, W])
        ab = sb("ab", [1, H, W])
        cof = sb("cof", [1, H, W])
        cob = sb("cob", [1, H, W])
        carry = sb("carry", [1, 2, H * CH])
        fac = sb("fac", [1, 4, H])
        hot0 = sb("hotfirst", [1, 2, P])
        ex = sb("ex", [P, H, CH])
        exin = sb("exin", [P, H, CH])
        pt = ctx.enter_context(nc.psum_tensor("pt", [P, 2, 512], F32))
        per = ctx.enter_context(nc.psum_tensor("per", [P, 2, 512], F32))
        psd = ctx.enter_context(nc.psum_tensor("psd", [P, 512], F32))
        prow = ctx.enter_context(nc.psum_tensor("prow2", [P, 512], F32))
        pacc = ctx.enter_context(nc.psum_tensor("pacc", [P, 2, 512], F32))

        gathered1 = [C.slots[u * CH:(u + 1) * CH] for u in range(2)]
        gathered = sem("chunk_gathered")
        idx_ready = sem("idx_ready")
        hot_ready = sem("hot_ready2")
        turned = sem("hot_turned")
        scaled_act = sem("scaled_act")
        copied = sem("hott_copied")
        er_ready = sem("er_ready")
        ers_ready = sem("ers_ready")
        s_ready = sem("s_ready")
        sd_turned = sem("sd_turned")
        sd_copied = sem("sd_copied")
        fb_ready = sem("fb_ready")
        rows_ready = sem("rows_ready")
        rows_copied = sem("rows_copied")
        carries_ready = sem("carries_ready")
        cols_ready = sem("cols_ready")
        fac_ready = sem("fac_ready")
        facm_ready = sem("facm_ready")
        m_ready = sem("m_ready")
        mt_ready = sem("mt_ready")
        exin_ready = sem("exin_ready")
        ex_ready = sem("ex_ready")
        scaled = sem("scaled")
        mm_done = sem("mm_done")
        acc_done = sem("acc_done")
        sc_ready = sem("sc_ready")
        ch0 = sem("dve_attn0")
        ch1 = sem("dve_attn1")
        ch2 = sem("dve_attn2")
        ctx.callback(clear, nc, sems)
        block = ctx.enter_context(nc.Block())

        @block.gpsimd
        def _(g):
            with g.Fori(0, NCH // 2) as i:
                for u in range(2):
                    k = 2 * i + u
                    g.wait_ge(mm_done, NGR * (k + 1))
                    g.tensor_copy(gidx[u][:, :], C.fidx[:, bass.ds(k * CH, CH)]).then_inc(idx_ready, 1)
                    g.wait_ge(idx_ready, k + 1)
                    g.nop(nofuse=True)
                    for b in range(CH):
                        g.indirect_dma_start(gat[u][:, b, 0:FW], None, D.tab.rearrange("n (r f) -> (n r) f", f=FW),
                                             bass.IndirectOffsetOnAxis(ap=gidx[u][:, b:b + 1], axis=0)
                                             ).then_inc(gathered1[u][b].sem, 16)

        @block.sync
        def _(sp):
            with sp.Fori(0, NCH // 2) as i:
                for u in range(2):
                    for b in range(CH):
                        sp.wait_ge(gathered1[u][b].sem, gathered1[u][b].base + 16 * i + 16)
                    sp.sem_inc(gathered, 1)

        @block.scalar
        def _(act):
            a = nc.scalar

            def copy(k, n):
                act.wait_ge(turned, NGR * k + n + 1)
                a.activation(hott[:, G * n:G * n + G, :], pt[:, n % 2, :].rearrange("p (b e) -> p b e", e=P),
                             ACT.Copy).then_inc(copied, 1)

            def scale(u, n):
                for j in range(G * n + G - 1, G * n + G):
                    for h in range(H):
                        row = gat[u][:, j, h * HD:(h + 1) * HD]
                        last = a.activation(row, row, ACT.Copy, scale=ex[:, h, j:j + 1])
                last.then_inc(scaled_act, 1)

            def chunk(k, u, more):
                act.wait_ge(sd_turned, k + 1)
                a.activation(sd[:, :, :], psd[0:ROWS, 0:2 * P].rearrange("p (a e) -> p a e", e=P),
                             ACT.Copy).then_inc(sd_copied, 1)
                act.wait_ge(rows_ready, k + 1)
                a.activation(rows[:, :, :, 1:CH + 1].rearrange("o a h b -> o (a h) b"),
                             prow[0:1, 0:4 * ROWS].rearrange("o (a b) -> o a b", b=CH), ACT.Copy
                             ).then_inc(rows_copied, 1)
                if more:
                    act.wait_ge(er_ready, k + 1)
                    copy(k + 1, 0)
                    copy(k + 1, 1)
                    copy(k + 1, 2)
                act.wait_ge(fac_ready, k + 1)
                a.activation(fac[:, 1, :], fac[:, 0, :], ACT.Exp).then_inc(facm_ready, 1)
                act.wait_ge(exin_ready, k + 1)
                a.activation(ex[:, :, :], exin[:, :, :], ACT.Exp).then_inc(ex_ready, 1)
                a.activation(gat[u][:, :, F:FW].rearrange("p b h -> p h b"), exin[:, :, :], ACT.Exp)
                act.wait_ge(ex_ready, k + 1)
                for n in range(NGR):
                    if more and n < 3:
                        copy(k + 1, n + 3)
                    scale(u, n)

            act.wait_ge(er_ready, 1)
            for n in range(NGR):
                copy(0, n)
            with act.Fori(0, NCH // 2 - 1) as i:
                for u in range(2):
                    chunk(2 * i + u, u, True)
            chunk(NCH - 2, 0, True)
            chunk(NCH - 1, 1, False)

        @block.vector
        def _(dve):
            v = nc.vector
            c0 = Chain(dve, ch0)
            for u in range(2):
                c0.link(v.memset(gat[u][:, :, FW:GW], 1.0))
            c0.link(v.memset(C.acc[:, :, :], 0.0))
            c0.link(v.memset(neg[:, 0:1], 0.0))
            c0.link(v.memset(neg[:, P:P + 1], 0.0))
            c0.link(v.memset(rows[:, :, :, :], -BIG))
            c0.link(v.memset(link[:, :, :, :], -BIG))
            c0.link(v.memset(af[:, :, :], -BIG))
            c0.link(v.memset(ab[:, :, :], -BIG))
            c0.link(v.memset(fac[:, 3, :], 1.0))
            dve.sem_inc(ers_ready, 1)
            dve.sem_inc(acc_done, 2)
            N1, N2 = 3, 15

            def part(tab, k, n0, n):
                if isinstance(k, int):
                    return tab[:, k * CH + n0:k * CH + n0 + n]
                return tab[:, bass.ds(k * CH + n0, n)]

            def one_hot(k, u, n):
                v.tensor_tensor(hot[u][:, G * n:G * n + G, :], col(part(C.locf, k, G * n, G), P),
                                across(C.iota[:, :], G), ALU.is_equal).then_inc(hot_ready, 1)

            def edge_er(k, u):
                c = Chain(dve, ch1, k * N1)
                c.link(v.tensor_tensor(tmask[:, :, :], col(part(C.typf, k, 0, CH), R),
                                       across(C.iota[:, 0:R], CH), ALU.is_equal))
                dve.wait_ge(er_ready, k + 2)
                for n, (b, m) in enumerate(((0, 16), (16, CH - 16))):
                    c.link(v.tensor_tensor(ertmp[:, b:b + m, :, :],
                                           per[:, n, 0:m * R * H].rearrange("p (b r h) -> p b r h", r=R, h=H),
                                           tmask[:, b:b + m, :].rearrange("p b (r o) -> p b r o", o=1)
                                           .to_broadcast([P, m, R, H]), ALU.mult))
                assert c.n == N1
                v.tensor_reduce(ersel[u][:, :, :].rearrange("p h b -> p b h"),
                                ertmp[:, :, :, :].rearrange("p b r h -> p b h r"), AX.X, ALU.add
                                ).then_inc(ers_ready, 1)

            def chunk(k, u, more):
                c = Chain(dve, ch2, k * N2)
                dve.wait_ge(ers_ready, k + 2)
                dve.wait_ge(gathered, k + 1)
                c.link(v.tensor_tensor(sc[:, :, :].rearrange("p h b -> p b h"), gat[u][:, :, F:FW],
                                       ersel[u][:, :, :].rearrange("p h b -> p b h"), ALU.add))
                v.tensor_copy(d4[:, :, :], part(C.dstf, k, 0, CH).rearrange("p (o b) -> p o b", o=1)
                              .to_broadcast([P, H, CH]))
                v.scalar_tensor_tensor(sc[:, :, :], sc[:, :, :], 0.2, sc[:, :, :], ALU.mult, ALU.max
                                       ).then_inc(s_ready, 1)
                c.link(v.tensor_scalar(hot0[:, 0, :], C.iota[0:1, :], part(C.locf[0:1, :], k, 0, 1), None, ALU.is_equal))
                c.link(v.tensor_scalar(hot0[:, 1, :], hot0[:, 0, :], -1.0, 1.0, ALU.mult, ALU.add))
                if more:
                    one_hot(k + 1, 1 - u, 0)
                dve.wait_ge(sd_copied, k + 1)
                c.link(v.tensor_tensor(neg[:, 1:P], sd[:, 1, 0:P - 1], sd[:, 1, 1:P], ALU.subtract))
                v.tensor_tensor_scan(fwd[:, :], neg[:, 0:P], sd[:, 0, :], -BIG, ALU.add, ALU.max)
                v.tensor_tensor_scan(bwd[:, ::-1], neg[:, P:0:-1], sd[:, 0, ::-1], -BIG, ALU.add,
                                     ALU.max).then_inc(fb_ready, 1)
                if more:
                    one_hot(k + 1, 1 - u, 1)
                    one_hot(k + 1, 1 - u, 2)
                dve.wait_ge(rows_copied, k + 1)
                lf, ff, df, dl = (rows[:, j, :, :] for j in range(4))
                inner = slice(1, CH + 1)
                c.link(v.tensor_tensor(link[:, 0, :, inner], df[:, :, inner], dl[:, :, 0:CH], ALU.is_equal))
                c.link(v.tensor_tensor(link[:, 1, :, inner], df[:, :, inner], dl[:, :, inner], ALU.is_equal))
                c.link(v.tensor_copy(fac[:, 2, :], link[:, 0, :, 1:2].rearrange("o h b -> o (h b)")))
                both = link[:, :, :, inner].rearrange("o a h b -> o (a h) b")
                c.link(v.tensor_scalar(both, both, 1.0, BIG, ALU.subtract, ALU.mult))
                v.tensor_tensor(af[:, :, inner], link[:, 0, :, inner], link[:, 1, :, inner], ALU.add)
                c.link(v.tensor_tensor(ab[:, :, inner], link[:, 0, :, 2:W], link[:, 1, :, inner], ALU.add))

                def flat(t):
                    return t.rearrange("o h b -> o (h b)")

                v.tensor_tensor_scan(flat(cof[:, :, :]), flat(af[:, :, :]), flat(lf), -BIG, ALU.add, ALU.max)
                c.link(v.tensor_tensor_scan(flat(cob[:, :, :])[:, ::-1], flat(ab[:, :, :])[:, ::-1],
                                            flat(ff)[:, ::-1], -BIG, ALU.add, ALU.max))
                cv = carry[:, :, :].rearrange("o a (h b) -> o a h b", h=H)
                v.tensor_tensor(cv[:, 0, :, :], cof[:, :, 0:CH], link[:, 0, :, inner], ALU.add)
                v.tensor_tensor(cv[:, 1, :, :], cob[:, :, 2:W], link[:, 0, :, 2:W], ALU.add
                                ).then_inc(carries_ready, 1)
                c.link(v.tensor_tensor(fac[:, 0, :].rearrange("o (h b) -> o h b", b=1), lf[:, :, 0:1],
                                       cob[:, :, 1:2], ALU.subtract))
                c.link(v.scalar_tensor_tensor(fac[:, 0, :], fac[:, 0, :], 0.0, fac[:, 2, :], ALU.min, ALU.mult))
                v.tensor_copy(lf[:, :, 0:1], cof[:, :, CH:CH + 1]).then_inc(fac_ready, 1)
                v.tensor_copy(dl[:, :, 0:1], dl[:, :, CH:CH + 1])
                if more:
                    one_hot(k + 1, 1 - u, 3)
                dve.wait_ge(cols_ready, k + 1)
                v.tensor_tensor_scan(fwd[:, :], neg[:, 0:P], sd[:, 0, :], psd[0:ROWS, 384:385], ALU.add, ALU.max)
                c.link(v.tensor_tensor_scan(bwd[:, ::-1], neg[:, P:0:-1], sd[:, 0, ::-1],
                                            psd[0:ROWS, 385:386], ALU.add, ALU.max))
                v.tensor_tensor(mx[:, :], fwd[:, :], bwd[:, :], ALU.max).then_inc(m_ready, 1)
                if more:
                    one_hot(k + 1, 1 - u, 4)
                dve.wait_ge(mt_ready, k + 1)
                v.tensor_tensor(exin[:, :, :], sc[:, :, :],
                                psd[:, 256:256 + ROWS].rearrange("p (h b) -> p h b", h=H), ALU.subtract
                                ).then_inc(exin_ready, 1)
                if more:
                    one_hot(k + 1, 1 - u, 5)
                dve.wait_ge(ex_ready, k + 1)
                t0 = dve.value_load(part(C.tpi, k, 0, 1), min_val=0, max_val=NT)
                dve.wait_ge(sc_ready, k + 1)
                dve.wait_ge(acc_done, NGR * k + 2)
                tile = C.acc[:, bass.ds(t0, 1), :].rearrange("p o f -> p (o f)")
                fv = prow[:, 400:400 + H]
                c.link(v.tensor_tensor(tile[:, 0:F].rearrange("p (h d) -> p h d", h=H),
                                       tile[:, 0:F].rearrange("p (h d) -> p h d", h=H), col(fv, HD), ALU.mult))
                c.link(v.tensor_tensor(tile[:, F:FW], tile[:, F:FW], fv, ALU.mult))
                assert c.n == N2, c.n

                def scale(n):
                    b, m = G * n, G - 1
                    gv = gat[u][:, b:b + m, 0:F].rearrange("p b (h d) -> p b h d", h=H)
                    v.tensor_tensor(gv, gv, ex[:, :, b:b + m].rearrange("p h (b o) -> p b h o", o=1)
                                    .to_broadcast([P, m, H, HD]), ALU.mult).then_inc(scaled, 1)

                scale(0)
                scale(1)
                for n in range(NGR):
                    if n + 2 < NGR:
                        scale(n + 2)
                    t = dve.value_load(part(C.tpi, k, G * n, 1), min_val=0, max_val=NT)
                    dve.wait_ge(mm_done, NGR * (k + 2) + n + 1)
                    if n:
                        dve.wait_ge(acc_done, NGR * k + n + 2)
                    tile = C.acc[:, bass.ds(t, 1), :].rearrange("p o f -> p (o f)")
                    v.tensor_tensor(tile, tile, pacc[:, n % 2, 0:GW], ALU.add).then_inc(acc_done, 1)
                    if more and n == 2:
                        edge_er(k + 1, 1 - u)

            for n in range(NGR):
                one_hot(0, 0, n)
            edge_er(0, 0)
            with dve.Fori(0, NCH // 2 - 1) as i:
                for u in range(2):
                    chunk(2 * i + u, u, True)
            chunk(NCH - 2, 0, True)
            chunk(NCH - 1, 1, False)

        @block.tensor
        def _(pe):
            t_ = nc.tensor
            pe.sem_inc(er_ready, 1)
            pe.sem_inc(mm_done, 2 * NGR)

            def turn(k, u, n):
                pe.wait_ge(hot_ready, NGR * k + n + 1)
                if n >= 2:
                    pe.wait_ge(copied, NGR * k + n - 1)
                for j in range(G):
                    last = t_.transpose(pt[:, n % 2, j * P:(j + 1) * P], hot[u][:, G * n + j, :], C.ident[:, :])
                last.then_inc(turned, 1)

            def pick_er(k, n):
                at = k * CH + G * n
                t = pe.value_load(C.tpi[0:1, at:at + 1] if isinstance(k, int) else C.tpi[0:1, bass.ds(at, 1)],
                                  min_val=0, max_val=NT)
                pe.wait_ge(copied, NGR * k + n + 1)
                for j in range(G * n, G * n + G):
                    last = t_.matmul(per[:, j // 16, (j % 16) * R * H:(j % 16 + 1) * R * H], hott[:, j, :],
                                     C.er[:, bass.ds(t, 1), :].rearrange("p o r -> p (o r)"),
                                     start=True, stop=True)
                if n == NGR - 1:
                    last.then_inc(er_ready, 1)

            def chunk(k, u, more):
                v = 1 - u
                pe.wait_ge(s_ready, k + 1)
                t_.transpose(psd[0:ROWS, 0:P], sc[:, :, :].rearrange("p h b -> p (h b)"), C.ident[:, :])
                t_.transpose(psd[0:ROWS, P:2 * P], d4[:, :, :].rearrange("p h b -> p (h b)"),
                             C.ident[:, :]).then_inc(sd_turned, 1)
                if more:
                    turn(k + 1, v, 0)
                pe.wait_ge(fb_ready, k + 1)
                for j, a in enumerate((fwd[:, P - 1:P], bwd[:, 0:1], sd[:, 1, 0:1], sd[:, 1, P - 1:P])):
                    last = t_.matmul(prow[0:1, j * ROWS:(j + 1) * ROWS], a, C.ident[0:ROWS, 0:ROWS],
                                     start=True, stop=True)
                last.then_inc(rows_ready, 1)
                if more:
                    turn(k + 1, v, 1)
                    pe.wait_ge(ers_ready, k + 2)
                    pick_er(k + 1, 0)
                    turn(k + 1, v, 2)
                    pick_er(k + 1, 1)
                pe.wait_ge(carries_ready, k + 1)
                for j in range(2):
                    last = t_.matmul(psd[0:ROWS, 384 + j:385 + j], carry[:, j, :], C.ones[0:1, 0:1],
                                     start=True, stop=True)
                last.then_inc(cols_ready, 1)
                if more:
                    pick_er(k + 1, 2)
                pe.wait_ge(facm_ready, k + 1)
                t_.matmul(prow[:, 400:400 + H], hot0[:, 0, :], fac[:, 1, :], start=True, stop=False)
                t_.matmul(prow[:, 400:400 + H], hot0[:, 1, :], fac[:, 3, :], start=False,
                          stop=True).then_inc(sc_ready, 1)
                pe.wait_ge(m_ready, k + 1)
                t_.transpose(psd[:, 256:256 + ROWS], mx[:, :], C.ident[0:ROWS, 0:ROWS]).then_inc(mt_ready, 1)
                if more:
                    turn(k + 1, v, 3)
                    turn(k + 1, v, 4)
                    pick_er(k + 1, 3)
                for n in range(NGR):
                    pe.wait_ge(scaled, NGR * k + n + 1)
                    pe.wait_ge(scaled_act, NGR * k + n + 1)
                    pe.wait_ge(acc_done, NGR * k + n + 1)
                    for j in range(G):
                        last = t_.matmul(pacc[:, n % 2, 0:GW], hot[u][:, G * n + j, :],
                                         gat[u][:, G * n + j, 0:GW], start=(j == 0), stop=(j == G - 1))
                    last.then_inc(mm_done, 1)
                    if more and n == 0:
                        turn(k + 1, v, 5)
                    if more and n < 2:
                        pick_er(k + 1, n + 4)

            pe.wait_ge(ers_ready, 1)
            turn(0, 0, 0)
            for n in range(NGR):
                if n + 1 < NGR:
                    turn(0, 0, n + 1)
                pick_er(0, n)
            with pe.Fori(0, NCH // 2 - 1) as i:
                for u in range(2):
                    chunk(2 * i + u, u, True)
            chunk(NCH - 2, 0, True)
            chunk(NCH - 1, 1, False)

    for slot in C.slots:
        slot.base += 16 * (NCH // 2)


def across(row, n):
    return row.rearrange("p (o m) -> p o m", o=1).to_broadcast([row.shape[0], n, row.shape[1]])


def layernorm(nc, c, act_sqrt, x, sq, mean, var):
    v = nc.vector
    nt = x.shape[1]
    c.link(v.tensor_reduce(mean, x, AX.X, ALU.add))
    c.link(v.tensor_scalar(mean, mean, 1.0 / F, None, ALU.mult))
    c.link(v.tensor_tensor(x, x, col(mean, F), ALU.subtract))
    c.link(v.tensor_tensor(sq, x, x, ALU.mult))
    c.link(v.tensor_reduce(var, sq, AX.X, ALU.add))
    c.link(v.tensor_scalar(var, var, 1.0 / F, 1e-5, ALU.mult, ALU.add))
    c.link(v.reciprocal(var, var))
    act_sqrt()
    c.link(v.tensor_tensor(x, x, col(var, F), ALU.mult))


def norm_phase(nc, C, D):
    ctx, sems = ExitStack(), []
    with ctx:
        def sb(name, shape, dt=F32):
            return ctx.enter_context(nc.sbuf_tensor(name, shape, dt))

        def sem(name):
            sems.append(nc.alloc_semaphore(name))
            return sems[-1]

        bias = sb("hbias", [P, F])
        rden = sb("rden", [P, NT, H])
        mean = sb("mean0", [P, NT])
        var = sb("var0", [P, NT])
        bias_loaded = sem("hbias_loaded")
        dch = sem("dve_norm0")
        var_ready = sem("var_ready0")
        std_ready = sem("std_ready0")
        deg_ready = sem("deg_ready0")
        hs_ready = sem("hs_ready")
        hs_stored = sem("hs_stored")
        ctx.callback(clear, nc, sems)
        block = ctx.enter_context(nc.Block())

        @block.sync
        def _(sp):
            sp.dma_start(bias[:, :], D.hbias.rearrange("(o f) -> o f", o=1).to_broadcast([P, F])
                         ).then_inc(bias_loaded, 16)
            sp.wait_ge(hs_ready, 1)
            sp.dma_start(D.hs.rearrange("(t p) f -> p t f", p=P), C.acc[:, 0:NT, 0:F]).then_inc(hs_stored, 16)
            sp.wait_ge(hs_stored, 16)

        @block.scalar
        def _(act):
            act.wait_ge(deg_ready, 1)
            nc.scalar.activation(C.rdego[:, :], C.rdego[:, :], ACT.Sqrt)
            nc.scalar.activation(C.rdegi[:, :], C.rdegi[:, :], ACT.Sqrt).then_inc(std_ready, 1)
            act.wait_ge(var_ready, 1)
            nc.scalar.activation(var[:, :], var[:, :], ACT.Sqrt).then_inc(std_ready, 1)

        @block.vector
        def _(dve):
            v = nc.vector
            c = Chain(dve, dch)
            c.link(v.tensor_scalar(C.rdego[:, :], C.dego[:, :], 1.0, None, ALU.max))
            c.link(v.reciprocal(C.rdego[:, :], C.rdego[:, :]))
            c.link(v.tensor_scalar(C.rdegi[:, :].rearrange("p (t o) -> p t o", o=1), C.acc[:, 0:NT, FW:GW],
                                   1.0, None, ALU.max))
            v.reciprocal(C.rdegi[:, :], C.rdegi[:, :]).then_inc(deg_ready, 1)
            c.link(v.tensor_scalar(rden[:, :, :], C.acc[:, 0:NT, F:FW], 1e-30, None, ALU.max))
            c.link(v.reciprocal(rden[:, :, :], rden[:, :, :]))
            hv = C.acc[:, 0:NT, 0:F].rearrange("p t (h d) -> p t h d", h=H)
            c.link(v.tensor_tensor(hv, hv, rden[:, :, :].rearrange("p t (h o) -> p t h o", o=1)
                                   .to_broadcast([P, NT, H, HD]), ALU.mult))
            c.link(v.tensor_tensor(C.x[:, :, :], C.x[:, :, :], C.acc[:, 0:NT, 0:F], ALU.add))
            dve.wait_ge(bias_loaded, 16)
            c.link(v.tensor_tensor(C.x[:, :, :], C.x[:, :, :], across(bias[:, :], NT), ALU.add))

            def root():
                v.tensor_copy(mean[:, :], var[:, :]).then_inc(var_ready, 1)
                dve.wait_ge(std_ready, 2)

            layernorm(nc, c, root, C.x[:, :, :], C.acc[:, 0:NT, 0:F], mean[:, :], var[:, :])
            v.tensor_tensor(C.acc[:, 0:NT, 0:F], C.x[:, :, :], col(C.rdego[:, :], F), ALU.mult
                            ).then_inc(hs_ready, 1)
            dve.wait_ge(hs_stored, 16)
            v.memset(C.acc[:, :, :], 0.0)


def conv_phase(nc, C, D):
    ctx, sems = ExitStack(), []
    with ctx:
        def sb(name, shape, dt=F32):
            return ctx.enter_context(nc.sbuf_tensor(name, shape, dt))

        def sem(name):
            sems.append(nc.alloc_semaphore(name))
            return sems[-1]

        gat = [sb(f"gatb{u}", [P, CH, F]) for u in range(2)]
        hot = [sb(f"hotb{u}", [P, CH, P]) for u in range(2)]
        gidx = [sb(f"gidxb{u}", [P, CH], I32) for u in range(2)]
        pacc = ctx.enter_context(nc.psum_tensor("paccb", [P, 2, 512], F32))
        gathered = [C.slots[u * CH:(u + 1) * CH] for u in range(2)]
        idx_ready = sem("idx_readyb")
        hot_ready = sem("hot_readyb")
        mm_done = sem("mm_doneb")
        acc_done = sem("acc_doneb")
        ctx.callback(clear, nc, sems)
        block = ctx.enter_context(nc.Block())

        @block.gpsimd
        def _(g):
            with g.Fori(0, NCH // 2) as i:
                for u in range(2):
                    k = 2 * i + u
                    g.wait_ge(mm_done, NGR * (k + 1))
                    g.tensor_copy(gidx[u][:, :], C.srci[:, bass.ds(k * CH, CH)]).then_inc(idx_ready, 1)
                    g.wait_ge(idx_ready, k + 1)
                    g.nop(nofuse=True)
                    for b in range(CH):
                        g.indirect_dma_start(gat[u][:, b, :], None, D.hs,
                                             bass.IndirectOffsetOnAxis(ap=gidx[u][:, b:b + 1], axis=0)
                                             ).then_inc(gathered[u][b].sem, 16)

        @block.vector
        def _(dve):
            v = nc.vector
            dve.sem_inc(acc_done, 2)
            with dve.Fori(0, NCH // 2) as i:
                for u in range(2):
                    k = 2 * i + u
                    v.tensor_tensor(hot[u][:, :, :], col(C.locf[:, bass.ds(k * CH, CH)], P),
                                    across(C.iota[:, :], CH), ALU.is_equal).then_inc(hot_ready, 1)
                    for n in range(NGR):
                        t = dve.value_load(C.tpi[0:1, bass.ds(k * CH + G * n, 1)], min_val=0, max_val=NT)
                        dve.wait_ge(mm_done, NGR * (k + 2) + n + 1)
                        if n:
                            dve.wait_ge(acc_done, NGR * k + n + 2)
                        tile = C.acc[:, bass.ds(t, 1), 0:F].rearrange("p o f -> p (o f)")
                        v.tensor_tensor(tile, tile, pacc[:, n % 2, 0:F], ALU.add).then_inc(acc_done, 1)

        @block.tensor
        def _(pe):
            pe.sem_inc(mm_done, 2 * NGR)
            with pe.Fori(0, NCH // 2) as i:
                for u in range(2):
                    k = 2 * i + u
                    pe.wait_ge(hot_ready, k + 1)
                    for j in range(CH):
                        pe.wait_ge(gathered[u][j].sem, gathered[u][j].base + 16 * i + 16)
                        if j % G == 0:
                            pe.wait_ge(acc_done, NGR * k + j // G + 1)
                        last = nc.tensor.matmul(pacc[:, j // G % 2, 0:F], hot[u][:, j, :], gat[u][:, j, :],
                                                start=(j % G == 0), stop=(j % G == G - 1))
                        if j % G == G - 1:
                            last.then_inc(mm_done, 1)

    for slot in C.slots:
        slot.base += 16 * (NCH // 2)


def gate_phase(nc, C, D):
    ctx, sems = ExitStack(), []
    with ctx:
        def sb(name, shape, dt=F32):
            return ctx.enter_context(nc.sbuf_tensor(name, shape, dt))

        def sem(name):
            sems.append(nc.alloc_semaphore(name))
            return sems[-1]

        w = sb("w_gcres", [P, 4, F])
        wgate = sb("wgate", [P, 2, NE])
        brow = sb("brow", [1, 2, F])
        bgrow = sb("bgrow", [1, NE])
        stage = [sb(f"stage{u}", [P, 2 * F]) for u in range(2)]
        xt = [sb(f"xmt{u}", [P, 4, P]) for u in range(2)]
        x2t = [sb(f"x2t{u}", [P, 2, P]) for u in range(2)]
        logit = sb("logit", [P, NT, NE])
        top = sb("top", [P, NT, 8])
        topi = sb("topi", [P, NT, 8], U32)
        topf = sb("topf", [P, NT, 2])
        m = [sb(f"mask{k}", [P, NT, NE]) for k in range(2)]
        mb = sb("mask_b", [P, NT, NE], BF16)
        tri = sb("tri", [P, P], BF16)
        onesb = sb("ones_b", [P, P], BF16)
        valid = sb("valid", [P, NT])
        ct = sb("ct", [P, NE, NT])
        inc = sb("inc", [P, NE, NT])
        again = sb("again", [P, NE, NT])
        rank = sb("rank", [P, NT, NE])
        tmp = sb("ranktmp", [P, NT, NE])
        tot = sb("tot", [P, NE])
        toti = sb("toti", [P, NE], I32)
        tiles = sb("tiles", [P, NE])
        onese = sb("ones_e", [P, NE])
        tend = sb("tend", [P, NE])
        toff = sb("toff", [P, NE])
        rk = sb("rk", [P, 2, NT])
        sl = sb("sl", [P, 2, NT])
        ok = sb("ok", [P, 2, NT])
        e1 = sb("e1", [P, NT])
        scat = sb("scat", [P, 2, NT], I32)
        scatf = sb("scatf", [P, 2, NT])
        ecmp = sb("ecmp", [P, NE])
        ecol = sb("ecol", [P, 1])
        bt = sb("b1_rows", [NE, HID])
        px = ctx.enter_context(nc.psum_tensor("pxg", [P, 512], F32))
        pm = ctx.enter_context(nc.psum_tensor("pmg", [P, 512], F32))
        pz = ctx.enter_context(nc.psum_tensor("pzg", [P, 512], F32))
        pl = ctx.enter_context(nc.psum_tensor("plg", [P, 512], F32))
        pr = ctx.enter_context(nc.psum_tensor("prg", [P, 4, 512], F32))

        w_loaded = sem("w_gcres_loaded")
        b_loaded = sem("bias_loaded1")
        consts = sem("gate_consts")
        dch = sem("dve_gate")
        lch = sem("dve_gate_loop")
        staged = sem("staged")
        turned = sem("turned_g")
        xt_ready = sem("xt_ready_g")
        x2_ready = sem("x2_ready")
        x2_copied = sem("x2_copied")
        x2_turned = sem("x2_turned")
        x2t_ready = sem("x2t_ready")
        l_ready = sem("l_ready")
        l_copied = sem("l_copied")
        masks_ready = sem("masks_ready")
        counts_ready = sem("counts_ready")
        counts_read = sem("counts_read")
        ranks_ready = sem("ranks_ready")
        diff_ready = sem("diff_ready")
        e_ready = sem("e_ready")
        slots_ready = sem("slots_ready")
        ecol_ready = sem("ecol_ready")
        erow_ready = sem("erow_ready")
        b1t_ready = sem("b1t_ready")
        b1t_copied = sem("b1t_copied")
        NS = 30
        scattered = C.slots[0:NS]
        ctx.callback(clear, nc, sems)
        block = ctx.enter_context(nc.Block())

        @block.sync
        def _(sp):
            sp.dma_start(w[:, 0:2, :], D.wgc.rearrange("(c p) n -> p c n", p=P)).then_inc(w_loaded, 16)
            sp.dma_start(w[:, 2:4, :], D.wres.rearrange("(c p) n -> p c n", p=P)).then_inc(w_loaded, 16)
            sp.dma_start(wgate[:, :, :], D.wg.rearrange("(c p) n -> p c n", p=P)).then_inc(w_loaded, 16)
            sp.dma_start(bt[:, :], D.b1).then_inc(b_loaded, 16)
            sp.dma_start(C.b2[:, :], D.b2).then_inc(b_loaded, 16)
            sp.dma_start(brow[:, 0, :], D.bgc.rearrange("(o f) -> o f", o=1)).then_inc(b_loaded, 16)
            sp.dma_start(brow[:, 1, :], D.bres.rearrange("(o f) -> o f", o=1)).then_inc(b_loaded, 16)
            sp.dma_start(bgrow[:, :], D.bg.rearrange("(o f) -> o f", o=1)).then_inc(b_loaded, 16)
            sp.wait_ge(w_loaded, 48)
            sp.wait_ge(b_loaded, 80)

        @block.gpsimd
        def _(g):
            g.memset(tri[:, :], 1.0).then_inc(consts, 1)
            g.wait_ge(consts, 1)
            g.affine_select(out=tri[:, :], in_=tri[:, :], compare_op=ALU.is_gt, fill=0.0, base=0,
                            pattern=[[1, P]], channel_multiplier=-1).then_inc(consts, 1)
            g.wait_ge(slots_ready, 1)
            for k in range(2):
                for t in range(NT):
                    n = k * NT + t
                    if n >= NS:
                        g.wait_ge(scattered[n % NS].sem, scattered[n % NS].base + 16 * (n // NS))
                    g.indirect_dma_start(D.buf, bass.IndirectOffsetOnAxis(ap=scat[:, k, t:t + 1], axis=0),
                                         C.x2[:, t, :], None, bounds_check=NX * P - 1, oob_is_err=False
                                         ).then_inc(scattered[n % NS].sem, 16)
            for slot in scattered:
                g.wait_ge(slot.sem, slot.base + 16 * (2 * NT // NS))

        @block.scalar
        def _(act):
            a = nc.scalar
            act.sem_inc(x2t_ready, 2)
            with act.Fori(0, NT // 2) as i:
                for u in range(2):
                    t = 2 * i + u
                    act.wait_ge(turned, t + 1)
                    act.wait_ge(x2_ready, t + 1)
                    a.activation(xt[u][:, :, :], px[:, :].rearrange("p (c n) -> p c n", n=P), ACT.Copy
                                 ).then_inc(xt_ready, 1)
                    act.wait_ge(x2_ready, t + 3)
                    a.activation(C.x2[:, bass.ds(t, 1), :].rearrange("p o f -> p (o f)"), pm[:, 0:F], ACT.Copy)
                    a.activation(stage[u][:, 0:F], pm[:, 0:F], ACT.Copy).then_inc(x2_copied, 1)
                    act.wait_ge(x2_turned, t + 1)
                    a.activation(x2t[u][:, :, :], pz[:, 0:F].rearrange("p (c n) -> p c n", n=P), ACT.Copy
                                 ).then_inc(x2t_ready, 1)
                    act.wait_ge(l_ready, t + 1)
                    a.activation(logit[:, bass.ds(t, 1), :].rearrange("p o f -> p (o f)"), pl[:, 0:NE],
                                 ACT.Copy).then_inc(l_copied, 1)
            act.wait_ge(b1t_ready, 1)
            for j in range(4):
                last = a.activation(C.b1t[:, :, j], pl[:, j * NE:(j + 1) * NE], ACT.Copy)
            last.then_inc(b1t_copied, 1)
            act.wait_ge(diff_ready, 1)
            a.activation(e1[:, :], e1[:, :], ACT.Exp).then_inc(e_ready, 1)

        @block.vector
        def _(dve):
            v = nc.vector
            c = Chain(dve, dch)
            dve.wait_ge(b_loaded, 80)
            c.link(v.tensor_tensor(brow[:, 0, :], brow[:, 0, :], brow[:, 1, :], ALU.add))
            c.link(v.memset(onesb[:, :], 1.0))
            c.link(v.memset(onese[:, :], 1.0))
            c.link(v.memset(valid[:, :], 1.0))
            c.link(v.tensor_scalar(valid[:, NT - 1:NT], C.ioch[:, :], float(LAST), None, ALU.is_lt))
            c.link(v.memset(again[:, :, :], 1.0))
            c.link(v.memset(again[:, :, 0:1], 0.0))
            with dve.Fori(0, NT // 2) as i:
                for u in range(2):
                    t = 2 * i + u
                    dve.wait_ge(x2t_ready, t + 1)
                    v.tensor_tensor(stage[u][:, 0:F], C.acc[:, bass.ds(t, 1), 0:F].rearrange("p o f -> p (o f)"),
                                    C.rdegi[:, bass.ds(t, 1)].to_broadcast([P, F]), ALU.mult)
                    v.tensor_copy(stage[u][:, F:2 * F], C.x[:, bass.ds(t, 1), :].rearrange("p o f -> p (o f)")
                                  ).then_inc(staged, 1)
            dve.wait_ge(l_copied, NT)
            for t in range(NT):
                c.link(v.max(top[:, t, :], logit[:, t, :]))
                v.max_index(topi[:, t, :], top[:, t, :], logit[:, t, :]).then_inc(lch, 1)
            dve.wait_ge(lch, NT)
            v.tensor_tensor(e1[:, :], top[:, :, 1], top[:, :, 0], ALU.subtract).then_inc(diff_ready, 1)
            c.link(v.tensor_copy(topf[:, :, :], topi[:, :, 0:2]))
            for k in range(2):
                c.link(v.tensor_tensor(m[k][:, :, :], topf[:, :, k:k + 1].to_broadcast([P, NT, NE]),
                                       across(C.iota[:, 0:NE], NT), ALU.is_equal))
                c.link(v.tensor_tensor(m[k][:, :, :], m[k][:, :, :], col(valid[:, :], NE), ALU.mult))
            v.tensor_tensor(mb[:, :, :], m[0][:, :, :], m[1][:, :, :], ALU.add).then_inc(masks_ready, 1)
            dve.wait_ge(counts_ready, 1)
            for q in range(4):
                n = min(8, NT - 8 * q)
                c.link(v.tensor_copy(ct[:, :, 8 * q:8 * q + n].rearrange("p e t -> p t e"),
                                     pr[:, q, 0:n * NE].rearrange("p (t e) -> p t e", e=NE)))
            v.tensor_copy(rk[:, 0, 0:1], ct[:, 0, 0:1]).then_inc(counts_read, 1)
            c.link(v.tensor_tensor_scan(inc[:, :, :].rearrange("p e t -> p (e t)"),
                                        again[:, :, :].rearrange("p e t -> p (e t)"),
                                        ct[:, :, :].rearrange("p e t -> p (e t)"), 0.0, ALU.mult, ALU.add))
            c.link(v.tensor_copy(tot[:, :], inc[:, :, NT - 1]))
            c.link(v.tensor_scalar(tiles[:, :], tot[:, :], float(CAP), float(P - 1), ALU.min, ALU.add))
            c.link(v.tensor_copy(toti[:, :], tiles[:, :]))
            c.link(v.tensor_scalar(toti[:, :], toti[:, :], 7, None, ALU.arith_shift_right))
            c.link(v.tensor_copy(tiles[:, :], toti[:, :]))
            c.link(v.tensor_tensor_scan(tend[:, :], onese[:, :], tiles[:, :], 0.0, ALU.mult, ALU.add))
            c.link(v.tensor_tensor(toff[:, :], tend[:, :], tiles[:, :], ALU.subtract))
            c.link(v.tensor_scalar(toff[:, :], toff[:, :], float(P), None, ALU.mult))
            c.link(v.tensor_scalar(ecmp[:, :], tend[:, :], C.ioch[:, 0:1], None, ALU.is_le))
            c.link(v.tensor_reduce(ecol[:, :], ecmp[:, :], AX.X, ALU.add))
            v.tensor_scalar(ecol[:, :], ecol[:, :], float(NE - 1), None, ALU.min).then_inc(ecol_ready, 1)
            c.link(v.tensor_tensor(inc[:, :, :], inc[:, :, :], ct[:, :, :], ALU.subtract))
            dve.wait_ge(ranks_ready, 1)
            for q in range(4):
                n = min(8, NT - 8 * q)
                c.link(v.tensor_tensor(rank[:, 8 * q:8 * q + n, :], pr[:, q, 0:n * NE].rearrange("p (t e) -> p t e", e=NE),
                                       inc[:, :, 8 * q:8 * q + n].rearrange("p e t -> p t e"), ALU.add))
            for k in range(2):
                c.link(v.tensor_tensor(tmp[:, :, :], rank[:, :, :], m[k][:, :, :], ALU.mult))
                c.link(v.tensor_reduce(rk[:, k, :], tmp[:, :, :], AX.X, ALU.add))
                c.link(v.tensor_tensor(tmp[:, :, :], across(toff[:, :], NT), m[k][:, :, :], ALU.mult))
                c.link(v.tensor_reduce(sl[:, k, :], tmp[:, :, :], AX.X, ALU.add))
            c.link(v.tensor_tensor(sl[:, :, :], sl[:, :, :], rk[:, :, :], ALU.add))
            c.link(v.tensor_scalar(ok[:, :, :], rk[:, :, :], float(CAP), None, ALU.is_lt))
            c.link(v.tensor_tensor(ok[:, :, :], ok[:, :, :], across(valid[:, :], 2), ALU.mult))
            c.link(v.tensor_tensor(sl[:, :, :], sl[:, :, :], ok[:, :, :], ALU.mult))
            c.link(v.tensor_scalar(scatf[:, :, :], ok[:, :, :], -float(NX * P), float(NX * P), ALU.mult, ALU.add))
            c.link(v.tensor_tensor(scatf[:, :, :], scatf[:, :, :], sl[:, :, :], ALU.add))
            c.link(v.tensor_copy(C.slot[:, :, :], sl[:, :, :]))
            v.tensor_copy(scat[:, :, :], scatf[:, :, :]).then_inc(slots_ready, 1)
            dve.wait_ge(e_ready, 1)
            c.link(v.tensor_scalar(C.gate[:, 0, :], e1[:, :], 1.0, None, ALU.add))
            c.link(v.reciprocal(C.gate[:, 0, :], C.gate[:, 0, :]))
            c.link(v.tensor_tensor(C.gate[:, 1, :], C.gate[:, 0, :], e1[:, :], ALU.mult))
            c.link(v.tensor_tensor(C.gate[:, :, :], C.gate[:, :, :], ok[:, :, :], ALU.mult))
            c.link(v.tensor_tensor(C.gm[:, :, :], m[0][:, :, :], col(C.gate[:, 0, :], NE), ALU.mult))
            c.link(v.tensor_tensor(tmp[:, :, :], m[1][:, :, :], col(C.gate[:, 1, :], NE), ALU.mult))
            c.link(v.tensor_tensor(C.gm[:, :, :], C.gm[:, :, :], tmp[:, :, :], ALU.add))
            c.link(v.tensor_copy(C.valid[:, :], valid[:, :]))
            dve.wait_ge(erow_ready, 1)
            v.tensor_copy(C.used[:, :], tend[0:1, NE - 1:NE])
            v.tensor_copy(C.expert[:, :], pz[0:1, 0:P]).then_inc(lch, 1)

        @block.tensor
        def _(pe):
            t_ = nc.tensor
            pe.wait_ge(w_loaded, 48)
            pe.wait_ge(b_loaded, 80)
            pe.sem_inc(x2_ready, 2)
            with pe.Fori(0, NT // 2) as i:
                for u in range(2):
                    t = 2 * i + u
                    pe.wait_ge(staged, t + 1)
                    for c in range(4):
                        last = t_.transpose(px[:, c * P:(c + 1) * P], stage[u][:, c * P:(c + 1) * P], C.ident[:, :])
                    last.then_inc(turned, 1)
                    pe.wait_ge(xt_ready, t + 1)
                    for c in range(4):
                        t_.matmul(pm[:, 0:F], xt[u][:, c, :], w[:, c, :], start=(c == 0), stop=False)
                    t_.matmul(pm[:, 0:F], C.ones[0:1, :], brow[:, 0, :], start=False, stop=True
                              ).then_inc(x2_ready, 1)
                    pe.wait_ge(x2_copied, t + 1)
                    for c in range(2):
                        last = t_.transpose(pz[:, c * P:(c + 1) * P], stage[u][:, c * P:(c + 1) * P], C.ident[:, :])
                    last.then_inc(x2_turned, 1)
                    pe.wait_ge(x2t_ready, t + 3)
                    for c in range(2):
                        t_.matmul(pl[:, 0:NE], x2t[u][:, c, :], wgate[:, c, :], start=(c == 0), stop=False)
                    t_.matmul(pl[:, 0:NE], C.ones[0:1, :], bgrow[:, :], start=False, stop=True
                              ).then_inc(l_ready, 1)
                    pe.wait_ge(l_copied, t + 1)
            for j in range(4):
                last = t_.transpose(pl[:, j * NE:(j + 1) * NE], bt[:, j * P:(j + 1) * P], C.ident[0:NE, 0:NE])
            last.then_inc(b1t_ready, 1)
            pe.wait_ge(masks_ready, 1)
            pe.wait_ge(consts, 2)
            for turn, (lhs, done) in enumerate(((onesb, counts_ready), (tri, ranks_ready))):
                if turn:
                    pe.wait_ge(counts_read, 1)
                for q in range(4):
                    n = min(8, NT - 8 * q)
                    last = t_.matmul(pr[:, q, 0:n * NE], lhs[:, :],
                                     mb[:, 8 * q:8 * q + n, :].rearrange("p t e -> p (t e)"), start=True, stop=True)
                last.then_inc(done, 1)
            pe.wait_ge(ecol_ready, 1)
            t_.matmul(pz[0:1, 0:P], ecol[:, :], C.ident[:, :], start=True, stop=True).then_inc(erow_ready, 1)

    for slot in scattered:
        slot.base += 16 * (2 * NT // NS)


def expert_phase(nc, C, D):
    ctx, sems = ExitStack(), []
    with ctx:
        def sb(name, shape, dt=F32):
            return ctx.enter_context(nc.sbuf_tensor(name, shape, dt))

        def sem(name):
            sems.append(nc.alloc_semaphore(name))
            return sems[-1]

        w1 = [sb(f"w1_{u}", [P, 2, HID]) for u in range(XG)]
        w2 = [sb(f"w2_{u}", [P, 4, F]) for u in range(XG)]
        xb = [sb(f"xb{u}", [P, F]) for u in range(XG)]
        xt = [sb(f"xbt{u}", [P, 2, P]) for u in range(XG)]
        h1 = [sb(f"h1_{u}", [P, 4, P]) for u in range(XG)]
        yb = [sb(f"yb{u}", [P, F]) for u in range(XG)]
        px = ctx.enter_context(nc.psum_tensor("pxe", [P, 2, 512], F32))
        ph = ctx.enter_context(nc.psum_tensor("phe", [P, 2, 512], F32))
        py = ctx.enter_context(nc.psum_tensor("pye", [P, 2, 512], F32))
        w_loaded = [sem(f"w_loaded{u}") for u in range(XG)]
        x_loaded = [sem(f"xb_loaded{u}") for u in range(XG)]
        y_stored = C.slots[0:XG]
        x_turned = sem("xb_turned")
        xt_ready = sem("xbt_ready")
        h_ready = sem("h_ready")
        g_ready = sem("g_ready")
        y_ready = sem("y_ready")
        y_copied = sem("y_copied")
        y_free = sem("y_free")
        ctx.callback(clear, nc, sems)
        block = ctx.enter_context(nc.Block())

        @block.sync
        def _(sp):
            used = sp.value_load(C.used[0:1, 0:1], min_val=1, max_val=NX)
            rows = D.buf.rearrange("(t p) f -> t p f", p=P)
            with sp.Fori(0, NX // XG) as i:
                with sp.If(used > XG * i):
                    for u in range(XG):
                        t = XG * i + u
                        e = sp.value_load(C.expert[0:1, bass.ds(t, 1)], min_val=0, max_val=NE - 1)
                        sp.wait_ge(y_ready, t + 1)
                        sp.dma_start(xb[u][:, :], rows[bass.ds(t, 1), :, :].rearrange("o p f -> (o p) f")
                                     ).then_inc(x_loaded[u], 16)
                        sp.dma_start(w1[u][:, :, :], D.w1[bass.ds(e, 1), :, :]
                                     .rearrange("o (p c) h -> (o p) c h", c=2)).then_inc(w_loaded[u], 16)
                        sp.dma_start(w2[u][:, :, :], D.w2[bass.ds(e, 1), :, :]
                                     .rearrange("o (c p) f -> (o p) c f", p=P)).then_inc(w_loaded[u], 16)

        @block.gpsimd
        def _(g):
            g.sem_inc(y_free, XG)
            used = g.value_load(C.used[0:1, 0:1], min_val=1, max_val=NX)
            rows = D.buf.rearrange("(t p) f -> t p f", p=P)
            with g.Fori(0, NX // XG) as i:
                with g.If(used > XG * i):
                    for u in range(XG):
                        t = XG * i + u
                        g.wait_ge(y_copied, t + 3)
                        g.dma_start(rows[bass.ds(t, 1), :, :].rearrange("o p f -> (o p) f"), yb[u][:, :]
                                    ).then_inc(y_stored[u].sem, 16)
                    for u in range(XG):
                        g.wait_ge(y_stored[u].sem, y_stored[u].base + 16 * i + 16)
                    g.sem_inc(y_free, XG)

        @block.scalar
        def _(act):
            used = act.value_load(C.used[0:1, 0:1], min_val=1, max_val=NX)
            with act.Fori(0, NX // XG) as i:
                with act.If(used > XG * i):
                    for u in range(XG):
                        t = XG * i + u
                        e = act.value_load(C.expert[0:1, bass.ds(t, 1)], min_val=0, max_val=NE - 1)
                        act.wait_ge(y_ready, t + 1)
                        act.wait_ge(h_ready, t + 1)
                        for j in range(4):
                            last = nc.scalar.activation(h1[u][:, j, :], ph[:, u % 2, j * P:(j + 1) * P], ACT.Gelu,
                                                        bias=C.b1t[:, bass.ds(e, 1), j])
                        last.then_inc(g_ready, 1)

        @block.vector
        def _(dve):
            v = nc.vector
            dve.sem_inc(y_copied, 2)
            used = dve.value_load(C.used[0:1, 0:1], min_val=1, max_val=NX)
            with dve.Fori(0, NX // XG) as i:
                with dve.If(used > XG * i):
                    def turned(u):
                        t = XG * i + u
                        dve.wait_ge(x_turned, t + 1)
                        v.tensor_copy(xt[u][:, :, :], px[:, u % 2, 0:F].rearrange("p (c n) -> p c n", n=P)
                                      ).then_inc(xt_ready, 1)

                    def result(u):
                        t = XG * i + u
                        if u == 0:
                            dve.wait_ge(y_free, XG * i + XG)
                        dve.wait_ge(y_ready, t + XG + 1)
                        v.tensor_copy(yb[u][:, :], py[:, u % 2, 0:F]).then_inc(y_copied, 1)

                    turned(0)
                    turned(1)
                    turned(2)
                    result(0)
                    turned(3)
                    result(1)
                    result(2)
                    result(3)

        @block.tensor
        def _(pe):
            t_ = nc.tensor
            pe.sem_inc(y_ready, XG)
            used = pe.value_load(C.used[0:1, 0:1], min_val=1, max_val=NX)
            with pe.Fori(0, NX // XG) as i:
                with pe.If(used > XG * i):
                    def turn(u):
                        pe.wait_ge(x_loaded[u], 16 * i + 16)
                        if u >= 2:
                            pe.wait_ge(xt_ready, XG * i + u - 1)
                        for c in range(2):
                            last = t_.transpose(px[:, u % 2, c * P:(c + 1) * P],
                                                xb[u][:, :].rearrange("p (k c) -> p c k", c=2)[:, c, :],
                                                C.ident[:, :])
                        last.then_inc(x_turned, 1)

                    def hidden(u):
                        pe.wait_ge(w_loaded[u], 32 * i + 32)
                        pe.wait_ge(xt_ready, XG * i + u + 1)
                        if u >= 2:
                            pe.wait_ge(g_ready, XG * i + u - 1)
                        for j in range(4):
                            for c in range(2):
                                last = t_.matmul(ph[:, u % 2, j * P:(j + 1) * P], w1[u][:, c, j * P:(j + 1) * P],
                                                 xt[u][:, c, :], start=(c == 0), stop=(c == 1))
                        last.then_inc(h_ready, 1)

                    def result(u):
                        pe.wait_ge(g_ready, XG * i + u + 1)
                        pe.wait_ge(y_copied, XG * i + u + 1)
                        for j in range(4):
                            last = t_.matmul(py[:, u % 2, 0:F], h1[u][:, j, :], w2[u][:, j, :],
                                             start=(j == 0), stop=(j == 3))
                        last.then_inc(y_ready, 1)

                    turn(0)
                    turn(1)
                    hidden(0)
                    turn(2)
                    hidden(1)
                    result(0)
                    turn(3)
                    hidden(2)
                    result(1)
                    hidden(3)
                    result(2)
                    result(3)


def output_phase(nc, C, D):
    ctx, sems = ExitStack(), []
    with ctx:
        def sb(name, shape, dt=F32):
            return ctx.enter_context(nc.sbuf_tensor(name, shape, dt))

        def sem(name):
            sems.append(nc.alloc_semaphore(name))
            return sems[-1]

        NY = 4
        y = [[sb(f"y{k}_{u}", [P, F]) for u in range(NY)] for k in range(2)]
        gmt = [sb(f"gmt{u}", [NE, P]) for u in range(2)]
        vm = sb("vm", [P, P])
        mean = sb("bn_mean", [P, F])
        rstd = sb("bn_rstd", [P, F])
        gb = sb("gamma_beta", [P, 2, F])
        lmean = sb("lmean", [P, NT])
        lvar = sb("lvar", [P, NT])
        sq = C.acc[:, 0:NT, 0:F]
        pg = ctx.enter_context(nc.psum_tensor("pgo", [P, 2, 512], F32))
        pb = ctx.enter_context(nc.psum_tensor("pbo", [P, 2, 512], F32))
        ps = ctx.enter_context(nc.psum_tensor("pso", [P, 512], F32))
        gathered = [C.slots[XG + k * NY:XG + (k + 1) * NY] for k in range(2)]
        gb_loaded = sem("gb_loaded")
        turned = sem("gm_turned")
        gmt_ready = sem("gmt_ready")
        b2_ready = sem("b2_ready")
        y_added = sem("y_added")
        dch = sem("dve_out")
        vm_ready = sem("vm_ready")
        y_ready = sem("y_all_ready")
        sums_ready = sem("sums_ready")
        sq_ready = sem("sq_ready")
        var_ready = sem("var_ready1")
        std_ready = sem("std_ready1")
        out_ready = sem("out_ready")
        stored = sem("out_stored")
        ctx.callback(clear, nc, sems)
        block = ctx.enter_context(nc.Block())

        @block.sync
        def _(sp):
            for k, a in enumerate((D.gamma, D.beta)):
                sp.dma_start(gb[:, k, :], a.rearrange("(o f) -> o f", o=1).to_broadcast([P, F])
                             ).then_inc(gb_loaded, 16)
            sp.wait_ge(out_ready, 1)
            sp.dma_start(D.out[0:(NT - 1) * P, :].rearrange("(t p) f -> p t f", p=P), C.x[:, 0:NT - 1, :]
                         ).then_inc(stored, 16)
            sp.dma_start(D.out[(NT - 1) * P:N, :], C.x[0:LAST, NT - 1, :]).then_inc(stored, 16)
            sp.wait_ge(stored, 32)

        @block.gpsimd
        def _(g):
            for t in range(NT):
                if t >= NY:
                    g.wait_ge(y_added, t - NY + 1)
                for k in range(2):
                    g.indirect_dma_start(y[k][t % NY][:, :], None, D.buf,
                                         bass.IndirectOffsetOnAxis(ap=C.slot[:, k, t:t + 1], axis=0)
                                         ).then_inc(gathered[k][t % NY].sem, 16)

        @block.scalar
        def _(act):
            for t in range(NT):
                act.wait_ge(turned, t + 1)
                if t >= 2:
                    act.wait_ge(b2_ready, t - 1)
                nc.scalar.activation(gmt[t % 2][:, :], pg[0:NE, t % 2, 0:P], ACT.Copy).then_inc(gmt_ready, 1)
            act.wait_ge(var_ready, 1)
            nc.scalar.activation(rstd[:, :], rstd[:, :], ACT.Sqrt).then_inc(std_ready, 1)
            act.wait_ge(var_ready, 2)
            nc.scalar.activation(lvar[:, :], lvar[:, :], ACT.Sqrt).then_inc(std_ready, 1)

        @block.vector
        def _(dve):
            v = nc.vector
            c = Chain(dve, dch)
            v.tensor_copy(vm[:, :], C.valid[:, NT - 1:NT].to_broadcast([P, P])).then_inc(vm_ready, 1)
            for t in range(NT):
                for k in range(2):
                    dve.wait_ge(gathered[k][t % NY].sem, gathered[k][t % NY].base + 16 * (t // NY) + 16)
                    c.link(v.scalar_tensor_tensor(C.x2[:, t, :], y[k][t % NY][:, :], C.gate[:, k, t:t + 1],
                                                  C.x2[:, t, :], ALU.mult, ALU.add))
                dve.wait_ge(b2_ready, t + 1)
                v.tensor_tensor(C.x2[:, t, :], C.x2[:, t, :], pb[:, t % 2, 0:F], ALU.add).then_inc(y_added, 1)
            dve.wait_ge(sums_ready, 1)
            c.link(v.tensor_scalar(mean[:, :], ps[:, 0:F], 1.0 / N, None, ALU.mult))
            c.link(v.tensor_tensor(C.x2[:, :, :], C.x2[:, :, :], across(mean[:, :], NT), ALU.subtract))
            v.tensor_tensor(sq, C.x2[:, :, :], C.x2[:, :, :], ALU.mult).then_inc(sq_ready, 1)
            dve.wait_ge(sums_ready, 2)
            c.link(v.tensor_scalar(rstd[:, :], ps[:, 0:F], 1.0 / N, 1e-5, ALU.mult, ALU.add))
            c.link(v.reciprocal(rstd[:, :], rstd[:, :]))
            v.tensor_copy(mean[:, :], rstd[:, :]).then_inc(var_ready, 1)
            dve.wait_ge(std_ready, 1)
            dve.wait_ge(gb_loaded, 32)
            c.link(v.tensor_tensor(rstd[:, :], rstd[:, :], gb[:, 0, :], ALU.mult))
            c.link(v.tensor_tensor(C.x2[:, :, :], C.x2[:, :, :], across(rstd[:, :], NT), ALU.mult))
            c.link(v.tensor_tensor(C.x2[:, :, :], C.x2[:, :, :], across(gb[:, 1, :], NT), ALU.add))
            c.link(v.tensor_tensor(C.x[:, :, :], C.x[:, :, :], C.x2[:, :, :], ALU.add))

            def root():
                v.tensor_copy(lmean[:, :], lvar[:, :]).then_inc(var_ready, 1)
                dve.wait_ge(std_ready, 2)

            layernorm(nc, c, root, C.x[:, :, :], sq, lmean[:, :], lvar[:, :])
            v.tensor_copy(lmean[:, :], lvar[:, :]).then_inc(out_ready, 1)

        @block.tensor
        def _(pe):
            t_ = nc.tensor
            for t in range(NT):
                if t >= 2:
                    pe.wait_ge(gmt_ready, t - 1)
                t_.transpose(pg[0:NE, t % 2, 0:P], C.gm[:, t, :], C.ident[:, :]).then_inc(turned, 1)
                pe.wait_ge(gmt_ready, t + 1)
                if t >= 2:
                    pe.wait_ge(y_added, t - 1)
                t_.matmul(pb[:, t % 2, 0:F], gmt[t % 2][:, :], C.b2[:, :], start=True, stop=True
                          ).then_inc(b2_ready, 1)
            pe.wait_ge(vm_ready, 1)
            pe.wait_ge(y_added, NT)
            for n, a in enumerate((C.x2, sq)):
                if n:
                    pe.wait_ge(sq_ready, 1)
                for t in range(NT):
                    last = t_.matmul(ps[:, 0:F], vm[:, :] if t == NT - 1 else C.ones[:, :], a[:, t, :],
                                     start=(t == 0), stop=(t == NT - 1))
                last.then_inc(sums_ready, 1)


class Slot:

    def __init__(self, sem):
        self.sem, self.base = sem, 0


class Bag:
    pass


def gnn_program(nc, x, src, dst, typ, conv, attl, attr, hbias, wgc, bgc, wres, bres, wg, bg, w1, b1, w2,
                b2, gamma, beta, out, dbg):
    D, C = Bag(), Bag()
    D.x, D.src, D.dst, D.typ = x, src, dst, typ
    D.conv, D.attl, D.attr = conv, attl, attr
    D.tab = nc.dram_tensor("feature_table", (NT * P, R * FW), F32, kind="Internal").ap()
    D.buf = nc.dram_tensor("expert_rows", (NX * P, F), F32, kind="Internal").ap()
    D.hbias, D.wgc, D.bgc, D.wres, D.bres, D.wg, D.bg = hbias, wgc, bgc, wres, bres, wg, bg
    D.w1, D.b1, D.w2, D.b2, D.gamma, D.beta, D.out = w1, b1, w2, b2, gamma, beta, out
    D.hs = nc.dram_tensor("scaled_rows", (NT * P, F), F32, kind="Internal").ap()
    D.rec = nc.dram_tensor("edge_records", (NRG * P, 4 * P), F32, kind="Internal").ap()
    ctx = ExitStack()
    with ctx:
        def sb(name, shape, dt=F32):
            return ctx.enter_context(nc.sbuf_tensor(name, shape, dt))

        C.ident = sb("ident", [P, P])
        C.anti = sb("anti", [P, P])
        C.iota = sb("iota", [P, P])
        C.iota2 = sb("iota2", [P, P])
        C.ioch = sb("ioch", [P, 1])
        C.ones = sb("ones", [P, P])
        C.x = sb("x_sb", [P, NT, F])
        C.acc = sb("acc", [P, NT + 1, GW])
        C.rdego = sb("rdego", [P, NT])
        C.rdegi = sb("rdegi", [P, NT])
        C.dego = sb("dego", [P, NT])
        C.slots = [Slot(ctx.enter_context(nc.semaphore(f"gather_slot{n}"))) for n in range(2 * CH)]
        C.first_slots = [Slot(ctx.enter_context(nc.semaphore(f"first_slot{n}"))) for n in range(NG)]
        edges = ctx.enter_context(ExitStack())

        def eb(name, shape, dt=F32):
            return edges.enter_context(nc.sbuf_tensor(name, shape, dt))

        C.er = eb("er", [P, NT + 1, R * H])
        C.fidx = eb("fidx", [P, NPAIR], I32)
        C.srci = eb("srci", [P, NPAIR], I32)
        C.dstf = eb("dstf", [P, NPAIR])
        C.typf = eb("typf", [P, NPAIR])
        C.locf = eb("locf", [P, NPAIR])
        C.srcraw = eb("srcraw", [P, NB])
        C.tpi = eb("tpi", [1, NG * P], I32)
        setup_phase(nc, C, D)
        table_phase(nc, C, D)
        attention_phase(nc, C, D)
        norm_phase(nc, C, D)
        conv_phase(nc, C, D)
        edges.close()
        C.x2 = sb("x2", [P, NT, F])
        C.b2 = sb("b2_sb", [NE, F])
        C.b1t = sb("b1t", [P, NE, 4])
        C.gate = sb("gate", [P, 2, NT])
        C.slot = sb("slot", [P, 2, NT], I32)
        C.gm = sb("gate_by_expert", [P, NT, NE])
        C.valid = sb("valid_rows", [P, NT])
        C.expert = sb("expert_of_tile", [1, P], I32)
        C.used = sb("tiles_used", [1, 1], I32)
        gate_phase(nc, C, D)
        expert_phase(nc, C, D)
        output_phase(nc, C, D)


_INS = ["x", "src", "dst", "edge_type_8", "L0_gnn_conv_weights", "L0_gnn_attn_l", "L0_gnn_attn_r",
        "L0_gnn_h_bias", "L1_gnn_W_gc", "L1_gnn_b_gc", "L1_gnn_W_res", "L1_gnn_b_res", "L1_gnn_Wg",
        "L1_gnn_bg", "L1_gnn_w1", "L1_gnn_b1", "L1_gnn_w2", "L1_gnn_b2", "L1_gnn_gamma", "L1_gnn_beta"]
DBG = False


def kernel(**inputs):
    import numpy as _np
    import concourse.bacc as _bacc
    from concourse import mybir as _mybir
    from concourse.bass_utils import run_bass_kernel_spmd as _run

    nc = _bacc.Bacc("TRN2", target_bir_lowering=False, num_devices=1)
    arrays, args = {}, []
    for name in _INS:
        a = _np.ascontiguousarray(inputs[name])
        arrays[f"in_{name}"] = a
        args.append(nc.dram_tensor(f"in_{name}", a.shape, _mybir.dt.from_np(a.dtype), kind="ExternalInput").ap())
    args.append(nc.dram_tensor("out", (N, F), _mybir.dt.float32, kind="ExternalOutput").ap())
    args.append(nc.dram_tensor("dbg", (8, 128, 8192), _mybir.dt.float32, kind="ExternalOutput").ap() if DBG else None)
    gnn_program(nc, *args)
    r = _run(nc, [arrays], core_ids=[0])
    return r.results[0]["out"]
```

```python
from contextlib import ExitStack

import concourse.bass as bass
from concourse import mybir

ALU = mybir.AluOpType
ACT = mybir.ActivationFunctionType
AX = mybir.AxisListType
F32 = mybir.dt.float32
BF16 = mybir.dt.bfloat16
I32 = mybir.dt.int32
U32 = mybir.dt.uint32

P = 128
N = 3750
E = 120000
F = 256
R = 8
H = 4
HD = F // H
NT = -(-N // P)
NB = -(-E // P)
G = 4
CH = 24
MOSTPAIRS = (NB + NT - 1 + NT * (G - 1)) // G * G
NCH = -(-MOSTPAIRS // CH)
NPAIR = NCH * CH
NGR = CH // G
NG = -(-NPAIR // P)
NRG = -(-(NB + 1) // P)
ROWS = CH * H
FULL = E // P
TAIL = E - FULL * P
LAST = N - (NT - 1) * P
FW = F + H
GW = FW + 1
GS = 264
BIG = 1.0e30
APART = 2.0 ** 80
W = CH + 2
PAD_DST = 8191
PAD_SRC = 4095
NE = 64
HID = 512
CAP = 1024
XG = 4
NX = -(-((2 * N + NE * (P - 1)) // P) // XG) * XG

ZR = -(-NX // (NT // 2))
NBUF = ZR * (NT // 2)


class Chain:

    def __init__(self, eng, sem, base=0):
        self.eng, self.sem, self.base, self.n = eng, sem, base, 0

    def link(self, ins):
        self.n += 1
        ins.then_inc(self.sem, 1)
        self.eng.wait_ge(self.sem, self.base + self.n)


def col(ap, n):
    return ap.rearrange("p (m o) -> p m o", o=1).to_broadcast([ap.shape[0], ap.shape[1], n])


def clear(nc, sems):
    nc.clear_and_free_semaphores(sems)
    nc.all_engine_barrier(sem_only=True)


def setup_phase(nc, C, D):
    ctx, sems = ExitStack(), []
    with ctx:
        def sb(name, shape, dt=F32):
            return ctx.enter_context(nc.sbuf_tensor(name, shape, dt))

        def sem(name):
            sems.append(nc.alloc_semaphore(name))
            return sems[-1]

        raw = sb("raw", [P, 3, NRG, P], I32)
        rec = sb("rec", [P, NRG, 4, P])
        rawsrc = sb("rawsrc", [P, NRG, P])
        pairrec = sb("pairrec", [P, NG, 4, P])
        loc = sb("loc", [P, NG, P])
        limit = sb("limit", [P, NT + 1])
        under = sb("under", [P, 2, NT + 1, NRG])
        below = sb("below", [P, 2, NT + 1])
        icount = sb("icount", [P, NT], I32)
        firstb = sb("firstb", [P, NT + 1])
        endb = sb("endb", [P, NT])
        count = sb("count", [P, NT])
        offend = sb("offend", [P, NT])
        shift = sb("shift", [P, NT + 1])
        step = sb("step", [P, NT])
        ones_t = sb("ones_t", [P, NT])
        pid = sb("pid", [P, NG])
        ge = sb("ge", [P, NG, NT])
        gest = sb("gest", [P, NG, NT])
        tp = sb("tp", [P, NG])
        tbase = sb("tbase", [P, NG])
        blk = sb("blk", [P, NG])
        blki = sb("blki", [P, NG], I32)
        ps = ctx.enter_context(nc.psum_tensor("ps_setup", [P, 4, 512], F32))
        pcount = ctx.enter_context(nc.psum_tensor("pcount", [P, 512], F32))
        prow = ctx.enter_context(nc.psum_tensor("prow", [1, 3, 512], F32))

        filled = sem("pads_filled")
        loaded = sem("edges_loaded")
        xloaded = sem("x_loaded")
        consts = sem("consts_ready")
        dch = sem("dve_setup")
        recs_ready = sem("recs_ready")
        recs_stored = sem("recs_stored")
        below_ready = sem("below_ready")
        starts_ready = sem("starts_ready")
        blk_ready = sem("blk_ready")
        gathered = C.first_slots
        loc_ready = sem("loc_ready")
        turned = sem("turned")
        evacuated = sem("turned_evacuated")
        tp_turned = sem("tp_turned")
        ctx.callback(clear, nc, sems)
        block = ctx.enter_context(nc.Block())

        @block.sync
        def _(sp):
            sp.wait_ge(filled, 4)
            for k, a in enumerate((D.src, D.dst, D.typ)):
                whole = (FULL // P) * P
                sp.dma_start(raw[:, k, 0:FULL // P, :],
                             a[0:whole * P].rearrange("(g p e) -> p g e", p=P, e=P)).then_inc(loaded, 16)
                sp.dma_start(raw[0:FULL - whole, k, FULL // P, :],
                             a[whole * P:FULL * P].rearrange("(p e) -> p e", e=P)).then_inc(loaded, 16)
                sp.dma_start(raw[FULL - whole:FULL - whole + 1, k, FULL // P, 0:TAIL],
                             a[FULL * P:E].rearrange("(p e) -> p e", p=1)).then_inc(loaded, 16)
            sp.dma_start(C.x[:, 0:NT - 1, :],
                         D.x[0:(NT - 1) * P, :].rearrange("(t p) f -> p t f", p=P)).then_inc(xloaded, 16)
            sp.dma_start(C.x[0:LAST, NT - 1, :], D.x[(NT - 1) * P:N, :]).then_inc(xloaded, 16)
            sp.wait_ge(recs_ready, 1)
            sp.dma_start(D.rec.rearrange("(g p) f -> p g f", p=P),
                         rec[:, :, :, :].rearrange("p g k e -> p g (k e)")).then_inc(recs_stored, 16)
            sp.wait_ge(xloaded, 32)
            sp.wait_ge(loc_ready, NG)
            for k in range(2):
                sp.dma_start(C.w[:, k, :].rearrange("p (a d) -> p a d", d=HD),
                             D.conv[:, :, k * P:(k + 1) * P, :].rearrange("r h k d -> k (r h) d")
                             ).then_inc(C.w_loaded, 16)
            for k, a in enumerate((D.attl, D.attr)):
                flat = a.rearrange("r h d -> (r h d)").rearrange("(o f) -> o f", o=1)
                sp.dma_start(C.att[:, k, :], flat.to_broadcast([P, R * F])).then_inc(C.w_loaded, 16)

        @block.gpsimd
        def _(g):
            g.memset(raw[:, 0, :, :], PAD_SRC).then_inc(filled, 1)
            g.memset(raw[:, 1, :, :], PAD_DST).then_inc(filled, 1)
            g.memset(raw[:, 2, :, :], 0).then_inc(filled, 1)
            g.memset(C.x[:, NT - 1, :], 0.0).then_inc(filled, 1)
            g.iota(C.iota[:, :], [[1, P]], base=0, channel_multiplier=0,
                   allow_small_or_imprecise_dtypes=True).then_inc(consts, 1)
            g.iota(C.ioch[:, :], [[0, 1]], base=0, channel_multiplier=1,
                   allow_small_or_imprecise_dtypes=True).then_inc(consts, 1)
            g.iota(pid[:, :], [[P, NG]], base=0, channel_multiplier=1,
                   allow_small_or_imprecise_dtypes=True).then_inc(consts, 1)
            g.memset(C.ones[:, :], 1.0).then_inc(consts, 1)
            g.wait_ge(recs_stored, 16)
            g.wait_ge(blk_ready, 1)
            for k in range(NG):
                g.indirect_dma_start(pairrec[:, k, :, :].rearrange("p k e -> p (k e)"), None, D.rec,
                                     bass.IndirectOffsetOnAxis(ap=blki[:, k:k + 1], axis=0)
                                     ).then_inc(gathered[k].sem, 16)

        @block.vector
        def _(dve):
            v = nc.vector
            c = Chain(dve, dch)
            dve.wait_ge(consts, 4)
            c.link(v.tensor_scalar(C.ident[:, :], C.iota[:, :], C.ioch[:, 0:1], None, ALU.is_equal))
            c.link(v.memset(ones_t[:, :], 1.0))
            dve.wait_ge(loaded, 9 * 16)
            c.link(v.tensor_copy(rawsrc[:, :, :], raw[:, 0, :, :]))
            c.link(v.tensor_scalar(rec[:, :, 1, :], raw[:, 0, :, :], float(N - 1), None, ALU.min))
            c.link(v.tensor_copy(rec[:, :, 2, :], raw[:, 1, :, :]))
            c.link(v.tensor_copy(rec[:, :, 3, :], raw[:, 2, :, :]))
            c.link(v.scalar_tensor_tensor(rec[:, :, 0, :], rec[:, :, 1, :], float(R), rec[:, :, 3, :],
                                          ALU.mult, ALU.add))
            dve.sem_inc(recs_ready, 1)
            c.link(v.tensor_scalar(limit[:, :], C.iota[:, 0:NT + 1], float(P), None, ALU.mult))
            for j, e in enumerate((P - 1, 0)):
                c.link(v.tensor_tensor(under[:, j, :, :],
                                       rec[:, :, 2, e:e + 1].rearrange("p g (o e) -> p o (g e)", o=1)
                                       .to_broadcast([P, NT + 1, NRG]), col(limit[:, :], NRG), ALU.is_lt))
            c.link(v.tensor_reduce(below[:, :, :], under[:, :, :, :], AX.X, ALU.add))
            dve.sem_inc(below_ready, 1)
            dve.wait_ge(starts_ready, 1)
            c.link(v.tensor_copy(firstb[:, :], pcount[:, 0:NT + 1]))
            c.link(v.tensor_copy(endb[:, :], pcount[:, NT + 2:2 * NT + 2]))
            c.link(v.tensor_tensor(count[:, :], endb[:, :], firstb[:, 0:NT], ALU.subtract))
            c.link(v.tensor_scalar(count[:, :], count[:, :], float(G - 1), None, ALU.add))
            c.link(v.tensor_copy(icount[:, :], count[:, :]))
            c.link(v.tensor_scalar(icount[:, :], icount[:, :], -G, None, ALU.bitwise_and))
            c.link(v.tensor_copy(count[:, :], icount[:, :]))
            c.link(v.tensor_tensor_scan(offend[:, :], ones_t[:, :], count[:, :], 0.0, ALU.mult, ALU.add))
            c.link(v.tensor_copy(shift[:, 0:1], firstb[:, 0:1]))
            c.link(v.tensor_tensor(shift[:, 1:NT + 1], firstb[:, 1:NT + 1], offend[:, :], ALU.subtract))
            c.link(v.tensor_tensor(step[:, :], shift[:, 1:NT + 1], shift[:, 0:NT], ALU.subtract))
            offb = offend[:, :].rearrange("p (o t) -> p o t", o=1).to_broadcast([P, NG, NT])
            stepb = step[:, :].rearrange("p (o t) -> p o t", o=1).to_broadcast([P, NG, NT])
            c.link(v.tensor_tensor(ge[:, :, :], offb, col(pid[:, :], NT), ALU.is_le))
            c.link(v.tensor_tensor(gest[:, :, :], ge[:, :, :], stepb, ALU.mult))
            c.link(v.tensor_reduce(tp[:, :], ge[:, :, :], AX.X, ALU.add))
            c.link(v.tensor_reduce(blk[:, :], gest[:, :, :], AX.X, ALU.add))
            c.link(v.tensor_tensor(blk[:, :], blk[:, :], pid[:, :], ALU.add))
            c.link(v.tensor_scalar(blk[:, :], blk[:, :], float(NB), 0.0, ALU.min, ALU.max))
            c.link(v.tensor_scalar(tbase[:, :], tp[:, :], float(P), None, ALU.mult))
            v.tensor_copy(blki[:, :], blk[:, :]).then_inc(blk_ready, 1)
            for k in range(NG):
                dve.wait_ge(gathered[k].sem, gathered[k].base + 16)
                v.tensor_scalar(loc[:, k, :], pairrec[:, k, 2, :], tbase[:, k:k + 1], None,
                                ALU.subtract).then_inc(loc_ready, 1)
            dests = [C.fidx, C.srci, C.dstf, C.typf, C.locf, C.srcraw]
            n = 0
            for k in range(NG):
                for j, d in enumerate(dests):
                    w = min(P, (NB if j == 5 else NPAIR) - k * P)
                    if w <= 0:
                        continue
                    dve.wait_ge(turned, n + 1)
                    v.tensor_scalar(d[:, k * P:k * P + w], ps[:, n % 4, 0:w], APART if j == 2 else 1.0, None,
                                    ALU.mult).then_inc(evacuated, 1)
                    n += 1
            dve.wait_ge(tp_turned, 1)
            v.tensor_copy(C.tpi[:, 0:NG * P], prow[0:1, :, :].rearrange("o a b -> o (a b)")[:, 0:NG * P]
                          ).then_inc(evacuated, 1)

        @block.tensor
        def _(pe):
            pe.wait_ge(below_ready, 1)
            nc.tensor.matmul(pcount[:, 0:2 * NT + 2], C.ones[:, :],
                             below[:, :, :].rearrange("p j t -> p (j t)"), start=True,
                             stop=True).then_inc(starts_ready, 1)
            n = 0
            for k in range(NG):
                pe.wait_ge(loc_ready, k + 1)
                for j, a in enumerate((pairrec[:, k, 0, :], pairrec[:, k, 1, :], pairrec[:, k, 2, :],
                                       pairrec[:, k, 3, :], loc[:, k, :], rawsrc[:, k % NRG, :])):
                    if j == 5 and k >= NRG:
                        continue
                    if n >= 4:
                        pe.wait_ge(evacuated, n - 3)
                    nc.tensor.transpose(ps[:, n % 4, 0:P], a, C.ident[:, :]).then_inc(turned, 1)
                    n += 1
            for k in range(NG):
                last = nc.tensor.matmul(prow[0:1, k // 4, (k % 4) * P:(k % 4 + 1) * P], tp[:, k:k + 1],
                                        C.ident[:, :], start=True, stop=True)
            last.then_inc(tp_turned, 1)

    for slot in gathered:
        slot.base += 16


HB = -(-NB // NT)


def table_phase(nc, C, D):
    ctx, sems = ExitStack(), []
    with ctx:
        def sb(name, shape, dt=F32):
            return ctx.enter_context(nc.sbuf_tensor(name, shape, dt))

        def sem(name):
            sems.append(nc.alloc_semaphore(name))
            return sems[-1]

        w, att = C.w, C.att
        prod = sb("att_prod", [P, R * F])
        watt = sb("watt", [P, 2, 2, R * H])
        xin = [sb(f"xin{u}", [P, F]) for u in range(2)]
        xt = [sb(f"xt{u}", [P, 2, P]) for u in range(2)]
        row = [sb(f"trow{u}", [P, R, FW]) for u in range(2)]
        low = sb("src_low", [P, NT * HB])
        high = sb("src_high", [P, NT * HB])
        isrc = sb("src_int", [P, NT * HB], I32)
        ihalf = sb("src_half", [P, NT * HB], I32)
        onelow = [sb(f"onelow{u}", [P, HB, P], BF16) for u in range(2)]
        onehigh = [sb(f"onehigh{u}", [P, HB, NT], BF16) for u in range(2)]
        zero = sb("zero_row", [P, F])
        zerob = sb("zero_b", [P, P], BF16)
        pfeat = ctx.enter_context(nc.psum_tensor("pfeat", [P, 4, 512], F32))
        px = ctx.enter_context(nc.psum_tensor("px", [P, 512], F32))
        pel = ctx.enter_context(nc.psum_tensor("pel", [P, 512], F32))
        phist = ctx.enter_context(nc.psum_tensor("phist", [P, 512], F32))

        dch = sem("dve_table")
        zeros = sem("zeros_ready")
        buf_zeroed = sem("buf_zeroed")
        prep = sem("prep_done")
        xin_ready = sem("xin_ready")
        x_turned = sem("x_turned")
        xt_ready = sem("xt_ready")
        hot_ready = sem("hot_ready")
        hot_free = sem("hot_free")
        feat_ready = sem("feat_ready")
        feat_free = sem("feat_free")
        el_ready = sem("el_ready")
        row_ready = sem("row_ready")
        row_free = sem("row_free")
        row_stored = [sem(f"row_stored{u}") for u in range(2)]
        hist_ready = sem("hist_ready")
        ctx.callback(clear, nc, sems)
        block = ctx.enter_context(nc.Block())

        @block.sync
        def _(sp):
            with sp.Fori(0, NT // 2) as i:
                for u in range(2):
                    sp.wait_ge(row_ready, 2 * i + u + 2)
                    sp.dma_start(D.tab.rearrange("(t p) f -> t p f", p=P)[bass.ds(2 * i + u, 1), :, :]
                                 .rearrange("o p f -> (o p) f"),
                                 row[u][:, :, :].rearrange("p r f -> p (r f)")).then_inc(row_stored[u], 16)
                    sp.wait_ge(row_stored[u], 16 * i + 16)
                    sp.sem_inc(row_free, 1)

        @block.scalar
        def _(act):
            act.sem_inc(row_free, 2)
            act.sem_inc(row_ready, 1)
            act.sem_inc(feat_free, 4)
            act.wait_ge(zeros, 1)
            with act.Fori(0, NT // 2) as i:
                act.dma_start(D.buf.rearrange("(t p m) f -> t p m f", p=P, m=ZR)[bass.ds(i, 1), :, :, :]
                              .rearrange("o p m f -> p (o m) f"),
                              zero[:, :].rearrange("p (o f) -> p o f", o=1).to_broadcast([P, ZR, F])
                              ).then_inc(buf_zeroed, 16)
                for u in range(2):
                    act.wait_ge(row_free, 2 * i + u + 1)
                    for q in range(4):
                        act.wait_ge(feat_ready, 4 * (2 * i + u) + q + 1)
                        nc.scalar.activation(row[u][:, 2 * q:2 * q + 2, 0:F],
                                             pfeat[:, q, :].rearrange("p (r f) -> p r f", r=2),
                                             ACT.Copy).then_inc(feat_free, 1)
                    act.wait_ge(el_ready, 2 * i + u + 3)
                    nc.scalar.activation(row[u][:, :, F:FW], pel[:, 0:R * H].rearrange("p (r h) -> p r h", h=H),
                                         ACT.Copy)
                    nc.scalar.activation(C.er[:, bass.ds(2 * i + u, 1), :],
                                         pel[:, R * H:2 * R * H].rearrange("p (o r) -> p o r", o=1),
                                         ACT.Copy).then_inc(row_ready, 1)
            act.wait_ge(hist_ready, 1)
            nc.scalar.activation(C.dego[:, :], phist[:, 0:NT], ACT.Copy)
            act.wait_ge(buf_zeroed, 16 * (NT // 2))

        @block.vector
        def _(dve):
            v = nc.vector
            c = Chain(dve, dch)
            v.memset(zero[:, :], 0.0).then_inc(zeros, 1)
            v.memset(C.er[:, NT, :], 0.0)
            c.link(v.memset(zerob[:, :], 0.0))
            for u in range(2):
                v.tensor_copy(xin[u][:, :], C.x[:, u, :]).then_inc(xin_ready, 1)
            c.link(v.memset(low[:, :], float(PAD_SRC)))
            c.link(v.tensor_copy(low[:, 0:NB], C.srcraw[:, :]))
            c.link(v.tensor_copy(isrc[:, :], low[:, :]))
            c.link(v.tensor_scalar(ihalf[:, :], isrc[:, :], P - 1, None, ALU.bitwise_and))
            c.link(v.tensor_copy(low[:, :], ihalf[:, :]))
            c.link(v.tensor_scalar(ihalf[:, :], isrc[:, :], 7, None, ALU.arith_shift_right))
            c.link(v.tensor_copy(high[:, :], ihalf[:, :]))
            dve.wait_ge(C.w_loaded, 64)
            for k in range(2):
                for j in range(2):
                    c.link(v.tensor_tensor(prod[:, :], w[:, k, :], att[:, j, :], ALU.mult))
                    c.link(v.tensor_reduce(watt[:, k, j, :], prod[:, :].rearrange("p (a d) -> p a d", d=HD),
                                           AX.X, ALU.add))
            dve.sem_inc(prep, 1)

            def tile(i, u, more):
                dve.wait_ge(x_turned, 2 * i + u + 1)
                dve.wait_ge(el_ready, 2 * i + u + 1)
                v.tensor_copy(xt[u][:, :, :], px[:, 0:F].rearrange("p (c n) -> p c n", c=2)
                              ).then_inc(xt_ready, 1)
                if more:
                    v.tensor_copy(xin[u][:, :], C.x[:, bass.ds(2 * i + u + 2, 1), :]
                                  .rearrange("p o f -> p (o f)")).then_inc(xin_ready, 1)
                dve.wait_ge(hot_free, 2 * i + u + 1)
                at = bass.ds((2 * i + u) * HB, HB)
                v.tensor_tensor(onelow[u][:, :, :], col(low[:, at], P),
                                C.iota[:, :].rearrange("p (o f) -> p o f", o=1).to_broadcast([P, HB, P]),
                                ALU.is_equal)
                v.tensor_tensor(onehigh[u][:, :, :], col(high[:, at], NT),
                                C.iota[:, 0:NT].rearrange("p (o f) -> p o f", o=1).to_broadcast([P, HB, NT]),
                                ALU.is_equal).then_inc(hot_ready, 1)

            with dve.Fori(0, NT // 2 - 1) as i:
                for u in range(2):
                    tile(i, u, True)
            for u in range(2):
                tile(NT // 2 - 1, u, False)

        @block.tensor
        def _(pe):
            pe.wait_ge(prep, 1)
            pe.sem_inc(hot_free, 2)
            pe.sem_inc(el_ready, 2)
            nc.tensor.matmul(phist[:, 0:NT], zerob[:, :], zerob[:, 0:NT], start=True, stop=False)

            def turn(t, u):
                pe.wait_ge(xin_ready, t + 1)
                for k in range(2):
                    last = nc.tensor.transpose(px[:, k * P:(k + 1) * P], xin[u][:, k * P:(k + 1) * P],
                                               C.ident[:, :])
                last.then_inc(x_turned, 1)

            def tile(t, u, more):
                pe.wait_ge(xt_ready, t + 1)
                for q in range(4):
                    pe.wait_ge(feat_free, 4 * t + q + 1)
                    for k in range(2):
                        last = nc.tensor.matmul(pfeat[:, q, :], xt[u][:, k, :], w[:, k, q * 512:(q + 1) * 512],
                                                start=(k == 0), stop=(k == 1))
                    last.then_inc(feat_ready, 1)
                    if more and q == 2:
                        turn(t + 1, 1 - u)
                pe.wait_ge(row_ready, t + 1)
                for k in range(2):
                    last = nc.tensor.matmul(pel[:, 0:2 * R * H], xt[u][:, k, :],
                                            watt[:, k, :, :].rearrange("p l a -> p (l a)"),
                                            start=(k == 0), stop=(k == 1))
                last.then_inc(el_ready, 1)
                pe.wait_ge(hot_ready, t + 1)
                for b in range(HB):
                    last = nc.tensor.matmul(phist[:, 0:NT], onelow[u][:, b, :], onehigh[u][:, b, :],
                                            start=False, stop=False)
                last.then_inc(hot_free, 1)

            turn(0, 0)
            with pe.Fori(0, NT // 2 - 1) as i:
                for u in range(2):
                    tile(2 * i + u, u, True)
            for u in range(2):
                tile(NT - 2 + u, u, u == 0)
            nc.tensor.matmul(phist[:, 0:NT], zerob[:, :], zerob[:, 0:NT], start=False,
                             stop=True).then_inc(hist_ready, 1)


def attention_phase(nc, C, D):
    ctx, sems = ExitStack(), []
    with ctx:
        def sb(name, shape, dt=F32):
            return ctx.enter_context(nc.sbuf_tensor(name, shape, dt))

        def sem(name):
            sems.append(nc.alloc_semaphore(name))
            return sems[-1]

        gat = [sb(f"gat{u}", [P, CH, GS]) for u in range(2)]
        hot = [sb(f"hot{u}", [P, CH, P]) for u in range(2)]
        hotb = sb("hotb", [P, CH, P], BF16)
        hott = sb("hott", [P, CH, P])
        identb = sb("identb", [P, P], BF16)
        bias = sb("hbias", [P, F])
        idle = sb("idle_in", [P, 512 - GS], BF16)
        gidx = [sb(f"gidx{u}", [P, CH], I32) for u in range(2)]
        tmask = sb("tmask", [P, CH, R])
        ertmp = sb("ertmp", [P, CH, R, H])
        ersel = [sb(f"ersel{u}", [P, H, CH]) for u in range(2)]
        sc = sb("scores", [P, H, CH])
        d4 = sb("dst4", [P, H, CH])
        sd = sb("sdrows", [ROWS, 2, P])
        neg = sb("neg", [ROWS, P + 1])
        fwd = sb("fwd", [ROWS, P])
        bwd = sb("bwd", [ROWS, P])
        mx = sb("mx", [ROWS, P])
        rows = sb("rows", [1, 4, H, W])
        link = sb("link", [1, 2, H, W])
        af = sb("af", [1, H, W])
        ab = sb("ab", [1, H, W])
        cof = sb("cof", [1, H, W])
        cob = sb("cob", [1, H, W])
        carry = sb("carry", [1, 2, H * CH])
        fac = sb("fac", [1, 4, H])
        hot0 = sb("hotfirst", [1, 2, P])
        ex = sb("ex", [P, H, CH])
        exin = sb("exin", [P, H, CH])
        pt = ctx.enter_context(nc.psum_tensor("pt", [P, 2, 1024], BF16))
        per = ctx.enter_context(nc.psum_tensor("per", [P, 2, 512], F32))
        psd = ctx.enter_context(nc.psum_tensor("psd", [P, 512], F32))
        prow = ctx.enter_context(nc.psum_tensor("prow2", [P, 512], F32))
        pacc = ctx.enter_context(nc.psum_tensor("pacc", [P, 2, 512], F32))

        gathered1 = [C.slots[u * CH:(u + 1) * CH] for u in range(2)]
        gathered = sem("chunk_gathered")
        idx_ready = sem("idx_ready")
        hot_ready = sem("hot_ready2")
        turned = sem("hot_turned")
        hot_long = sem("hot_long")
        scaled_act = sem("scaled_act")
        copied = sem("hott_copied")
        er_ready = sem("er_ready")
        ers_ready = sem("ers_ready")
        s_ready = sem("s_ready")
        sd_turned = sem("sd_turned")
        sd_copied = sem("sd_copied")
        fb_ready = sem("fb_ready")
        rows_ready = sem("rows_ready")
        rows_copied = sem("rows_copied")
        carries_ready = sem("carries_ready")
        cols_ready = sem("cols_ready")
        fac_ready = sem("fac_ready")
        facm_ready = sem("facm_ready")
        m_ready = sem("m_ready")
        mt_ready = sem("mt_ready")
        exin_ready = sem("exin_ready")
        ex_ready = sem("ex_ready")
        scaled = sem("scaled")
        mm_done = sem("mm_done")
        acc_done = sem("acc_done")
        sc_ready = sem("sc_ready")
        ch0 = sem("dve_attn0")
        ch1 = sem("dve_attn1")
        ch2 = sem("dve_attn2")
        ch3 = sem("dve_attn3")
        bias_loaded = sem("hbias_loaded")
        ctx.callback(clear, nc, sems)
        block = ctx.enter_context(nc.Block())

        @block.gpsimd
        def _(g):
            with g.Fori(0, NCH // 2) as i:
                for u in range(2):
                    k = 2 * i + u
                    g.wait_ge(mm_done, NGR * k + 2)
                    g.tensor_copy(gidx[u][:, :], C.fidx[:, bass.ds(k * CH, CH)]).then_inc(idx_ready, 1)
                    g.wait_ge(idx_ready, k + 1)
                    for b in range(CH):
                        if b % (2 * G) == 0:
                            g.wait_ge(mm_done, NGR * k + b // G + 2)
                            g.nop(nofuse=True)
                        g.indirect_dma_start(gat[u][:, b, 0:FW], None, D.tab.rearrange("n (r f) -> (n r) f", f=FW),
                                             bass.IndirectOffsetOnAxis(ap=gidx[u][:, b:b + 1], axis=0)
                                             ).then_inc(gathered1[u][b].sem, 16)

        @block.sync
        def _(sp):
            sp.dma_start(bias[:, :], D.hbias.rearrange("(o f) -> o f", o=1).to_broadcast([P, F])
                         ).then_inc(bias_loaded, 16)
            with sp.Fori(0, NCH // 2) as i:
                for u in range(2):
                    for b in range(CH):
                        sp.wait_ge(gathered1[u][b].sem, gathered1[u][b].base + 16 * i + 16)
                    sp.sem_inc(gathered, 1)

        @block.scalar
        def _(act):
            a = nc.scalar

            def copy(k, u, n):
                act.wait_ge(turned, NGR * k + n + 1)
                a.activation(hott[:, G * n:G * n + G, :], pt[:, n % 2, 0:G * P].rearrange("p (b e) -> p b e", e=P),
                             ACT.Copy).then_inc(copied, 1)
                a.activation(hot[u][:, G * n:G * n + G, :], hotb[:, G * n:G * n + G, :], ACT.Copy
                             ).then_inc(hot_long, 1)

            def scale(u, n):
                for j in range(G * n + G - 1, G * n + G):
                    for h in range(H):
                        row = gat[u][:, j, h * HD:(h + 1) * HD]
                        last = a.activation(row, row, ACT.Copy, scale=ex[:, h, j:j + 1])
                last.then_inc(scaled_act, 1)

            def start(k):
                act.wait_ge(sd_turned, k + 1)
                a.activation(sd[:, :, :], psd[0:ROWS, 0:2 * P].rearrange("p (a e) -> p a e", e=P),
                             ACT.Copy).then_inc(sd_copied, 1)
                act.wait_ge(rows_ready, k + 1)
                a.activation(rows[:, :, :, 1:CH + 1].rearrange("o a h b -> o (a h) b"),
                             prow[0:1, 0:4 * ROWS].rearrange("o (a b) -> o a b", b=CH), ACT.Copy
                             ).then_inc(rows_copied, 1)

            def chunk(k, u, more):
                if more:
                    act.wait_ge(er_ready, k + 1)
                    copy(k + 1, 1 - u, 0)
                    copy(k + 1, 1 - u, 1)
                act.wait_ge(fac_ready, k + 1)
                a.activation(fac[:, 1, :], fac[:, 0, :], ACT.Exp).then_inc(facm_ready, 1)
                if more:
                    copy(k + 1, 1 - u, 2)
                    copy(k + 1, 1 - u, 3)
                act.wait_ge(exin_ready, k + 1)
                a.activation(ex[:, :, :], exin[:, :, :], ACT.Exp).then_inc(ex_ready, 1)
                a.activation(gat[u][:, :, F:FW].rearrange("p b h -> p h b"), exin[:, :, :], ACT.Exp)
                act.wait_ge(ex_ready, k + 1)
                for n in range(NGR):
                    scale(u, n)
                    if more and n < 2:
                        copy(k + 1, 1 - u, n + 4)
                if more:
                    start(k + 1)

            act.sem_inc(hot_long, NGR)
            act.wait_ge(er_ready, 1)
            for n in range(NGR):
                copy(0, 0, n)
            start(0)
            with act.Fori(0, NCH // 2 - 1) as i:
                for u in range(2):
                    chunk(2 * i + u, u, True)
            chunk(NCH - 2, 0, True)
            chunk(NCH - 1, 1, False)

        @block.vector
        def _(dve):
            v = nc.vector
            c0 = Chain(dve, ch0)
            for u in range(2):
                c0.link(v.memset(gat[u][:, :, FW:GW], 1.0))
            c0.link(v.memset(C.acc[:, :, :], 0.0))
            c0.link(v.memset(neg[:, 0:1], 0.0))
            c0.link(v.memset(neg[:, P:P + 1], 0.0))
            c0.link(v.memset(rows[:, :, :, :], -BIG))
            c0.link(v.memset(link[:, :, :, :], -BIG))
            c0.link(v.memset(af[:, :, :], -BIG))
            c0.link(v.memset(ab[:, :, :], -BIG))
            c0.link(v.memset(fac[:, 3, :], 1.0))
            c0.link(v.tensor_copy(identb[:, :], C.ident[:, :]))
            c0.link(v.memset(idle[:, :], 0.0))
            dve.sem_inc(ers_ready, 1)
            dve.sem_inc(acc_done, 2)
            N1, N2, N3 = 3, 11, 4

            def part(tab, k, n0, n):
                if isinstance(k, int):
                    return tab[:, k * CH + n0:k * CH + n0 + n]
                return tab[:, bass.ds(k * CH + n0, n)]

            def one_hot(k, n):
                dve.wait_ge(hot_long, NGR * k + n + 1)
                v.tensor_tensor(hotb[:, G * n:G * n + G, :], col(part(C.locf, k, G * n, G), P),
                                across(C.iota[:, :], G), ALU.is_equal).then_inc(hot_ready, 1)

            def edge_er(k, u):
                c = Chain(dve, ch1, k * N1)
                c.link(v.tensor_tensor(tmask[:, :, :], col(part(C.typf, k, 0, CH), R),
                                       across(C.iota[:, 0:R], CH), ALU.is_equal))
                dve.wait_ge(er_ready, k + 2)
                for n, (b, m) in enumerate(((0, 16), (16, CH - 16))):
                    c.link(v.tensor_tensor(ertmp[:, b:b + m, :, :],
                                           per[:, n, 0:m * R * H].rearrange("p (b r h) -> p b r h", r=R, h=H),
                                           tmask[:, b:b + m, :].rearrange("p b (r o) -> p b r o", o=1)
                                           .to_broadcast([P, m, R, H]), ALU.mult))
                assert c.n == N1
                v.tensor_reduce(ersel[u][:, :, :].rearrange("p h b -> p b h"),
                                ertmp[:, :, :, :].rearrange("p b r h -> p b h r"), AX.X, ALU.add
                                ).then_inc(ers_ready, 1)

            def scores(k, u):
                c = Chain(dve, ch3, k * N3)
                dve.wait_ge(ers_ready, k + 2)
                dve.wait_ge(gathered, k + 1)
                c.link(v.tensor_tensor(sc[:, :, :].rearrange("p h b -> p b h"), gat[u][:, :, F:FW],
                                       ersel[u][:, :, :].rearrange("p h b -> p b h"), ALU.add))
                v.tensor_copy(d4[:, :, :], part(C.dstf, k, 0, CH).rearrange("p (o b) -> p o b", o=1)
                              .to_broadcast([P, H, CH]))
                v.scalar_tensor_tensor(sc[:, :, :], sc[:, :, :], 0.2, sc[:, :, :], ALU.mult, ALU.max
                                       ).then_inc(s_ready, 1)
                c.link(v.tensor_scalar(hot0[:, 0, :], C.iota[0:1, :], part(C.locf[0:1, :], k, 0, 1), None,
                                       ALU.is_equal))
                c.link(v.tensor_scalar(hot0[:, 1, :], hot0[:, 0, :], -1.0, 1.0, ALU.mult, ALU.add))
                return c

            def scans(k, c):
                dve.wait_ge(sd_copied, k + 1)
                c.link(v.tensor_tensor(neg[:, 1:P], sd[:, 1, 0:P - 1], sd[:, 1, 1:P], ALU.subtract))
                v.tensor_tensor_scan(fwd[:, :], neg[:, 0:P], sd[:, 0, :], -BIG, ALU.add, ALU.max)
                v.tensor_tensor_scan(bwd[:, ::-1], neg[:, P:0:-1], sd[:, 0, ::-1], -BIG, ALU.add,
                                     ALU.max).then_inc(fb_ready, 1)
                assert c.n == N3

            def chunk(k, u, more, more2):
                c = Chain(dve, ch2, k * N2)

                def scale(n):
                    b, m = G * n, G - 1
                    gv = gat[u][:, b:b + m, 0:F].rearrange("p b (h d) -> p b h d", h=H)
                    v.tensor_tensor(gv, gv, ex[:, :, b:b + m].rearrange("p h (b o) -> p b h o", o=1)
                                    .to_broadcast([P, m, H, HD]), ALU.mult).then_inc(scaled, 1)

                def add(n):
                    t = dve.value_load(part(C.tpi, k, G * n, 1), min_val=0, max_val=NT)
                    dve.wait_ge(mm_done, NGR * (k + 2) + n + 1)
                    if n:
                        dve.wait_ge(acc_done, NGR * k + n + 2)
                    tile = C.acc[:, bass.ds(t, 1), :].rearrange("p o f -> p (o f)")
                    v.tensor_tensor(tile, tile, pacc[:, n % 2, 0:GW], ALU.add).then_inc(acc_done, 1)

                dve.wait_ge(rows_copied, k + 1)
                lf, ff, df, dl = (rows[:, j, :, :] for j in range(4))
                inner = slice(1, CH + 1)
                c.link(v.tensor_tensor(link[:, 0, :, inner], df[:, :, inner], dl[:, :, 0:CH], ALU.is_equal))
                c.link(v.tensor_tensor(link[:, 1, :, inner], df[:, :, inner], dl[:, :, inner], ALU.is_equal))
                c.link(v.tensor_copy(fac[:, 2, :], link[:, 0, :, 1:2].rearrange("o h b -> o (h b)")))
                both = link[:, :, :, inner].rearrange("o a h b -> o (a h) b")
                c.link(v.tensor_scalar(both, both, 1.0, BIG, ALU.subtract, ALU.mult))
                v.tensor_tensor(af[:, :, inner], link[:, 0, :, inner], link[:, 1, :, inner], ALU.add)
                c.link(v.tensor_tensor(ab[:, :, inner], link[:, 0, :, 2:W], link[:, 1, :, inner], ALU.add))

                def flat(t):
                    return t.rearrange("o h b -> o (h b)")

                v.tensor_tensor_scan(flat(cof[:, :, :]), flat(af[:, :, :]), flat(lf), -BIG, ALU.add, ALU.max)
                c.link(v.tensor_tensor_scan(flat(cob[:, :, :])[:, ::-1], flat(ab[:, :, :])[:, ::-1],
                                            flat(ff)[:, ::-1], -BIG, ALU.add, ALU.max))
                cv = carry[:, :, :].rearrange("o a (h b) -> o a h b", h=H)
                v.tensor_tensor(cv[:, 0, :, :], cof[:, :, 0:CH], link[:, 0, :, inner], ALU.add)
                v.tensor_tensor(cv[:, 1, :, :], cob[:, :, 2:W], link[:, 0, :, 2:W], ALU.add
                                ).then_inc(carries_ready, 1)
                c.link(v.tensor_tensor(fac[:, 0, :].rearrange("o (h b) -> o h b", b=1), lf[:, :, 0:1],
                                       cob[:, :, 1:2], ALU.subtract))
                c.link(v.scalar_tensor_tensor(fac[:, 0, :], fac[:, 0, :], 0.0, fac[:, 2, :], ALU.min, ALU.mult))
                v.tensor_copy(lf[:, :, 0:1], cof[:, :, CH:CH + 1]).then_inc(fac_ready, 1)
                v.tensor_copy(dl[:, :, 0:1], dl[:, :, CH:CH + 1])
                if more:
                    one_hot(k + 1, 2)
                    one_hot(k + 1, 3)
                dve.wait_ge(cols_ready, k + 1)
                v.tensor_tensor_scan(fwd[:, :], neg[:, 0:P], sd[:, 0, :], psd[0:ROWS, 384:385], ALU.add, ALU.max)
                c.link(v.tensor_tensor_scan(bwd[:, ::-1], neg[:, P:0:-1], sd[:, 0, ::-1],
                                            psd[0:ROWS, 385:386], ALU.add, ALU.max))
                v.tensor_tensor(mx[:, :], fwd[:, :], bwd[:, :], ALU.max).then_inc(m_ready, 1)
                if more:
                    one_hot(k + 1, 4)
                dve.wait_ge(mt_ready, k + 1)
                v.tensor_tensor(exin[:, :, :], sc[:, :, :],
                                psd[:, 256:256 + ROWS].rearrange("p (h b) -> p h b", h=H), ALU.subtract
                                ).then_inc(exin_ready, 1)
                if more:
                    one_hot(k + 1, 5)
                dve.wait_ge(ex_ready, k + 1)
                scale(0)
                t0 = dve.value_load(part(C.tpi, k, 0, 1), min_val=0, max_val=NT)
                dve.wait_ge(sc_ready, k + 1)
                dve.wait_ge(acc_done, NGR * k + 2)
                tile = C.acc[:, bass.ds(t0, 1), :].rearrange("p o f -> p (o f)")
                fv = prow[:, 400:400 + H]
                c.link(v.tensor_tensor(tile[:, 0:F].rearrange("p (h d) -> p h d", h=H),
                                       tile[:, 0:F].rearrange("p (h d) -> p h d", h=H), col(fv, HD), ALU.mult))
                c.link(v.tensor_tensor(tile[:, F:FW], tile[:, F:FW], fv, ALU.mult))
                assert c.n == N2, c.n

                scale(1)
                for n in range(NGR - 2):
                    scale(n + 2)
                    if more and n == NGR - 3:
                        c3 = scores(k + 1, 1 - u)
                    add(n)
                    if more and n == 1:
                        edge_er(k + 1, 1 - u)
                if more2:
                    one_hot(k + 2, 0)
                add(NGR - 2)
                if more:
                    scans(k + 1, c3)
                if more2:
                    one_hot(k + 2, 1)
                add(NGR - 1)

            for n in range(NGR):
                one_hot(0, n)
            edge_er(0, 0)
            dve.wait_ge(bias_loaded, 16)
            c0.link(v.tensor_tensor(C.x[:, :, :], C.x[:, :, :], across(bias[:, :], NT), ALU.add))
            scans(0, scores(0, 0))
            one_hot(1, 0)
            one_hot(1, 1)
            with dve.Fori(0, NCH // 2 - 1) as i:
                for u in range(2):
                    chunk(2 * i + u, u, True, True)
            chunk(NCH - 2, 0, True, False)
            chunk(NCH - 1, 1, False, False)

        @block.tensor
        def _(pe):
            t_ = nc.tensor
            pe.sem_inc(er_ready, 1)
            pe.sem_inc(mm_done, 2 * NGR)

            def turn(k, n):
                pe.wait_ge(hot_ready, NGR * k + n + 1)
                if n >= 2:
                    pe.wait_ge(copied, NGR * k + n - 1)
                for j in range(G):
                    last = t_.transpose(pt[:, n % 2, j * P:(j + 1) * P], hotb[:, G * n + j, :], identb[:, :])
                last.then_inc(turned, 1)

            def pick_er(k, n):
                at = k * CH + G * n
                t = pe.value_load(C.tpi[0:1, at:at + 1] if isinstance(k, int) else C.tpi[0:1, bass.ds(at, 1)],
                                  min_val=0, max_val=NT)
                pe.wait_ge(copied, NGR * k + n + 1)
                for j in range(G * n, G * n + G):
                    last = t_.matmul(per[:, j // 16, (j % 16) * R * H:(j % 16 + 1) * R * H], hott[:, j, :],
                                     C.er[:, bass.ds(t, 1), :].rearrange("p o r -> p (o r)"),
                                     start=True, stop=True)
                if n == NGR - 1:
                    last.then_inc(er_ready, 1)

            def turn_scores(k):
                pe.wait_ge(s_ready, k + 1)
                t_.transpose(psd[0:ROWS, 0:P], sc[:, :, :].rearrange("p h b -> p (h b)"), C.ident[:, :])
                t_.transpose(psd[0:ROWS, P:2 * P], d4[:, :, :].rearrange("p h b -> p (h b)"),
                             C.ident[:, :]).then_inc(sd_turned, 1)

            def row_ends(k):
                pe.wait_ge(fb_ready, k + 1)
                for j, a in enumerate((fwd[:, P - 1:P], bwd[:, 0:1], sd[:, 1, 0:1], sd[:, 1, P - 1:P])):
                    last = t_.matmul(prow[0:1, j * ROWS:(j + 1) * ROWS], a, C.ident[0:ROWS, 0:ROWS],
                                     start=True, stop=True)
                last.then_inc(rows_ready, 1)

            def stay_warm(n):
                for _ in range(n):
                    t_.matmul(pacc[:, 0, GS:512], identb[:, :], idle[:, :], start=True, stop=True)

            def sums(k, u, n):
                pe.wait_ge(scaled, NGR * k + n + 1)
                pe.wait_ge(scaled_act, NGR * k + n + 1)
                pe.wait_ge(acc_done, NGR * k + n + 1)
                for j in range(G):
                    last = t_.matmul(pacc[:, n % 2, 0:GW], hot[u][:, G * n + j, :],
                                     gat[u][:, G * n + j, 0:GW], start=(j == 0), stop=(j == G - 1))
                last.then_inc(mm_done, 1)

            def chunk(k, u, more):
                pe.wait_ge(acc_done, NGR * k + 1)
                stay_warm(0)
                if more:
                    turn(k + 1, 0)
                    turn(k + 1, 1)
                    pe.wait_ge(ers_ready, k + 2)
                    pick_er(k + 1, 0)
                    pick_er(k + 1, 1)
                stay_warm(12)
                pe.wait_ge(carries_ready, k + 1)
                for j in range(2):
                    last = t_.matmul(psd[0:ROWS, 384 + j:385 + j], carry[:, j, :], C.ones[0:1, 0:1],
                                     start=True, stop=True)
                last.then_inc(cols_ready, 1)
                if more:
                    turn(k + 1, 2)
                stay_warm(4)
                pe.wait_ge(facm_ready, k + 1)
                t_.matmul(prow[:, 400:400 + H], hot0[:, 0, :], fac[:, 1, :], start=True, stop=False)
                t_.matmul(prow[:, 400:400 + H], hot0[:, 1, :], fac[:, 3, :], start=False,
                          stop=True).then_inc(sc_ready, 1)
                if more:
                    turn(k + 1, 3)
                stay_warm(8)
                pe.wait_ge(m_ready, k + 1)
                t_.transpose(psd[:, 256:256 + ROWS], mx[:, :], C.ident[0:ROWS, 0:ROWS]).then_inc(mt_ready, 1)
                if more:
                    pick_er(k + 1, 2)
                    turn(k + 1, 4)
                    pick_er(k + 1, 3)
                stay_warm(0)
                for n in range(NGR - 2):
                    sums(k, u, n)
                    if more and n == 0:
                        turn(k + 1, 5)
                    if more and n < 2:
                        pick_er(k + 1, n + 4)
                if more:
                    turn_scores(k + 1)
                sums(k, u, NGR - 2)
                sums(k, u, NGR - 1)
                if more:
                    row_ends(k + 1)

            pe.wait_ge(ers_ready, 1)
            turn(0, 0)
            for n in range(NGR):
                if n + 1 < NGR:
                    turn(0, n + 1)
                pick_er(0, n)
            turn_scores(0)
            row_ends(0)
            with pe.Fori(0, NCH // 2 - 1) as i:
                for u in range(2):
                    chunk(2 * i + u, u, True)
            chunk(NCH - 2, 0, True)
            chunk(NCH - 1, 1, False)

    for slot in C.slots:
        slot.base += 16 * (NCH // 2)


def across(row, n):
    return row.rearrange("p (o m) -> p o m", o=1).to_broadcast([row.shape[0], n, row.shape[1]])


def one(a, t):
    return (a[:, t:t + 1, :] if isinstance(t, int) else a[:, bass.ds(t, 1), :]).rearrange("p o f -> p (o f)")


TC = 5


def row_stats(nc, c, x, stats, moments):
    for t in range(x.shape[1]):
        last = nc.vector.bn_stats(stats[:, t, :], x[:, t, :])
    c.link(last)
    for t in range(x.shape[1]):
        last = nc.vector.bn_aggr(moments[:, t, :], stats[:, t, :])
    c.link(last)
    var = moments[:, :, 1:2]
    c.link(nc.vector.tensor_scalar(var, var, 1e-5, None, ALU.add))
    c.link(nc.vector.reciprocal(var, var))


def norm_phase(nc, C, D):
    ctx, sems = ExitStack(), []
    with ctx:
        def sb(name, shape, dt=F32):
            return ctx.enter_context(nc.sbuf_tensor(name, shape, dt))

        def sem(name):
            sems.append(nc.alloc_semaphore(name))
            return sems[-1]

        rden = sb("rden", [P, NT, H])
        stats = sb("stats0", [P, NT, 6])
        moments = sb("moments0", [P, NT, 2])
        hs = sb("hs", [P, NT, F])
        dch = sem("dve_norm0")
        var_ready = sem("var_ready0")
        std_ready = sem("std_ready0")
        deg_ready = sem("deg_ready0")
        x_ready = sem("x_ready0")
        acc_free = sem("acc_free")
        acc_zeroed = sem("acc_zeroed")
        hs_ready = sem("hs_ready")
        hs_stored = sem("hs_stored")
        ctx.callback(clear, nc, sems)
        block = ctx.enter_context(nc.Block())

        @block.sync
        def _(sp):
            rows = D.hs.rearrange("(t p) f -> p t f", p=P)
            for n in range(NT // TC):
                sp.wait_ge(hs_ready, n + 1)
                sp.dma_start(rows[:, n * TC:n * TC + TC, :], hs[:, n * TC:n * TC + TC, :]).then_inc(hs_stored, 16)
            sp.wait_ge(hs_stored, 16 * (NT // TC))

        @block.gpsimd
        def _(g):
            g.wait_ge(acc_free, 1)
            g.memset(C.acc[:, :, :], 0.0).then_inc(acc_zeroed, 1)
            g.wait_ge(acc_zeroed, 1)

        @block.scalar
        def _(act):
            act.wait_ge(deg_ready, 1)
            nc.scalar.activation(C.rdego[:, :], C.rdego[:, :], ACT.Sqrt)
            nc.scalar.activation(C.rdegi[:, :], C.rdegi[:, :], ACT.Sqrt).then_inc(std_ready, 1)
            act.wait_ge(var_ready, 1)
            nc.scalar.activation(moments[:, :, 1], moments[:, :, 1], ACT.Sqrt).then_inc(std_ready, 1)
            act.wait_ge(std_ready, 1)
            for n in range(NT // TC):
                act.wait_ge(x_ready, n + 1)
                for t in range(n * TC, n * TC + TC):
                    last = nc.scalar.activation(hs[:, t, :], C.x[:, t, :], ACT.Copy, scale=C.rdego[:, t:t + 1])
                last.then_inc(hs_ready, 1)

        @block.vector
        def _(dve):
            v = nc.vector
            c = Chain(dve, dch)
            c.link(v.tensor_scalar(C.rdego[:, :], C.dego[:, :], 1.0, None, ALU.max))
            c.link(v.reciprocal(C.rdego[:, :], C.rdego[:, :]))
            c.link(v.tensor_scalar(C.rdegi[:, :].rearrange("p (t o) -> p t o", o=1), C.acc[:, 0:NT, FW:GW],
                                   1.0, None, ALU.max))
            v.reciprocal(C.rdegi[:, :], C.rdegi[:, :]).then_inc(deg_ready, 1)
            c.link(v.tensor_scalar(rden[:, :, :], C.acc[:, 0:NT, F:FW], 1e-30, None, ALU.max))
            c.link(v.reciprocal(rden[:, :, :], rden[:, :, :]))
            hv = C.acc[:, 0:NT, 0:F].rearrange("p t (h d) -> p t h d", h=H)
            c.link(v.tensor_tensor(hv, hv, rden[:, :, :].rearrange("p t (h o) -> p t h o", o=1)
                                   .to_broadcast([P, NT, H, HD]), ALU.mult))
            c.link(v.tensor_tensor(C.x[:, :, :], C.x[:, :, :], C.acc[:, 0:NT, 0:F], ALU.add))
            dve.sem_inc(acc_free, 1)
            row_stats(nc, c, C.x, stats, moments)
            dve.sem_inc(var_ready, 1)
            dve.wait_ge(std_ready, 2)
            for n in range(NT // TC):
                for t in range(n * TC, n * TC + TC):
                    last = v.tensor_scalar(C.x[:, t, :], C.x[:, t, :], moments[:, t, 0:1], moments[:, t, 1:2],
                                           ALU.subtract, ALU.mult)
                last.then_inc(x_ready, 1)


def conv_phase(nc, C, D):
    ctx, sems = ExitStack(), []
    with ctx:
        def sb(name, shape, dt=F32):
            return ctx.enter_context(nc.sbuf_tensor(name, shape, dt))

        def sem(name):
            sems.append(nc.alloc_semaphore(name))
            return sems[-1]

        gat = [sb(f"gatb{u}", [P, CH, F]) for u in range(2)]
        hot = [sb(f"hotb{u}", [P, CH, P]) for u in range(2)]
        gidx = [sb(f"gidxb{u}", [P, CH], I32) for u in range(2)]
        pacc = ctx.enter_context(nc.psum_tensor("paccb", [P, 2, 512], F32))
        gathered = [C.slots[u * CH:(u + 1) * CH] for u in range(2)]
        idx_ready = sem("idx_readyb")
        hot_ready = sem("hot_readyb")
        mm_done = sem("mm_doneb")
        acc_done = sem("acc_doneb")
        ctx.callback(clear, nc, sems)
        block = ctx.enter_context(nc.Block())

        @block.gpsimd
        def _(g):
            with g.Fori(0, NCH // 2) as i:
                for u in range(2):
                    k = 2 * i + u
                    g.wait_ge(mm_done, NGR * (k + 1))
                    g.tensor_copy(gidx[u][:, :], C.srci[:, bass.ds(k * CH, CH)]).then_inc(idx_ready, 1)
                    g.wait_ge(idx_ready, k + 1)
                    g.nop(nofuse=True)
                    for b in range(CH):
                        g.indirect_dma_start(gat[u][:, b, :], None, D.hs,
                                             bass.IndirectOffsetOnAxis(ap=gidx[u][:, b:b + 1], axis=0)
                                             ).then_inc(gathered[u][b].sem, 16)

        @block.vector
        def _(dve):
            v = nc.vector
            dve.sem_inc(acc_done, 2)
            with dve.Fori(0, NCH // 2) as i:
                for u in range(2):
                    k = 2 * i + u
                    v.tensor_tensor(hot[u][:, :, :], col(C.locf[:, bass.ds(k * CH, CH)], P),
                                    across(C.iota[:, :], CH), ALU.is_equal).then_inc(hot_ready, 1)
                    for n in range(NGR):
                        t = dve.value_load(C.tpi[0:1, bass.ds(k * CH + G * n, 1)], min_val=0, max_val=NT)
                        dve.wait_ge(mm_done, NGR * (k + 2) + n + 1)
                        if n:
                            dve.wait_ge(acc_done, NGR * k + n + 2)
                        tile = C.acc[:, bass.ds(t, 1), 0:F].rearrange("p o f -> p (o f)")
                        v.tensor_tensor(tile, tile, pacc[:, n % 2, 0:F], ALU.add).then_inc(acc_done, 1)

        @block.tensor
        def _(pe):
            pe.sem_inc(mm_done, 2 * NGR)
            with pe.Fori(0, NCH // 2) as i:
                for u in range(2):
                    k = 2 * i + u
                    pe.wait_ge(hot_ready, k + 1)
                    for j in range(CH):
                        pe.wait_ge(gathered[u][j].sem, gathered[u][j].base + 16 * i + 16)
                        if j % G == 0:
                            pe.wait_ge(acc_done, NGR * k + j // G + 1)
                        last = nc.tensor.matmul(pacc[:, j // G % 2, 0:F], hot[u][:, j, :], gat[u][:, j, :],
                                                start=(j % G == 0), stop=(j % G == G - 1))
                        if j % G == G - 1:
                            last.then_inc(mm_done, 1)

    for slot in C.slots:
        slot.base += 16 * (NCH // 2)


def gate_phase(nc, C, D):
    ctx, sems = ExitStack(), []
    with ctx:
        def sb(name, shape, dt=F32):
            return ctx.enter_context(nc.sbuf_tensor(name, shape, dt))

        def sem(name):
            sems.append(nc.alloc_semaphore(name))
            return sems[-1]

        w = sb("w_gcres", [P, 4, F])
        wgate = sb("wgate", [P, 2, NE])
        brow = sb("brow", [1, 2, F])
        bgrow = sb("bgrow", [1, NE])
        stage = [sb(f"stage{u}", [P, 2 * F]) for u in range(2)]
        xt = [sb(f"xmt{u}", [P, 4, P]) for u in range(2)]
        x2t = [sb(f"x2t{u}", [P, 2, P]) for u in range(2)]
        logit = [sb(f"logit{u}", [P, NE]) for u in range(2)]
        tp = [sb(f"tile_top{u}", [P, 8]) for u in range(2)]
        ti = [sb(f"tile_topi{u}", [P, 8], U32) for u in range(2)]
        top = sb("top", [P, NT, 8])
        topi = sb("topi", [P, NT, 8], U32)
        topf = sb("topf", [P, NT, 2])
        m = [sb(f"mask{k}", [P, NT, NE]) for k in range(2)]
        mb = sb("mask_b", [P, NT, NE], BF16)
        tri = sb("tri", [P, P], BF16)
        onesb = sb("ones_b", [P, P], BF16)
        valid = sb("valid", [P, NT])
        ct = sb("ct", [P, NE, NT])
        inc = sb("inc", [P, NE, NT])
        again = sb("again", [P, NE, NT])
        rank = sb("rank", [P, NT, NE])
        tmp = sb("ranktmp", [P, NT, NE])
        tot = sb("tot", [P, NE])
        toti = sb("toti", [P, NE], I32)
        tiles = sb("tiles", [P, NE])
        onese = sb("ones_e", [P, NE])
        tend = sb("tend", [P, NE])
        toff = sb("toff", [P, NE])
        rk = sb("rk", [P, 2, NT])
        sl = sb("sl", [P, 2, NT])
        ok = sb("ok", [P, 2, NT])
        e1 = sb("e1", [P, NT])
        scat = sb("scat", [P, 2, NT], I32)
        scatf = sb("scatf", [P, 2, NT])
        ecmp = sb("ecmp", [P, NE])
        ecol = sb("ecol", [P, 1])
        bt = sb("b1_rows", [NE, HID])
        px = ctx.enter_context(nc.psum_tensor("pxg", [P, 512], F32))
        pm = ctx.enter_context(nc.psum_tensor("pmg", [P, 512], F32))
        pz = ctx.enter_context(nc.psum_tensor("pzg", [P, 512], F32))
        pl = ctx.enter_context(nc.psum_tensor("plg", [P, 512], F32))
        pr = ctx.enter_context(nc.psum_tensor("prg", [P, 4, 512], F32))

        w_loaded = sem("w_gcres_loaded")
        b_loaded = sem("bias_loaded1")
        consts = sem("gate_consts")
        dch = sem("dve_gate")
        lch = sem("dve_gate_loop")
        top_ready = sem("top_ready")
        index_ready = sem("index_ready")
        staged = sem("staged")
        turned = sem("turned_g")
        xt_ready = sem("xt_ready_g")
        x2_ready = sem("x2_ready")
        x2_copied = sem("x2_copied")
        x2_turned = sem("x2_turned")
        x2t_ready = sem("x2t_ready")
        l_ready = sem("l_ready")
        l_copied = sem("l_copied")
        masks_ready = sem("masks_ready")
        counts_ready = sem("counts_ready")
        counts_read = sem("counts_read")
        ranks_ready = sem("ranks_ready")
        diff_ready = sem("diff_ready")
        e_ready = sem("e_ready")
        slots_ready = sem("slots_ready")
        ecol_ready = sem("ecol_ready")
        erow_ready = sem("erow_ready")
        b1t_ready = sem("b1t_ready")
        b1t_copied = sem("b1t_copied")
        NS = 30
        scattered = C.slots[0:NS]
        ctx.callback(clear, nc, sems)
        block = ctx.enter_context(nc.Block())

        @block.sync
        def _(sp):
            sp.dma_start(w[:, 0:2, :], D.wgc.rearrange("(c p) n -> p c n", p=P)).then_inc(w_loaded, 16)
            sp.dma_start(w[:, 2:4, :], D.wres.rearrange("(c p) n -> p c n", p=P)).then_inc(w_loaded, 16)
            sp.dma_start(wgate[:, :, :], D.wg.rearrange("(c p) n -> p c n", p=P)).then_inc(w_loaded, 16)
            sp.dma_start(bt[:, :], D.b1).then_inc(b_loaded, 16)
            sp.dma_start(C.b2[:, :], D.b2).then_inc(b_loaded, 16)
            sp.dma_start(brow[:, 0, :], D.bgc.rearrange("(o f) -> o f", o=1)).then_inc(b_loaded, 16)
            sp.dma_start(brow[:, 1, :], D.bres.rearrange("(o f) -> o f", o=1)).then_inc(b_loaded, 16)
            sp.dma_start(bgrow[:, :], D.bg.rearrange("(o f) -> o f", o=1)).then_inc(b_loaded, 16)
            sp.wait_ge(w_loaded, 48)
            sp.wait_ge(b_loaded, 80)

        @block.gpsimd
        def _(g):
            g.memset(tri[:, :], 1.0).then_inc(consts, 1)
            g.wait_ge(consts, 1)
            g.affine_select(out=tri[:, :], in_=tri[:, :], compare_op=ALU.is_gt, fill=0.0, base=0,
                            pattern=[[1, P]], channel_multiplier=-1).then_inc(consts, 1)
            for k in range(2):
                g.wait_ge(slots_ready, k + 1)
                for t in range(NT):
                    n = k * NT + t
                    if n >= NS:
                        g.wait_ge(scattered[n % NS].sem, scattered[n % NS].base + 16 * (n // NS))
                    g.indirect_dma_start(D.buf, bass.IndirectOffsetOnAxis(ap=scat[:, k, t:t + 1], axis=0),
                                         C.x2[:, t, :], None, bounds_check=NX * P - 1, oob_is_err=False
                                         ).then_inc(scattered[n % NS].sem, 16)
            for slot in scattered:
                g.wait_ge(slot.sem, slot.base + 16 * (2 * NT // NS))

        @block.scalar
        def _(act):
            a = nc.scalar
            act.sem_inc(x2t_ready, 2)

            def copy_xt(t, u):
                act.wait_ge(turned, t + 1)
                act.wait_ge(x2_ready, t + 1)
                a.activation(xt[u][:, :, :], px[:, :].rearrange("p (c n) -> p c n", n=P), ACT.Copy
                             ).then_inc(xt_ready, 1)

            def copy_logits(t, u):
                act.wait_ge(l_ready, t + 1)
                act.wait_ge(index_ready, t + 1)
                a.activation(logit[u][:, :], pl[:, 0:NE], ACT.Copy).then_inc(l_copied, 1)

            def tile(t, u, first=False, last=False):
                act.wait_ge(x2_ready, t + 3)
                to = C.x2[:, t:t + 1, :] if isinstance(t, int) else C.x2[:, bass.ds(t, 1), :]
                a.activation(to.rearrange("p o f -> p (o f)"), pm[:, 0:F], ACT.Copy)
                a.activation(stage[u][:, 0:F], pm[:, 0:F], ACT.Copy).then_inc(x2_copied, 1)
                if not last:
                    copy_xt(t + 1, 1 - u)
                if not first:
                    copy_logits(t - 1, 1 - u)
                act.wait_ge(x2_turned, t + 1)
                a.activation(x2t[u][:, :, :], pz[:, 0:F].rearrange("p (c n) -> p c n", n=P), ACT.Copy
                             ).then_inc(x2t_ready, 1)

            copy_xt(0, 0)
            tile(0, 0, first=True)
            tile(1, 1)
            with act.Fori(0, NT // 2 - 2) as i:
                for u in range(2):
                    tile(2 * i + u + 2, u)
            tile(NT - 2, 0)
            tile(NT - 1, 1, last=True)
            copy_logits(NT - 1, 1)
            act.wait_ge(b1t_ready, 1)
            for j in range(4):
                last = a.activation(C.b1t[:, :, j], pl[:, j * NE:(j + 1) * NE], ACT.Copy)
            last.then_inc(b1t_copied, 1)
            act.wait_ge(diff_ready, 1)
            a.activation(e1[:, :], e1[:, :], ACT.Exp).then_inc(e_ready, 1)

        @block.vector
        def _(dve):
            v = nc.vector
            c = Chain(dve, dch)
            dve.wait_ge(b_loaded, 80)
            c.link(v.tensor_tensor(brow[:, 0, :], brow[:, 0, :], brow[:, 1, :], ALU.add))
            c.link(v.memset(onesb[:, :], 1.0))
            c.link(v.memset(onese[:, :], 1.0))
            c.link(v.memset(valid[:, :], 1.0))
            c.link(v.tensor_scalar(valid[:, NT - 1:NT], C.ioch[:, :], float(LAST), None, ALU.is_lt))
            c.link(v.memset(again[:, :, :], 1.0))
            c.link(v.memset(again[:, :, 0:1], 0.0))

            def stage_tile(t, u):
                dve.wait_ge(x2t_ready, t + 1)
                v.tensor_tensor(stage[u][:, 0:F], one(C.acc, t)[:, 0:F],
                                (C.rdegi[:, t:t + 1] if isinstance(t, int) else C.rdegi[:, bass.ds(t, 1)])
                                .to_broadcast([P, F]), ALU.mult)
                v.tensor_copy(stage[u][:, F:2 * F], one(C.x, t)).then_inc(staged, 1)

            def top_two(t, u):
                dve.wait_ge(l_copied, t + 2)
                dve.nop(nofuse=True)
                v.max(tp[u][:, :], logit[u][:, :]).then_inc(top_ready, 1)
                dve.wait_ge(top_ready, t + 1)
                dve.nop(nofuse=True)
                v.max_index(ti[u][:, :], tp[u][:, :], logit[u][:, :]).then_inc(index_ready, 1)
                v.tensor_copy(one(top, t), tp[u][:, :])
                dve.wait_ge(index_ready, t + 3)
                v.tensor_copy(one(topi, t), ti[u][:, :]).then_inc(lch, 1)

            dve.sem_inc(index_ready, 2)
            for t in range(2):
                stage_tile(t, t)
            with dve.Fori(0, NT // 2 - 1) as i:
                for u in range(2):
                    stage_tile(2 * i + u + 2, u)
                    top_two(2 * i + u, u)
            for t in range(NT - 2, NT):
                top_two(t, t % 2)
            dve.wait_ge(lch, NT)
            v.tensor_tensor(e1[:, :], top[:, :, 1], top[:, :, 0], ALU.subtract).then_inc(diff_ready, 1)
            c.link(v.tensor_copy(topf[:, :, :], topi[:, :, 0:2]))
            for k in range(2):
                c.link(v.tensor_tensor(m[k][:, :, :], topf[:, :, k:k + 1].to_broadcast([P, NT, NE]),
                                       across(C.iota[:, 0:NE], NT), ALU.is_equal))
                c.link(v.tensor_tensor(m[k][:, :, :], m[k][:, :, :], col(valid[:, :], NE), ALU.mult))
            v.tensor_tensor(mb[:, :, :], m[0][:, :, :], m[1][:, :, :], ALU.add).then_inc(masks_ready, 1)
            dve.wait_ge(counts_ready, 1)
            for q in range(4):
                n = min(8, NT - 8 * q)
                c.link(v.tensor_copy(ct[:, :, 8 * q:8 * q + n].rearrange("p e t -> p t e"),
                                     pr[:, q, 0:n * NE].rearrange("p (t e) -> p t e", e=NE)))
            dve.sem_inc(counts_read, 1)
            c.link(v.tensor_tensor_scan(inc[:, :, :].rearrange("p e t -> p (e t)"),
                                        again[:, :, :].rearrange("p e t -> p (e t)"),
                                        ct[:, :, :].rearrange("p e t -> p (e t)"), 0.0, ALU.mult, ALU.add))
            c.link(v.tensor_copy(tot[:, :], inc[:, :, NT - 1]))
            c.link(v.tensor_scalar(tiles[:, :], tot[:, :], float(CAP), float(P - 1), ALU.min, ALU.add))
            c.link(v.tensor_copy(toti[:, :], tiles[:, :]))
            c.link(v.tensor_scalar(toti[:, :], toti[:, :], 7, None, ALU.arith_shift_right))
            c.link(v.tensor_copy(tiles[:, :], toti[:, :]))
            c.link(v.tensor_tensor_scan(tend[:, :], onese[:, :], tiles[:, :], 0.0, ALU.mult, ALU.add))
            c.link(v.tensor_tensor(toff[:, :], tend[:, :], tiles[:, :], ALU.subtract))
            c.link(v.tensor_scalar(toff[:, :], toff[:, :], float(P), None, ALU.mult))
            c.link(v.tensor_scalar(ecmp[:, :], tend[:, :], C.ioch[:, 0:1], None, ALU.is_le))
            c.link(v.tensor_reduce(ecol[:, :], ecmp[:, :], AX.X, ALU.add))
            v.tensor_scalar(ecol[:, :], ecol[:, :], float(NE - 1), None, ALU.min).then_inc(ecol_ready, 1)
            c.link(v.tensor_tensor(inc[:, :, :], inc[:, :, :], ct[:, :, :], ALU.subtract))
            dve.wait_ge(ranks_ready, 1)
            for q in range(4):
                n = min(8, NT - 8 * q)
                c.link(v.tensor_tensor(rank[:, 8 * q:8 * q + n, :],
                                       pr[:, q, 0:n * NE].rearrange("p (t e) -> p t e", e=NE),
                                       inc[:, :, 8 * q:8 * q + n].rearrange("p e t -> p t e"), ALU.add))
            for k in range(2):
                c.link(v.tensor_tensor(tmp[:, :, :], rank[:, :, :], m[k][:, :, :], ALU.mult))
                c.link(v.tensor_reduce(rk[:, k, :], tmp[:, :, :], AX.X, ALU.add))
                c.link(v.tensor_tensor(tmp[:, :, :], across(toff[:, :], NT), m[k][:, :, :], ALU.mult))
                c.link(v.tensor_reduce(sl[:, k, :], tmp[:, :, :], AX.X, ALU.add))
                c.link(v.tensor_tensor(sl[:, k, :], sl[:, k, :], rk[:, k, :], ALU.add))
                c.link(v.tensor_scalar(ok[:, k, :], rk[:, k, :], float(CAP), None, ALU.is_lt))
                c.link(v.tensor_tensor(ok[:, k, :], ok[:, k, :], valid[:, :], ALU.mult))
                c.link(v.tensor_tensor(sl[:, k, :], sl[:, k, :], ok[:, k, :], ALU.mult))
                c.link(v.tensor_scalar(scatf[:, k, :], ok[:, k, :], -float(NX * P), float(NX * P), ALU.mult, ALU.add))
                c.link(v.tensor_tensor(scatf[:, k, :], scatf[:, k, :], sl[:, k, :], ALU.add))
                v.tensor_copy(scat[:, k, :], scatf[:, k, :]).then_inc(slots_ready, 1)
            c.link(v.tensor_copy(C.slot[:, :, :], sl[:, :, :]))
            dve.wait_ge(e_ready, 1)
            c.link(v.tensor_scalar(C.gate[:, 0, :], e1[:, :], 1.0, None, ALU.add))
            c.link(v.reciprocal(C.gate[:, 0, :], C.gate[:, 0, :]))
            c.link(v.tensor_tensor(C.gate[:, 1, :], C.gate[:, 0, :], e1[:, :], ALU.mult))
            c.link(v.tensor_tensor(C.gate[:, :, :], C.gate[:, :, :], ok[:, :, :], ALU.mult))
            c.link(v.tensor_tensor(C.gm[:, :, :], m[0][:, :, :], col(C.gate[:, 0, :], NE), ALU.mult))
            c.link(v.tensor_tensor(tmp[:, :, :], m[1][:, :, :], col(C.gate[:, 1, :], NE), ALU.mult))
            c.link(v.tensor_tensor(C.gm[:, :, :], C.gm[:, :, :], tmp[:, :, :], ALU.add))
            c.link(v.tensor_copy(C.valid[:, :], valid[:, :]))
            dve.wait_ge(erow_ready, 1)
            v.tensor_copy(C.used[:, :], tend[0:1, NE - 1:NE])
            v.tensor_copy(C.expert[:, :], pz[0:1, 0:P]).then_inc(lch, 1)

        @block.tensor
        def _(pe):
            t_ = nc.tensor
            pe.wait_ge(w_loaded, 48)
            pe.wait_ge(b_loaded, 80)
            pe.sem_inc(x2_ready, 2)

            def turn(t, u):
                pe.wait_ge(staged, t + 1)
                for c in range(4):
                    last = t_.transpose(px[:, c * P:(c + 1) * P], stage[u][:, c * P:(c + 1) * P], C.ident[:, :])
                last.then_inc(turned, 1)

            def logits(t, u):
                pe.wait_ge(x2t_ready, t + 3)
                pe.wait_ge(l_copied, t + 1)
                for c in range(2):
                    t_.matmul(pl[:, 0:NE], x2t[u][:, c, :], wgate[:, c, :], start=(c == 0), stop=False)
                t_.matmul(pl[:, 0:NE], C.ones[0:1, :], bgrow[:, :], start=False, stop=True
                          ).then_inc(l_ready, 1)

            def tile(t, u, first=False, last=False):
                pe.wait_ge(xt_ready, t + 1)
                for c in range(4):
                    t_.matmul(pm[:, 0:F], xt[u][:, c, :], w[:, c, :], start=(c == 0), stop=False)
                t_.matmul(pm[:, 0:F], C.ones[0:1, :], brow[:, 0, :], start=False, stop=True
                          ).then_inc(x2_ready, 1)
                if not last:
                    turn(t + 1, 1 - u)
                if not first:
                    logits(t - 1, 1 - u)
                pe.wait_ge(x2_copied, t + 1)
                for c in range(2):
                    done = t_.transpose(pz[:, c * P:(c + 1) * P], stage[u][:, c * P:(c + 1) * P], C.ident[:, :])
                done.then_inc(x2_turned, 1)

            pe.sem_inc(l_copied, 1)
            turn(0, 0)
            tile(0, 0, first=True)
            tile(1, 1)
            with pe.Fori(0, NT // 2 - 2) as i:
                for u in range(2):
                    tile(2 * i + u + 2, u)
            tile(NT - 2, 0)
            tile(NT - 1, 1, last=True)
            logits(NT - 1, 1)
            pe.wait_ge(l_copied, NT + 1)
            for j in range(4):
                last = t_.transpose(pl[:, j * NE:(j + 1) * NE], bt[:, j * P:(j + 1) * P], C.ident[0:NE, 0:NE])
            last.then_inc(b1t_ready, 1)
            pe.wait_ge(masks_ready, 1)
            pe.wait_ge(consts, 2)
            for turn, (lhs, done) in enumerate(((onesb, counts_ready), (tri, ranks_ready))):
                if turn:
                    pe.wait_ge(counts_read, 1)
                for q in range(4):
                    n = min(8, NT - 8 * q)
                    last = t_.matmul(pr[:, q, 0:n * NE], lhs[:, :],
                                     mb[:, 8 * q:8 * q + n, :].rearrange("p t e -> p (t e)"), start=True, stop=True)
                last.then_inc(done, 1)
            pe.wait_ge(ecol_ready, 1)
            t_.matmul(pz[0:1, 0:P], ecol[:, :], C.ident[:, :], start=True, stop=True).then_inc(erow_ready, 1)

    for slot in scattered:
        slot.base += 16 * (2 * NT // NS)


def expert_phase(nc, C, D):
    ctx, sems = ExitStack(), []
    with ctx:
        def sb(name, shape, dt=F32):
            return ctx.enter_context(nc.sbuf_tensor(name, shape, dt))

        def sem(name):
            sems.append(nc.alloc_semaphore(name))
            return sems[-1]

        w1 = [sb(f"w1_{u}", [P, 2, HID]) for u in range(XG)]
        w2 = [sb(f"w2_{u}", [P, 4, F]) for u in range(XG)]
        xb = [sb(f"xb{u}", [P, F]) for u in range(XG)]
        xt = [sb(f"xbt{u}", [P, 2, P]) for u in range(XG)]
        h1 = [sb(f"h1_{u}", [P, 4, P]) for u in range(XG)]
        yb = [sb(f"yb{u}", [P, F]) for u in range(XG)]
        px = ctx.enter_context(nc.psum_tensor("pxe", [P, 2, 512], F32))
        ph = ctx.enter_context(nc.psum_tensor("phe", [P, 2, 512], F32))
        py = ctx.enter_context(nc.psum_tensor("pye", [P, 2, 512], F32))
        w_loaded = [sem(f"w_loaded{u}") for u in range(XG)]
        x_loaded = [sem(f"xb_loaded{u}") for u in range(XG)]
        y_stored = C.slots[0:XG]
        x_turned = sem("xb_turned")
        xt_ready = sem("xbt_ready")
        h_ready = sem("h_ready")
        g_ready = sem("g_ready")
        y_ready = sem("y_ready")
        y_copied = sem("y_copied")
        y_free = sem("y_free")
        ctx.callback(clear, nc, sems)
        block = ctx.enter_context(nc.Block())

        @block.sync
        def _(sp):
            used = sp.value_load(C.used[0:1, 0:1], min_val=1, max_val=NX)
            rows = D.buf.rearrange("(t p) f -> t p f", p=P)
            with sp.Fori(0, NX // XG) as i:
                with sp.If(used > XG * i):
                    for u in range(XG):
                        t = XG * i + u
                        e = sp.value_load(C.expert[0:1, bass.ds(t, 1)], min_val=0, max_val=NE - 1)
                        sp.wait_ge(y_ready, t + 1)
                        sp.dma_start(xb[u][:, :], rows[bass.ds(t, 1), :, :].rearrange("o p f -> (o p) f")
                                     ).then_inc(x_loaded[u], 16)
                        sp.dma_start(w1[u][:, :, :], D.w1[bass.ds(e, 1), :, :]
                                     .rearrange("o (p c) h -> (o p) c h", c=2)).then_inc(w_loaded[u], 16)
                        sp.dma_start(w2[u][:, :, :], D.w2[bass.ds(e, 1), :, :]
                                     .rearrange("o (c p) f -> (o p) c f", p=P)).then_inc(w_loaded[u], 16)

        @block.gpsimd
        def _(g):
            g.sem_inc(y_free, XG)
            used = g.value_load(C.used[0:1, 0:1], min_val=1, max_val=NX)
            rows = D.buf.rearrange("(t p) f -> t p f", p=P)
            with g.Fori(0, NX // XG) as i:
                with g.If(used > XG * i):
                    for u in range(XG):
                        t = XG * i + u
                        g.wait_ge(y_copied, t + 3)
                        g.dma_start(rows[bass.ds(t, 1), :, :].rearrange("o p f -> (o p) f"), yb[u][:, :]
                                    ).then_inc(y_stored[u].sem, 16)
                    for u in range(XG):
                        g.wait_ge(y_stored[u].sem, y_stored[u].base + 16 * i + 16)
                    g.sem_inc(y_free, XG)

        @block.scalar
        def _(act):
            used = act.value_load(C.used[0:1, 0:1], min_val=1, max_val=NX)
            with act.Fori(0, NX // XG) as i:
                with act.If(used > XG * i):
                    for u in range(XG):
                        t = XG * i + u
                        e = act.value_load(C.expert[0:1, bass.ds(t, 1)], min_val=0, max_val=NE - 1)
                        act.wait_ge(y_ready, t + 1)
                        act.wait_ge(h_ready, t + 1)
                        for j in range(4):
                            last = nc.scalar.activation(h1[u][:, j, :], ph[:, u % 2, j * P:(j + 1) * P], ACT.Gelu,
                                                        bias=C.b1t[:, bass.ds(e, 1), j])
                        last.then_inc(g_ready, 1)

        @block.vector
        def _(dve):
            v = nc.vector
            dve.sem_inc(y_copied, 2)
            used = dve.value_load(C.used[0:1, 0:1], min_val=1, max_val=NX)
            with dve.Fori(0, NX // XG) as i:
                with dve.If(used > XG * i):
                    def turned(u):
                        t = XG * i + u
                        dve.wait_ge(x_turned, t + 1)
                        v.tensor_copy(xt[u][:, :, :], px[:, u % 2, 0:F].rearrange("p (c n) -> p c n", n=P)
                                      ).then_inc(xt_ready, 1)

                    def result(u):
                        t = XG * i + u
                        if u == 0:
                            dve.wait_ge(y_free, XG * i + XG)
                        dve.wait_ge(y_ready, t + XG + 1)
                        v.tensor_copy(yb[u][:, :], py[:, u % 2, 0:F]).then_inc(y_copied, 1)

                    turned(0)
                    turned(1)
                    turned(2)
                    result(0)
                    turned(3)
                    result(1)
                    result(2)
                    result(3)

        @block.tensor
        def _(pe):
            t_ = nc.tensor
            pe.sem_inc(y_ready, XG)
            used = pe.value_load(C.used[0:1, 0:1], min_val=1, max_val=NX)
            with pe.Fori(0, NX // XG) as i:
                with pe.If(used > XG * i):
                    def turn(u):
                        pe.wait_ge(x_loaded[u], 16 * i + 16)
                        if u >= 2:
                            pe.wait_ge(xt_ready, XG * i + u - 1)
                        for c in range(2):
                            last = t_.transpose(px[:, u % 2, c * P:(c + 1) * P],
                                                xb[u][:, :].rearrange("p (k c) -> p c k", c=2)[:, c, :],
                                                C.ident[:, :])
                        last.then_inc(x_turned, 1)

                    def hidden(u):
                        pe.wait_ge(w_loaded[u], 32 * i + 32)
                        pe.wait_ge(xt_ready, XG * i + u + 1)
                        if u >= 2:
                            pe.wait_ge(g_ready, XG * i + u - 1)
                        for j in range(4):
                            for c in range(2):
                                last = t_.matmul(ph[:, u % 2, j * P:(j + 1) * P], w1[u][:, c, j * P:(j + 1) * P],
                                                 xt[u][:, c, :], start=(c == 0), stop=(c == 1))
                        last.then_inc(h_ready, 1)

                    def result(u):
                        pe.wait_ge(g_ready, XG * i + u + 1)
                        pe.wait_ge(y_copied, XG * i + u + 1)
                        for j in range(4):
                            last = t_.matmul(py[:, u % 2, 0:F], h1[u][:, j, :], w2[u][:, j, :],
                                             start=(j == 0), stop=(j == 3))
                        last.then_inc(y_ready, 1)

                    turn(0)
                    turn(1)
                    hidden(0)
                    turn(2)
                    hidden(1)
                    result(0)
                    turn(3)
                    hidden(2)
                    result(1)
                    hidden(3)
                    result(2)
                    result(3)


def output_phase(nc, C, D):
    ctx, sems = ExitStack(), []
    with ctx:
        def sb(name, shape, dt=F32):
            return ctx.enter_context(nc.sbuf_tensor(name, shape, dt))

        def sem(name):
            sems.append(nc.alloc_semaphore(name))
            return sems[-1]

        NY = 4
        y = [[sb(f"y{k}_{u}", [P, F]) for u in range(NY)] for k in range(2)]
        gmt = [sb(f"gmt{u}", [NE, P]) for u in range(2)]
        vm = sb("vm", [P, P])
        mean = sb("bn_mean", [P, F])
        rstd = sb("bn_rstd", [P, F])
        gb = sb("gamma_beta", [P, 2, F])
        stats = sb("stats1", [P, NT, 6])
        moments = sb("moments1", [P, NT, 2])
        shift = sb("shift1", [P, NT])
        sq = C.acc[:, 0:NT, 0:F]
        HERE = 2
        pg = ctx.enter_context(nc.psum_tensor("pgo", [P, 2, 512], F32))
        pb = ctx.enter_context(nc.psum_tensor("pbo", [P, 2, 512], F32))
        ps = ctx.enter_context(nc.psum_tensor("pso", [P, 512], F32))
        gathered = [C.slots[XG + k * NY:XG + (k + 1) * NY] for k in range(2)]
        gb_loaded = sem("gb_loaded")
        turned = sem("gm_turned")
        gmt_ready = sem("gmt_ready")
        b2_ready = sem("b2_ready")
        y_added = sem("y_added")
        dch = sem("dve_out")
        vm_ready = sem("vm_ready")
        yc_ready = sem("yc_ready")
        sums_ready = sem("sums_ready")
        sq_ready = sem("sq_ready")
        var_ready = sem("var_ready1")
        std_ready = sem("std_ready1")
        shift_ready = sem("shift_ready")
        out_ready = sem("out_ready")
        out_ready_act = sem("out_ready_act")
        stored = sem("out_stored")
        ctx.callback(clear, nc, sems)
        block = ctx.enter_context(nc.Block())

        @block.sync
        def _(sp):
            for k, a in enumerate((D.gamma, D.beta)):
                sp.dma_start(gb[:, k, :], a.rearrange("(o f) -> o f", o=1).to_broadcast([P, F])
                             ).then_inc(gb_loaded, 16)
            for n in range(NT // TC):
                sp.wait_ge(out_ready, n + 1)
                sp.wait_ge(out_ready_act, n + 1)
                t0, t1 = n * TC, min(n * TC + TC, NT - 1)
                sp.dma_start(D.out[t0 * P:t1 * P, :].rearrange("(t p) f -> p t f", p=P), C.x[:, t0:t1, :]
                             ).then_inc(stored, 16)
            sp.dma_start(D.out[(NT - 1) * P:N, :], C.x[0:LAST, NT - 1, :]).then_inc(stored, 16)
            sp.wait_ge(stored, 16 * (NT // TC + 1))

        @block.gpsimd
        def _(g):
            for t in range(NT):
                if t >= NY:
                    g.wait_ge(y_added, t - NY + 1)
                for k in range(2):
                    g.indirect_dma_start(y[k][t % NY][:, :], None, D.buf,
                                         bass.IndirectOffsetOnAxis(ap=C.slot[:, k, t:t + 1], axis=0)
                                         ).then_inc(gathered[k][t % NY].sem, 16)

        @block.scalar
        def _(act):
            for t in range(NT):
                act.wait_ge(turned, t + 1)
                if t >= 2:
                    act.wait_ge(b2_ready, t - 1)
                nc.scalar.activation(gmt[t % 2][:, :], pg[0:NE, t % 2, 0:P], ACT.Copy).then_inc(gmt_ready, 1)
            for n in range(NT // TC):
                act.wait_ge(yc_ready, n + 1)
                nc.scalar.activation(sq[:, n * TC:n * TC + TC, :], C.x2[:, n * TC:n * TC + TC, :], ACT.Square
                                     ).then_inc(sq_ready, 1)
            act.wait_ge(var_ready, 1)
            nc.scalar.activation(rstd[:, :], rstd[:, :], ACT.Sqrt).then_inc(std_ready, 1)
            act.wait_ge(var_ready, 2)
            nc.scalar.activation(moments[:, :, 1], moments[:, :, 1], ACT.Sqrt).then_inc(std_ready, 1)
            act.wait_ge(shift_ready, 1)
            for n in range(NT // TC):
                for t in range(n * TC + TC - HERE, n * TC + TC):
                    last = nc.scalar.activation(C.x[:, t, :], C.x[:, t, :], ACT.Identity, bias=shift[:, t:t + 1],
                                                scale=moments[:, t, 1:2])
                last.then_inc(out_ready_act, 1)

        @block.vector
        def _(dve):
            v = nc.vector
            c = Chain(dve, dch)
            v.tensor_copy(vm[:, :], C.valid[:, NT - 1:NT].to_broadcast([P, P])).then_inc(vm_ready, 1)
            for t in range(NT):
                for k in range(2):
                    dve.wait_ge(gathered[k][t % NY].sem, gathered[k][t % NY].base + 16 * (t // NY) + 16)
                    c.link(v.scalar_tensor_tensor(C.x2[:, t, :], y[k][t % NY][:, :], C.gate[:, k, t:t + 1],
                                                  C.x2[:, t, :], ALU.mult, ALU.add))
                dve.wait_ge(b2_ready, t + 1)
                v.tensor_tensor(C.x2[:, t, :], C.x2[:, t, :], pb[:, t % 2, 0:F], ALU.add).then_inc(y_added, 1)
            dve.wait_ge(sums_ready, 1)
            c.link(v.tensor_scalar(mean[:, :], ps[:, 0:F], 1.0 / N, None, ALU.mult))
            for n in range(NT // TC):
                yc = C.x2[:, n * TC:n * TC + TC, :]
                v.tensor_tensor(yc, yc, across(mean[:, :], TC), ALU.subtract).then_inc(yc_ready, 1)
            dve.wait_ge(gb_loaded, 32)
            c.link(v.tensor_tensor(C.x[:, :, :], C.x[:, :, :], across(gb[:, 1, :], NT), ALU.add))
            dve.wait_ge(sums_ready, 2)
            c.link(v.tensor_scalar(rstd[:, :], ps[:, 0:F], 1.0 / N, 1e-5, ALU.mult, ALU.add))
            c.link(v.reciprocal(rstd[:, :], rstd[:, :]))
            dve.sem_inc(var_ready, 1)
            dve.wait_ge(std_ready, 1)
            c.link(v.tensor_tensor(rstd[:, :], rstd[:, :], gb[:, 0, :], ALU.mult))
            c.link(v.tensor_tensor(C.x2[:, :, :], C.x2[:, :, :], across(rstd[:, :], NT), ALU.mult))
            c.link(v.tensor_tensor(C.x[:, :, :], C.x[:, :, :], C.x2[:, :, :], ALU.add))
            row_stats(nc, c, C.x, stats, moments)
            dve.sem_inc(var_ready, 1)
            dve.wait_ge(std_ready, 2)
            v.scalar_tensor_tensor(shift[:, :], moments[:, :, 0], -1.0, moments[:, :, 1], ALU.mult, ALU.mult
                                   ).then_inc(shift_ready, 1)
            for n in range(NT // TC):
                for t in range(n * TC, n * TC + TC - HERE):
                    last = v.tensor_scalar(C.x[:, t, :], C.x[:, t, :], moments[:, t, 0:1], moments[:, t, 1:2],
                                           ALU.subtract, ALU.mult)
                last.then_inc(out_ready, 1)

        @block.tensor
        def _(pe):
            t_ = nc.tensor

            def column_sum(a, t):
                last = t_.matmul(ps[:, 0:F], vm[:, :] if t == NT - 1 else C.ones[:, :], a[:, t, :],
                                 start=(t == 0), stop=(t == NT - 1))
                if t == NT - 1:
                    last.then_inc(sums_ready, 1)

            pe.wait_ge(vm_ready, 1)
            for t in range(NT):
                if t >= 2:
                    pe.wait_ge(gmt_ready, t - 1)
                t_.transpose(pg[0:NE, t % 2, 0:P], C.gm[:, t, :], C.ident[:, :]).then_inc(turned, 1)
                pe.wait_ge(gmt_ready, t + 1)
                if t >= 2:
                    pe.wait_ge(y_added, t - 1)
                    column_sum(C.x2, t - 2)
                t_.matmul(pb[:, t % 2, 0:F], gmt[t % 2][:, :], C.b2[:, :], start=True, stop=True
                          ).then_inc(b2_ready, 1)
            for t in range(NT - 2, NT):
                pe.wait_ge(y_added, t + 1)
                column_sum(C.x2, t)
            for t in range(NT):
                if t % TC == 0:
                    pe.wait_ge(sq_ready, t // TC + 1)
                column_sum(sq, t)


class Slot:

    def __init__(self, sem):
        self.sem, self.base = sem, 0


class Bag:
    pass


def gnn_program(nc, x, src, dst, typ, conv, attl, attr, hbias, wgc, bgc, wres, bres, wg, bg, w1, b1, w2,
                b2, gamma, beta, out):
    D, C = Bag(), Bag()
    D.x, D.src, D.dst, D.typ = x, src, dst, typ
    D.conv, D.attl, D.attr = conv, attl, attr
    D.tab = nc.dram_tensor("feature_table", (NT * P, R * FW), F32, kind="Internal").ap()
    D.buf = nc.dram_tensor("expert_rows", (NBUF * P, F), F32, kind="Internal").ap()
    D.hbias, D.wgc, D.bgc, D.wres, D.bres, D.wg, D.bg = hbias, wgc, bgc, wres, bres, wg, bg
    D.w1, D.b1, D.w2, D.b2, D.gamma, D.beta, D.out = w1, b1, w2, b2, gamma, beta, out
    D.hs = nc.dram_tensor("scaled_rows", (NT * P, F), F32, kind="Internal").ap()
    D.rec = nc.dram_tensor("edge_records", (NRG * P, 4 * P), F32, kind="Internal").ap()
    ctx = ExitStack()
    with ctx:
        def sb(name, shape, dt=F32):
            return ctx.enter_context(nc.sbuf_tensor(name, shape, dt))

        C.ident = sb("ident", [P, P])
        C.iota = sb("iota", [P, P])
        C.ioch = sb("ioch", [P, 1])
        C.ones = sb("ones", [P, P])
        C.x = sb("x_sb", [P, NT, F])
        C.acc = sb("acc", [P, NT + 1, GW])
        C.rdego = sb("rdego", [P, NT])
        C.rdegi = sb("rdegi", [P, NT])
        C.dego = sb("dego", [P, NT])
        C.slots = [Slot(ctx.enter_context(nc.semaphore(f"gather_slot{n}"))) for n in range(2 * CH)]
        C.first_slots = [Slot(ctx.enter_context(nc.semaphore(f"first_slot{n}"))) for n in range(NG)]
        edges = ctx.enter_context(ExitStack())

        def eb(name, shape, dt=F32):
            return edges.enter_context(nc.sbuf_tensor(name, shape, dt))

        C.er = eb("er", [P, NT + 1, R * H])
        C.fidx = eb("fidx", [P, NPAIR], I32)
        C.srci = eb("srci", [P, NPAIR], I32)
        C.dstf = eb("dstf", [P, NPAIR])
        C.typf = eb("typf", [P, NPAIR])
        C.locf = eb("locf", [P, NPAIR])
        C.srcraw = eb("srcraw", [P, NB])
        C.tpi = eb("tpi", [1, NG * P], I32)
        C.w_loaded = ctx.enter_context(nc.semaphore("conv_loaded"))
        with ExitStack() as weights:
            C.w = weights.enter_context(nc.sbuf_tensor("conv_w", [P, 2, R * F], F32))
            C.att = weights.enter_context(nc.sbuf_tensor("att", [P, 2, R * F], F32))
            setup_phase(nc, C, D)
            table_phase(nc, C, D)
        attention_phase(nc, C, D)
        norm_phase(nc, C, D)
        conv_phase(nc, C, D)
        edges.close()
        C.x2 = sb("x2", [P, NT, F])
        C.b2 = sb("b2_sb", [NE, F])
        C.b1t = sb("b1t", [P, NE, 4])
        C.gate = sb("gate", [P, 2, NT])
        C.slot = sb("slot", [P, 2, NT], I32)
        C.gm = sb("gate_by_expert", [P, NT, NE])
        C.valid = sb("valid_rows", [P, NT])
        C.expert = sb("expert_of_tile", [1, P], I32)
        C.used = sb("tiles_used", [1, 1], I32)
        gate_phase(nc, C, D)
        expert_phase(nc, C, D)
        output_phase(nc, C, D)


_INS = ["x", "src", "dst", "edge_type_8", "L0_gnn_conv_weights", "L0_gnn_attn_l", "L0_gnn_attn_r",
        "L0_gnn_h_bias", "L1_gnn_W_gc", "L1_gnn_b_gc", "L1_gnn_W_res", "L1_gnn_b_res", "L1_gnn_Wg",
        "L1_gnn_bg", "L1_gnn_w1", "L1_gnn_b1", "L1_gnn_w2", "L1_gnn_b2", "L1_gnn_gamma", "L1_gnn_beta"]


def kernel(**inputs):
    import numpy as _np
    import concourse.bacc as _bacc
    from concourse import mybir as _mybir
    from concourse.bass_utils import run_bass_kernel_spmd as _run

    nc = _bacc.Bacc("TRN2", target_bir_lowering=False, num_devices=1)
    arrays, args = {}, []
    for name in _INS:
        a = _np.ascontiguousarray(inputs[name])
        arrays[f"in_{name}"] = a
        args.append(nc.dram_tensor(f"in_{name}", a.shape, _mybir.dt.from_np(a.dtype), kind="ExternalInput").ap())
    args.append(nc.dram_tensor("out", (N, F), _mybir.dt.float32, kind="ExternalOutput").ap())
    gnn_program(nc, *args)
    r = _run(nc, [arrays], core_ids=[0])
    return r.results[0]["out"]
```
